# Optimizing a Trainium2 kernel written in Bass

```python
import numpy as np
import jax
import jax.numpy as jnp

def _softmax(x, axis=-1):
    return jax.nn.softmax(x, axis=axis)

def _gelu(x):
    return jax.nn.gelu(x, approximate=True)

def _silu(x):
    return jax.nn.silu(x)

def _sigmoid(x):
    return jax.nn.sigmoid(x)

def _layernorm(x, axis=-1, eps=1e-05):
    m = jnp.mean(x, axis=axis, keepdims=True)
    v = jnp.var(x, axis=axis, keepdims=True)
    return (x - m) / jnp.sqrt(v + eps)

def _scatter_add(tgt, idx, src, axis=0):
    return tgt.at[idx].add(src)

def _segment_sum(src, seg, n):
    return jax.ops.segment_sum(src, seg, n)
kernel_name = 'mk_hybrid_d1_jaxref_r8_c0749b'

def setup_inputs(seed: int=0):
    np.random.seed(seed)
    _w = jnp.asarray

    def _L0_attn_a_setup():
        import jax, jax.numpy as jnp
        import numpy as np
        H, HD, CHUNK = (16, 64, 128)

        def _rotary(x):
            N, d = (x.shape[-2], x.shape[-1])
            inv_freq = 1.0 / 10000.0 ** (jnp.arange(0, d, 2, dtype=jnp.float32) / d)
            ang = jnp.arange(N, dtype=jnp.float32)[:, None] * inv_freq[None, :]
            ang = jnp.repeat(ang, 2, axis=-1)
            cos, sin = (jnp.cos(ang), jnp.sin(ang))
            x1, x2 = (x[..., 0::2], x[..., 1::2])
            xr = jnp.stack([-x2, x1], axis=-1).reshape(x.shape)
            return x * cos + xr * sin

        def _split_heads(t, B, N):
            return t.reshape(B, N, H, HD).transpose(0, 2, 1, 3)

        def _chunked(Q, KK, VK):
            B, h, N, d = Q.shape
            nc = N // CHUNK

            def to_chunks(t):
                return t.reshape(B, h, nc, CHUNK, d).transpose(2, 0, 1, 3, 4)
            S0 = jnp.eye(d, dtype=Q.dtype) * jnp.sqrt(jnp.float32(d))
            S0 = jnp.broadcast_to(S0, (B, h, d, d))

            def step(SK_state, inp):
                q, kk, vk = inp
                ok = jnp.einsum('bhni,bhnj->bhnij', kk, vk)
                SK = jnp.cumsum(ok, axis=2) + SK_state[:, :, None]
                norm = jnp.sqrt(jnp.sum(SK * SK, axis=(-2, -1), keepdims=True)) + 1e-08
                SKn = SK / norm
                y = jnp.einsum('bhni,bhnji->bhnj', q, SKn)
                return (SK[:, :, -1], y)
            _, ys = jax.lax.scan(step, S0, (to_chunks(Q), to_chunks(KK), to_chunks(VK)))
            return ys.transpose(1, 2, 0, 3, 4).reshape(B, h, N, d)
        key = jax.random.key(seed)
        ks = jax.random.split(key, 5)
        B, N, D = (2, 256, 128)
        X = jax.random.normal(ks[0], (B, N, D), jnp.float32)
        w_qkv = jax.random.normal(ks[1], (D, 3 * H * HD), jnp.float32) * 0.02
        w_kvkv = jax.random.normal(ks[2], (D, 4 * H * HD), jnp.float32) * 0.02
        w_out = jax.random.normal(ks[3], (H * HD, D), jnp.float32) * 0.02
        b_out = jnp.zeros((D,), jnp.float32)
        return {'X': X, 'w_qkv': w_qkv, 'w_kvkv': w_kvkv, 'w_out': w_out, 'b_out': b_out}
    _L0_attn_a_in = _L0_attn_a_setup()

    def _L0_attn_b_setup():
        import jax, jax.numpy as jnp
        import numpy as np
        N_LAYER, N_HEAD, D_MODEL, D_FF = (6, 16, 128, 512)
        D_HEAD = D_MODEL // N_HEAD
        M_FEAT = 2 * D_MODEL // N_HEAD
        CHUNK = 128
        LN_EPS = 1e-05
        ATT_EPS = 1e-06
        B, S = (4, 256)

        def _layer_norm(x, g, b):
            mu = x.mean(-1, keepdims=True)
            var = ((x - mu) ** 2).mean(-1, keepdims=True)
            return (x - mu) * jax.lax.rsqrt(var + LN_EPS) * g + b

        def _favor_phi(x, omega):
            x = x * D_HEAD ** (-0.25)
            u = jnp.einsum('bhsd,dm->bhsm', x, omega)
            nrm = 0.5 * jnp.sum(x * x, axis=-1, keepdims=True)
            phi = jnp.concatenate([jnp.exp(u - nrm), jnp.exp(-u - nrm)], axis=-1)
            return phi * M_FEAT ** (-0.5)

        def _causal_linear_attention(Qp, Kp, V):
            b, h, s, m = Qp.shape
            d = V.shape[-1]
            c = s // CHUNK
            Qc = Qp.reshape(b, h, c, CHUNK, m)
            Kc = Kp.reshape(b, h, c, CHUNK, m)
            Vc = V.reshape(b, h, c, CHUNK, d)
            kv = jnp.einsum('bhclm,bhcld->bhcmd', Kc, Vc)
            ksum = Kc.sum(axis=3)
            kv_pre = jnp.cumsum(kv, axis=2) - kv
            ks_pre = jnp.cumsum(ksum, axis=2) - ksum
            scores = jnp.einsum('bhcim,bhcjm->bhcij', Qc, Kc)
            mask = jnp.tril(jnp.ones((CHUNK, CHUNK), bool))
            scores = jnp.where(mask, scores, 0.0)
            num = jnp.einsum('bhcij,bhcjd->bhcid', scores, Vc) + jnp.einsum('bhcim,bhcmd->bhcid', Qc, kv_pre)
            den = scores.sum(-1) + jnp.einsum('bhcim,bhcm->bhci', Qc, ks_pre)
            out = num / (den[..., None] + ATT_EPS)
            return out.reshape(b, h, s, d)

        def _forward(x, Wq, bq, Wk, bk, Wv, bv, Wo, bo, omega, g1, be1, W1, bf1, W2, bf2, g2, be2):
            bsz, slen, _ = x.shape
            out = x
            for l in range(N_LAYER):

                def proj(W, bvec):
                    y = jnp.einsum('bsd,de->bse', out, W) + bvec
                    return y.reshape(bsz, slen, N_HEAD, D_HEAD).transpose(0, 2, 1, 3)
                q = proj(Wq[l], bq[l])
                k = proj(Wk[l], bk[l])
                v = proj(Wv[l], bv[l])
                Qp = _favor_phi(q, omega[l])
                Kp = _favor_phi(k, omega[l])
                a = _causal_linear_attention(Qp, Kp, v)
                a = a.transpose(0, 2, 1, 3).reshape(bsz, slen, D_MODEL)
                a = jnp.einsum('bsd,de->bse', a, Wo[l]) + bo[l]
                h1 = _layer_norm(out + a, g1[l], be1[l])
                y = jax.nn.relu(jnp.einsum('bsd,df->bsf', h1, W1[l]) + bf1[l])
                y = jnp.einsum('bsf,fd->bsd', y, W2[l]) + bf2[l]
                out = _layer_norm(h1 + y, g2[l], be2[l])
            return out
        key = jax.random.key(seed)
        ks = jax.random.split(key, 12)
        s = D_MODEL ** (-0.5)
        f32 = jnp.float32
        return {'x': jax.random.normal(ks[0], (B, S, D_MODEL), f32), 'Wq': jax.random.normal(ks[1], (N_LAYER, D_MODEL, D_MODEL), f32) * s, 'bq': jnp.zeros((N_LAYER, D_MODEL), f32), 'Wk': jax.random.normal(ks[2], (N_LAYER, D_MODEL, D_MODEL), f32) * s, 'bk': jnp.zeros((N_LAYER, D_MODEL), f32), 'Wv': jax.random.normal(ks[3], (N_LAYER, D_MODEL, D_MODEL), f32) * s, 'bv': jnp.zeros((N_LAYER, D_MODEL), f32), 'Wo': jax.random.normal(ks[4], (N_LAYER, D_MODEL, D_MODEL), f32) * s, 'bo': jnp.zeros((N_LAYER, D_MODEL), f32), 'omega': jax.random.normal(ks[5], (N_LAYER, D_HEAD, M_FEAT // 2), f32), 'g1': jnp.ones((N_LAYER, D_MODEL), f32), 'be1': jnp.zeros((N_LAYER, D_MODEL), f32), 'W1': jax.random.normal(ks[6], (N_LAYER, D_MODEL, D_FF), f32) * s, 'bf1': jnp.zeros((N_LAYER, D_FF), f32), 'W2': jax.random.normal(ks[7], (N_LAYER, D_FF, D_MODEL), f32) * D_FF ** (-0.5), 'bf2': jnp.zeros((N_LAYER, D_MODEL), f32), 'g2': jnp.ones((N_LAYER, D_MODEL), f32), 'be2': jnp.zeros((N_LAYER, D_MODEL), f32)}
    _L0_attn_b_in = _L0_attn_b_setup()

    def _L0_ffn_setup():
        import jax, jax.numpy as jnp
        import numpy as np
        B, S, D = (2, 64, 128)
        E, K, I = (16, 8, 128)
        I_SH = 128
        ROUTE_SCALE = 2.826
        key = jax.random.key(seed)
        ks = jax.random.split(key, 8)
        s = 0.02
        return {'x': jax.random.normal(ks[0], (B, S, D), dtype=jnp.float32), 'gate_w': jax.random.normal(ks[1], (E, D), dtype=jnp.float32) * s, 'expert_bias': jnp.zeros((E,), dtype=jnp.float32), 'w_gate': jax.random.normal(ks[2], (E, I, D), dtype=jnp.float32) * s, 'w_up': jax.random.normal(ks[3], (E, I, D), dtype=jnp.float32) * s, 'w_down': jax.random.normal(ks[4], (E, D, I), dtype=jnp.float32) * s, 'shared_gate_w': jax.random.normal(ks[5], (I_SH, D), dtype=jnp.float32) * s, 'shared_up_w': jax.random.normal(ks[6], (I_SH, D), dtype=jnp.float32) * s, 'shared_down_w': jax.random.normal(ks[7], (D, I_SH), dtype=jnp.float32) * s}
    _L0_ffn_in = _L0_ffn_setup()
    _d = {'L0_attn_a_X': _L0_attn_a_in['X'], 'L0_attn_a_w_qkv': _L0_attn_a_in['w_qkv'], 'L0_attn_a_w_kvkv': _L0_attn_a_in['w_kvkv'], 'L0_attn_a_w_out': _L0_attn_a_in['w_out'], 'L0_attn_a_b_out': _L0_attn_a_in['b_out'], 'L0_attn_b_Wq': _L0_attn_b_in['Wq'], 'L0_attn_b_bq': _L0_attn_b_in['bq'], 'L0_attn_b_Wk': _L0_attn_b_in['Wk'], 'L0_attn_b_bk': _L0_attn_b_in['bk'], 'L0_attn_b_Wv': _L0_attn_b_in['Wv'], 'L0_attn_b_bv': _L0_attn_b_in['bv'], 'L0_attn_b_Wo': _L0_attn_b_in['Wo'], 'L0_attn_b_bo': _L0_attn_b_in['bo'], 'L0_attn_b_omega': _L0_attn_b_in['omega'], 'L0_attn_b_g1': _L0_attn_b_in['g1'], 'L0_attn_b_be1': _L0_attn_b_in['be1'], 'L0_attn_b_W1': _L0_attn_b_in['W1'], 'L0_attn_b_bf1': _L0_attn_b_in['bf1'], 'L0_attn_b_W2': _L0_attn_b_in['W2'], 'L0_attn_b_bf2': _L0_attn_b_in['bf2'], 'L0_attn_b_g2': _L0_attn_b_in['g2'], 'L0_attn_b_be2': _L0_attn_b_in['be2'], 'L0_ffn_gate_w': _L0_ffn_in['gate_w'], 'L0_ffn_expert_bias': _L0_ffn_in['expert_bias'], 'L0_ffn_w_gate': _L0_ffn_in['w_gate'], 'L0_ffn_w_up': _L0_ffn_in['w_up'], 'L0_ffn_w_down': _L0_ffn_in['w_down'], 'L0_ffn_shared_gate_w': _L0_ffn_in['shared_gate_w'], 'L0_ffn_shared_up_w': _L0_ffn_in['shared_up_w'], 'L0_ffn_shared_down_w': _L0_ffn_in['shared_down_w']}
    _x0 = _d['L0_attn_a_X']
    _d['L0_attn_a_X'] = jax.random.normal(jax.random.fold_in(jax.random.key(seed), 1), (8, 512, 128), dtype=_x0.dtype)
    del _x0
    return _d

def reference(L0_attn_a_X, L0_attn_a_w_qkv, L0_attn_a_w_kvkv, L0_attn_a_w_out, L0_attn_a_b_out, L0_attn_b_Wq, L0_attn_b_bq, L0_attn_b_Wk, L0_attn_b_bk, L0_attn_b_Wv, L0_attn_b_bv, L0_attn_b_Wo, L0_attn_b_bo, L0_attn_b_omega, L0_attn_b_g1, L0_attn_b_be1, L0_attn_b_W1, L0_attn_b_bf1, L0_attn_b_W2, L0_attn_b_bf2, L0_attn_b_g2, L0_attn_b_be2, L0_ffn_gate_w, L0_ffn_expert_bias, L0_ffn_w_gate, L0_ffn_w_up, L0_ffn_w_down, L0_ffn_shared_gate_w, L0_ffn_shared_up_w, L0_ffn_shared_down_w):

    def _L0_attn_a_ref(X, w_qkv, w_kvkv, w_out, b_out):
        import jax, jax.numpy as jnp
        import numpy as np
        H, HD, CHUNK = (16, 64, 128)

        def _rotary(x):
            N, d = (x.shape[-2], x.shape[-1])
            inv_freq = 1.0 / 10000.0 ** (jnp.arange(0, d, 2, dtype=jnp.float32) / d)
            ang = jnp.arange(N, dtype=jnp.float32)[:, None] * inv_freq[None, :]
            ang = jnp.repeat(ang, 2, axis=-1)
            cos, sin = (jnp.cos(ang), jnp.sin(ang))
            x1, x2 = (x[..., 0::2], x[..., 1::2])
            xr = jnp.stack([-x2, x1], axis=-1).reshape(x.shape)
            return x * cos + xr * sin

        def _split_heads(t, B, N):
            return t.reshape(B, N, H, HD).transpose(0, 2, 1, 3)

        def _chunked(Q, KK, VK):
            B, h, N, d = Q.shape
            nc = N // CHUNK

            def to_chunks(t):
                return t.reshape(B, h, nc, CHUNK, d).transpose(2, 0, 1, 3, 4)
            S0 = jnp.eye(d, dtype=Q.dtype) * jnp.sqrt(jnp.float32(d))
            S0 = jnp.broadcast_to(S0, (B, h, d, d))

            def step(SK_state, inp):
                q, kk, vk = inp
                ok = jnp.einsum('bhni,bhnj->bhnij', kk, vk)
                SK = jnp.cumsum(ok, axis=2) + SK_state[:, :, None]
                norm = jnp.sqrt(jnp.sum(SK * SK, axis=(-2, -1), keepdims=True)) + 1e-08
                SKn = SK / norm
                y = jnp.einsum('bhni,bhnji->bhnj', q, SKn)
                return (SK[:, :, -1], y)
            _, ys = jax.lax.scan(step, S0, (to_chunks(Q), to_chunks(KK), to_chunks(VK)))
            return ys.transpose(1, 2, 0, 3, 4).reshape(B, h, N, d)
        B, N, D = X.shape
        q, k, v = jnp.split(X @ w_qkv, 3, axis=-1)
        Q = _split_heads(q, B, N)
        K = _split_heads(k, B, N)
        V = _split_heads(v, B, N)
        kk, vk, _kv, _vv = jnp.split(X @ w_kvkv, 4, axis=-1)
        KK = _split_heads(kk, B, N)
        VK = _split_heads(vk, B, N)
        Qn = _chunked(Q, KK, VK)
        Qr = _rotary(Qn)
        Kr = _rotary(K)
        scale = 1.0 / jnp.sqrt(jnp.float32(HD))
        scores = jnp.einsum('bhqd,bhkd->bhqk', Qr, Kr) * scale
        mask = jnp.tril(jnp.ones((N, N), dtype=bool))
        scores = jnp.where(mask, scores, -jnp.inf)
        attn = jax.nn.softmax(scores, axis=-1)
        out = jnp.einsum('bhqk,bhkd->bhqd', attn, V)
        out = out.transpose(0, 2, 1, 3).reshape(B, N, H * HD)
        return out @ w_out + b_out

    def _L0_attn_b_ref(x, Wq, bq, Wk, bk, Wv, bv, Wo, bo, omega, g1, be1, W1, bf1, W2, bf2, g2, be2):
        import jax, jax.numpy as jnp
        import numpy as np
        N_LAYER, N_HEAD, D_MODEL, D_FF = (6, 16, 128, 512)
        D_HEAD = D_MODEL // N_HEAD
        M_FEAT = 2 * D_MODEL // N_HEAD
        CHUNK = 128
        LN_EPS = 1e-05
        ATT_EPS = 1e-06
        B, S = (4, 256)

        def _layer_norm(x, g, b):
            mu = x.mean(-1, keepdims=True)
            var = ((x - mu) ** 2).mean(-1, keepdims=True)
            return (x - mu) * jax.lax.rsqrt(var + LN_EPS) * g + b

        def _favor_phi(x, omega):
            x = x * D_HEAD ** (-0.25)
            u = jnp.einsum('bhsd,dm->bhsm', x, omega)
            nrm = 0.5 * jnp.sum(x * x, axis=-1, keepdims=True)
            phi = jnp.concatenate([jnp.exp(u - nrm), jnp.exp(-u - nrm)], axis=-1)
            return phi * M_FEAT ** (-0.5)

        def _causal_linear_attention(Qp, Kp, V):
            b, h, s, m = Qp.shape
            d = V.shape[-1]
            c = s // CHUNK
            Qc = Qp.reshape(b, h, c, CHUNK, m)
            Kc = Kp.reshape(b, h, c, CHUNK, m)
            Vc = V.reshape(b, h, c, CHUNK, d)
            kv = jnp.einsum('bhclm,bhcld->bhcmd', Kc, Vc)
            ksum = Kc.sum(axis=3)
            kv_pre = jnp.cumsum(kv, axis=2) - kv
            ks_pre = jnp.cumsum(ksum, axis=2) - ksum
            scores = jnp.einsum('bhcim,bhcjm->bhcij', Qc, Kc)
            mask = jnp.tril(jnp.ones((CHUNK, CHUNK), bool))
            scores = jnp.where(mask, scores, 0.0)
            num = jnp.einsum('bhcij,bhcjd->bhcid', scores, Vc) + jnp.einsum('bhcim,bhcmd->bhcid', Qc, kv_pre)
            den = scores.sum(-1) + jnp.einsum('bhcim,bhcm->bhci', Qc, ks_pre)
            out = num / (den[..., None] + ATT_EPS)
            return out.reshape(b, h, s, d)

        def _forward(x, Wq, bq, Wk, bk, Wv, bv, Wo, bo, omega, g1, be1, W1, bf1, W2, bf2, g2, be2):
            bsz, slen, _ = x.shape
            out = x
            for l in range(N_LAYER):

                def proj(W, bvec):
                    y = jnp.einsum('bsd,de->bse', out, W) + bvec
                    return y.reshape(bsz, slen, N_HEAD, D_HEAD).transpose(0, 2, 1, 3)
                q = proj(Wq[l], bq[l])
                k = proj(Wk[l], bk[l])
                v = proj(Wv[l], bv[l])
                Qp = _favor_phi(q, omega[l])
                Kp = _favor_phi(k, omega[l])
                a = _causal_linear_attention(Qp, Kp, v)
                a = a.transpose(0, 2, 1, 3).reshape(bsz, slen, D_MODEL)
                a = jnp.einsum('bsd,de->bse', a, Wo[l]) + bo[l]
                h1 = _layer_norm(out + a, g1[l], be1[l])
                y = jax.nn.relu(jnp.einsum('bsd,df->bsf', h1, W1[l]) + bf1[l])
                y = jnp.einsum('bsf,fd->bsd', y, W2[l]) + bf2[l]
                out = _layer_norm(h1 + y, g2[l], be2[l])
            return out
        return _forward(x, Wq, bq, Wk, bk, Wv, bv, Wo, bo, omega, g1, be1, W1, bf1, W2, bf2, g2, be2)

    def _L0_ffn_ref(x, gate_w, expert_bias, w_gate, w_up, w_down, shared_gate_w, shared_up_w, shared_down_w):
        import jax, jax.numpy as jnp
        import numpy as np
        B, S, D = (2, 64, 128)
        E, K, I = (16, 8, 128)
        I_SH = 128
        ROUTE_SCALE = 2.826
        gates = jnp.einsum('bsd,ed->bse', x, gate_w)
        scores = jax.nn.sigmoid(gates.astype(jnp.float32))
        sel_scores = scores + expert_bias
        _, inds = jax.lax.top_k(sel_scores, K)
        selected = jnp.take_along_axis(scores, inds, axis=-1)
        selected = selected / selected.sum(axis=-1, keepdims=True)
        selected = selected * ROUTE_SCALE
        onehot = jax.nn.one_hot(inds, E, dtype=selected.dtype)
        combine = jnp.einsum('bske,bsk->bse', onehot, selected)
        hg = jnp.einsum('bsd,eid->bsei', x, w_gate)
        hu = jnp.einsum('bsd,eid->bsei', x, w_up)
        h = jax.nn.silu(hg) * hu
        ye = jnp.einsum('bsei,edi->bsed', h, w_down)
        y = jnp.einsum('bsed,bse->bsd', ye, combine).astype(x.dtype)
        g = jnp.einsum('bsd,id->bsi', x, shared_gate_w)
        u = jnp.einsum('bsd,id->bsi', x, shared_up_w)
        y = y + jnp.einsum('bsi,di->bsd', jax.nn.silu(g) * u, shared_down_w)
        return y
    x = L0_attn_a_X
    x = x + _L0_attn_a_ref(_layernorm(x, axis=-1), L0_attn_a_w_qkv, L0_attn_a_w_kvkv, L0_attn_a_w_out, L0_attn_a_b_out)
    x = x + _L0_ffn_ref(_layernorm(x, axis=-1), L0_ffn_gate_w, L0_ffn_expert_bias, L0_ffn_w_gate, L0_ffn_w_up, L0_ffn_w_down, L0_ffn_shared_gate_w, L0_ffn_shared_up_w, L0_ffn_shared_down_w)
    x = x + _L0_attn_b_ref(_layernorm(x, axis=-1), L0_attn_b_Wq, L0_attn_b_bq, L0_attn_b_Wk, L0_attn_b_bk, L0_attn_b_Wv, L0_attn_b_bv, L0_attn_b_Wo, L0_attn_b_bo, L0_attn_b_omega, L0_attn_b_g1, L0_attn_b_be1, L0_attn_b_W1, L0_attn_b_bf1, L0_attn_b_W2, L0_attn_b_bf2, L0_attn_b_g2, L0_attn_b_be2)
    x = x + _L0_ffn_ref(_layernorm(x, axis=-1), L0_ffn_gate_w, L0_ffn_expert_bias, L0_ffn_w_gate, L0_ffn_w_up, L0_ffn_w_down, L0_ffn_shared_gate_w, L0_ffn_shared_up_w, L0_ffn_shared_down_w)
    return x

_drawn_inputs = setup_inputs


def setup_inputs(seed=0):
    import zlib

    import numpy as np

    out = dict(_drawn_inputs(seed))
    spreads = {'L0_attn_a_b_out': (0.0, 0.1),
     'L0_attn_b_bq': (0.0, 0.34),
     'L0_attn_b_bk': (0.0, 0.443),
     'L0_attn_b_bv': (0.0, 0.1),
     'L0_attn_b_bo': (0.0, 0.1),
     'L0_attn_b_g1': (1.0, 0.2),
     'L0_attn_b_be1': (0.0, 0.1),
     'L0_attn_b_bf1': (0.0, 0.1),
     'L0_attn_b_bf2': (0.0, 0.1),
     'L0_attn_b_g2': (1.0, 0.2),
     'L0_attn_b_be2': (0.0, 0.1),
     'L0_ffn_expert_bias': (0.0, 0.8)}
    factors = {'L0_attn_a_w_kvkv': 8.0,
     'L0_ffn_gate_w': 8.0,
     'L0_ffn_w_gate': 7.316,
     'L0_ffn_w_up': 7.45,
     'L0_ffn_w_down': 7.494,
     'L0_ffn_shared_gate_w': 7.544,
     'L0_ffn_shared_up_w': 7.427,
     'L0_ffn_shared_down_w': 7.377}
    for name, (base, spread) in spreads.items():
        noise = np.random.default_rng([zlib.crc32(name.encode()), seed]).standard_normal(out[name].shape)
        drawn = base * np.exp(spread * noise) if base else spread * noise
        out[name] = jnp.asarray(drawn.astype(out[name].dtype))
    for name, factor in factors.items():
        out[name] = (out[name] * factor).astype(out[name].dtype)
    return out
```

```python
from contextlib import ExitStack

import concourse.bass as bass
import concourse.mybir as mybir
import numpy as np

F32 = mybir.dt.float32
BF16 = mybir.dt.bfloat16
ALU = mybir.AluOpType
ACT = mybir.ActivationFunctionType
AX = mybir.AxisListType
P = 128
TILES = 4
SEQ = TILES * P
LN_EPS = 1e-5

STAGES = ("a", "ffn", "b", "ffn")

def layernorm_steps(nc, dve, m, s, g, read):
    for c in range(TILES):
        nc.vector.bn_stats(m["stats"][:, c, :], read(c)).then_inc(s["stats_done"], 1)
    dve.wait_ge(s["stats_done"], (g + 1) * TILES)
    dve.nop(nofuse=True)
    for c in range(TILES):
        nc.vector.bn_aggr(m["mean_var"][:, c, :], m["stats"][:, c, :]).then_inc(s["mv_done"], 1)
    dve.wait_ge(s["mv_done"], (g + 1) * TILES)
    nc.vector.tensor_scalar(m["var_eps"][:], m["mean_var"][:, :, 1], LN_EPS, None,
                            ALU.add).then_inc(s["eps_done"], 1)
    dve.wait_ge(s["rstd_done"], g + 1)
    for c in range(TILES):
        nc.vector.tensor_scalar(m["xn"][:, c, :], read(c), m["mean_var"][:, c, 0:1], m["rstd"][:, c:c + 1],
                                ALU.subtract, ALU.mult).then_inc(s["xn_done"], 1)


def norm_block(nc, mem, groups, attention, tag):
    with ExitStack() as ctx:
        def sb(name, shape, dt=F32):
            return ctx.enter_context(nc.sbuf_tensor(tag + name, shape, dt))

        def sem(name):
            return ctx.enter_context(nc.semaphore(tag + name))

        m = {"stats": sb("stats", [P, TILES, 6]), "mean_var": sb("mean_var", [P, TILES, 2]),
             "var_eps": sb("var_eps", [P, TILES]), "rstd": sb("rstd", [P, TILES]),
             "xn": sb("xn", [P, TILES, P])}
        s = {n: sem(n) for n in ("stats_done", "mv_done", "eps_done", "rstd_done", "xn_done")}
        turned, xT_done, out_done = sem("turned"), sem("xT_done"), sem("out_done")
        ps_t = ctx.enter_context(nc.psum_tensor(tag + "ps_t", [P, 512], F32))
        with nc.Block() as block:
            @block.vector
            def _(dve):
                with dve.Fori(0, groups) as g:
                    x4 = mem["x"][:, bass.ds(g * SEQ, SEQ)]
                    layernorm_steps(nc, dve, m, s, g, lambda c: mem["x"][:, bass.ds(g * SEQ + c * P, P)])
                    dve.wait_ge(s["xn_done"], (g + 1) * TILES)
                    if attention:
                        nc.vector.tensor_tensor(
                            x4, x4, mem["b_out4"][:], ALU.add).then_inc(out_done, 1)
                        dve.wait_ge(turned, g + 1)
                    else:
                        nc.vector.tensor_copy(mem["o"][:, bass.ds(g * SEQ, SEQ)],
                                              m["xn"][:].rearrange("p c d -> p (c d)")).then_inc(out_done, 1)

            @block.gpsimd
            def _(pool):
                with pool.Fori(0, groups) as g:
                    pool.wait_ge(s["eps_done"], g + 1)
                    nc.gpsimd.tensor_tensor(m["rstd"][:], m["var_eps"][:], mem["minus_half"][:, 0:TILES],
                                            ALU.pow).then_inc(s["rstd_done"], 1)

            if attention:
                @block.tensor
                def _(pe):
                    with pe.Fori(0, groups) as g:
                        pe.wait_ge(s["xn_done"], g * TILES + TILES)
                        pe.wait_ge(xT_done, g + 1)
                        for c in range(TILES):
                            t = nc.tensor.transpose(ps_t[:, c * P:(c + 1) * P], m["xn"][:, c, :], mem["ident"][:])
                        t.then_inc(turned, 1)

                @block.scalar
                def _(act):
                    act.sem_inc(xT_done, 1)
                    with act.Fori(0, groups) as g:
                        act.wait_ge(turned, g + 1)
                        nc.scalar.copy(mem["xT"][:, bass.ds(g * SEQ, SEQ)], ps_t[:]).then_inc(xT_done, 1)


def attention_block(nc, mem, ins, B):
    H, HD, EPS = 16, 64, 1e-8
    PAIRS = H // 2
    with ExitStack() as ctx:
        def sb(name, shape, dt=F32):
            return ctx.enter_context(nc.sbuf_tensor("a_" + name, shape, dt))

        def bank(name):
            return ctx.enter_context(nc.psum_tensor("a_" + name, [P, 512], F32))

        def sem(name):
            return ctx.enter_context(nc.semaphore("a_" + name))

        staged = sb("staged", [P, 6 * P])
        w_qvk = sb("w_qvk", [P, 3 * P])
        w_rk = sb("w_rk", [P, P])
        w_tok = sb("w_tok", [P, 4 * P])
        w_o = sb("w_o", [P, P])
        xTb = sb("xTb", [P, SEQ])
        qv = sb("qv", [P, TILES, 2, P])
        tok = sb("tok", [P, TILES, 4 * P])
        kcos, ksin = sb("kcos", [P, SEQ]), sb("ksin", [P, SEQ])
        keys = [sb(f"keys{h}", [P, SEQ]) for h in range(2)]
        state = sb("state", [P, TILES, P])
        lin = [sb(f"lin{h}", [P, TILES, 2, P]) for h in range(2)]
        zk = sb("zk", [P, TILES, 2, HD])
        inc = sb("inc", [P, 2 * TILES])
        norm2 = sb("norm2", [P, 2 * TILES])
        norm = sb("norm", [P, 2 * TILES])
        norm8 = sb("norm8", [P, 2 * TILES])
        scale = sb("scale", [P, 2 * TILES])
        query = [sb(f"query{h}", [P, SEQ]) for h in range(2)]
        neg_max = sb("neg_max", [P, 2 * TILES])
        shift = sb("shift", [P, 2 * TILES])
        row_sum = sb("row_sum", [P, 2 * TILES])
        inv_sum = sb("inv_sum", [P, 2 * TILES])
        prob = [sb(f"prob{i}", [P, SEQ]) for i in range(2)]
        probT = [sb(f"probT{i}", [P, SEQ]) for i in range(2)]
        heads = sb("heads", [P, TILES, 2 * HD])
        headsT = sb("headsT", [P, SEQ])
        ps_a = [bank(f"ps_a{i}") for i in range(2)]
        ps_s = [bank(f"ps_s{i}") for i in range(2)]
        ps_y = [bank(f"ps_y{i}") for i in range(2)]
        ps_z = bank("ps_z")
        ps_d = bank("ps_d")

        NAMES = dict(proj=8, states=1, lins=4, zs=1, cum=1, ys=2, scores=8, turns=8, pvs=8, headT=1, outs=1,
                     qvs=2, toks=4, keyT=2, exps=8, probTs=8, headTc=1,
                     kmul=2, statec=3, masked=4, zkm=2, incs=1, n2=1, n8=1, scales=1, queries=2, negs=8,
                     shifts=8, inv=1, headn=1, xadd=1, xcopy=1, kadd=2, pows=1)
        s = {n: sem(n) for n in NAMES}
        w_loaded, w_act, w_pool = sem("w_loaded"), sem("w_act"), sem("w_pool")

        def begin(e, names):
            for n in names.split():
                e.sem_inc(s[n], 1)

        def wait(e, name, it, n):
            e.wait_ge(s[name], it * NAMES[name] + (n + 1))

        def flat(ap):
            return ap.rearrange("p a b c -> p (a b c)") if len(ap.shape) == 4 else ap.rearrange("p a b -> p (a b)")

        with nc.Block() as block:
            @block.sync
            def _(sp):
                sp.sem_inc(w_act, 1)
                sp.sem_inc(w_pool, 1)
                with sp.Fori(0, PAIRS) as hp:
                    sp.wait_ge(w_act, hp + 1)
                    sp.wait_ge(w_pool, hp + 1)
                    sp.dma_start(staged[:], ins["pairs"][bass.ds(hp, 1), :, :].squeeze(0)).then_inc(w_loaded, 16)

            @block.gpsimd
            def _(pool):
                begin(pool, "xcopy kadd pows")
                with pool.Fori(0, PAIRS) as hp:
                    pool.wait_ge(w_loaded, hp * 16 + 16)
                    wait(pool, "outs", hp * B, 0)
                    pool.nop(nofuse=True)
                    k_, kk_ = staged[:, 2 * P:3 * P], staged[:, 3 * P:4 * P]
                    nc.gpsimd.tensor_scalar(w_rk[:, 0:P:2], k_[:, 1:P:2], -1.0, None, ALU.mult)
                    nc.gpsimd.tensor_copy(w_rk[:, 1:P:2], k_[:, 0:P:2])
                    for h in range(2):
                        kk_h = kk_[:, h * HD:(h + 1) * HD]
                        at = h * P
                        nc.gpsimd.tensor_copy(w_tok[:, at:at + HD], kk_h)
                        nc.gpsimd.tensor_scalar(w_tok[:, at + HD:at + P:2], kk_h[:, 1:HD:2], -1.0, None, ALU.mult)
                        t = nc.gpsimd.tensor_copy(w_tok[:, at + HD + 1:at + P:2], kk_h[:, 0:HD:2])
                    t.then_inc(w_pool, 1)
                    with pool.Fori(0, B) as b:
                        it = hp * B + b
                        wait(pool, "proj", it, 0)
                        pool.nop(nofuse=True)
                        nc.gpsimd.tensor_copy(xTb[:], mem["xT"][:, bass.ds(b * SEQ, SEQ)]).then_inc(s["xcopy"], 1)
                        wait(pool, "kmul", it, 2)
                        for h in range(2):
                            r = slice(h * HD, (h + 1) * HD)
                            nc.gpsimd.tensor_tensor(keys[h][r, :], kcos[r, :], ksin[r, :],
                                                    ALU.add).then_inc(s["kadd"], 1)
                            wait(pool, "kadd", it, h + 1)
                        wait(pool, "n2", it, 1)
                        nc.gpsimd.tensor_tensor(norm[:], norm2[:], mem["plus_half"][:, 0:2 * TILES],
                                                ALU.pow).then_inc(s["pows"], 1)

            @block.tensor
            def _(pe):
                begin(pe, "proj states lins zs cum ys scores turns pvs headT outs")
                with pe.Fori(0, PAIRS) as hp:
                    pe.wait_ge(w_act, hp + 2)
                    pe.wait_ge(w_pool, hp + 2)
                    pe.nop(nofuse=True)
                    with pe.Fori(0, B) as b:
                        it = hp * B + b
                        wait(pe, "xcopy", it, 1)
                        for n in range(8):
                            if n == 0:
                                wait(pe, "probTs", it, 0)
                            elif n in (2, 3):
                                wait(pe, "qvs", it, n - 1)
                            elif n >= 4:
                                wait(pe, "toks", it, n - 3)
                            o = ps_a[n % 2][:]
                            if n in (0, 1, 6, 7):
                                w = {0: w_qvk[:, P:2 * P], 1: w_qvk[:, 0:P], 6: w_qvk[:, 2 * P:3 * P],
                                     7: w_rk[:]}[n]
                                t = nc.tensor.matmul(o, w, xTb[:], start=True, stop=True)
                            else:
                                t = nc.tensor.matmul(o, xTb[:, (n - 2) * P:(n - 1) * P], w_tok[:],
                                                     start=True, stop=True)
                            t.then_inc(s["proj"], 1)

                        def rows(h):
                            return slice(h * HD, (h + 1) * HD)

                        def lin_scores(half):
                            for h in range(2):
                                if half:
                                    wait(pe, "masked", it, 1 + h)
                                for c in (2 * half, 2 * half + 1):
                                    t = nc.tensor.matmul(ps_s[h][:, (c % 2) * 2 * P:(c % 2 + 1) * 2 * P],
                                                         qv[rows(h), c, 1, :],
                                                         qv[rows(h), c, :, :].rearrange("p a n -> p (a n)"),
                                                         start=True, stop=True)
                                t.then_inc(s["lins"], 1)

                        wait(pe, "qvs", it, 2)
                        lin_scores(0)
                        wait(pe, "toks", it, 4)
                        for c in range(TILES - 1):
                            for h in range(2):
                                t = nc.tensor.matmul(ps_d[rows(h), c * P:(c + 1) * P],
                                                     tok[:, c, 3 * P + h * HD:3 * P + (h + 1) * HD],
                                                     tok[:, c, h * P:(h + 1) * P], start=True, stop=True)
                        t.then_inc(s["states"], 1)
                        lin_scores(1)
                        wait(pe, "statec", it, 3)
                        wait(pe, "masked", it, 4)
                        wait(pe, "xadd", it, 0)
                        for c in range(TILES):
                            for h in range(2):
                                o = (ps_z, ps_y[1])[h][:, c * HD:(c + 1) * HD]
                                nc.tensor.matmul(o, lin[h][:, c, 1, :], tok[:, c, h * P:h * P + HD],
                                                 start=True, stop=False)
                                t = nc.tensor.matmul(o, qv[rows(h), c, 1, :], state[rows(h), c, 0:HD],
                                                     start=False, stop=True)
                        t.then_inc(s["zs"], 1)

                        def ys(h):
                            for c in range(TILES):
                                o = ps_y[h][:, c * P:(c + 1) * P]
                                nc.tensor.matmul(o, tok[:, c, h * P:(h + 1) * P], lin[h][:, c, 0, :],
                                                 start=True, stop=False)
                                t = nc.tensor.matmul(o, state[rows(h), c, :], qv[rows(h), c, 0, :],
                                                     start=False, stop=True)
                            t.then_inc(s["ys"], 1)

                        ys(0)
                        wait(pe, "incs", it, 1)
                        N2 = 2 * TILES
                        o = ps_d[:, 3 * P:3 * P + N2]
                        nc.tensor.matmul(o, mem["twos_upto"][:], inc[:], start=True, stop=False)
                        for back in range(1, TILES):
                            t = nc.tensor.matmul(o[:, 2 * back:N2], mem["twos"][:], inc[:, 0:N2 - 2 * back],
                                                 start=False, stop=back == TILES - 1)
                        t.then_inc(s["cum"], 1)
                        ys(1)

                        def scores(u):
                            h, c = divmod(u, TILES)
                            if c == 0:
                                wait(pe, "queries", it, h + 1)
                                wait(pe, "keyT", it, h + 1)
                                wait(pe, "kadd", it, 2)
                            if u >= 2:
                                wait(pe, "exps", it, u - 1)
                            o = ps_s[u % 2]
                            nc.tensor.matmul(o[:, 0:(c + 1) * P], query[h][:, c * P:(c + 1) * P],
                                             keys[h][:, 0:(c + 1) * P], start=True, stop=False)
                            nc.tensor.matmul(o[:, c * P:(c + 1) * P], mem["ident16"][:], mem["future16"][:],
                                             start=False, stop=True).then_inc(s["scores"], 1)

                        def turn(u):
                            c = u % TILES
                            wait(pe, "exps", it, u + 1)
                            if u < 2:
                                wait(pe, "kmul", it, u + 1)
                            else:
                                wait(pe, "probTs", it, u - 1)
                            for j in range(c + 1):
                                t = nc.tensor.transpose(ps_a[u % 2][:, j * P:(j + 1) * P],
                                                        prob[u % 2][:, j * P:(j + 1) * P], mem["ident"][:])
                            t.then_inc(s["turns"], 1)

                        def weigh(u):
                            h, c = divmod(u, TILES)
                            wait(pe, "probTs", it, u + 1)
                            for j in range(c + 1):
                                t = nc.tensor.matmul(ps_z[:, (2 * c + h) * HD:(2 * c + h + 1) * HD],
                                                     probT[u % 2][:, j * P:(j + 1) * P],
                                                     tok[:, j, 2 * P + h * HD:2 * P + (h + 1) * HD],
                                                     start=j == 0, stop=j == c)
                            t.then_inc(s["pvs"], 1)

                        U = 2 * TILES
                        for u in range(U + 2):
                            if u < U:
                                scores(u)
                            if 1 <= u <= U:
                                turn(u - 1)
                            if u >= 2:
                                weigh(u - 2)
                        wait(pe, "headn", it, 1)
                        for c in range(TILES):
                            t = nc.tensor.transpose(ps_y[0][:, c * P:(c + 1) * P], heads[:, c, :], mem["ident"][:])
                        t.then_inc(s["headT"], 1)
                        wait(pe, "headTc", it, 1)
                        for c in range(TILES):
                            t = nc.tensor.matmul(ps_y[1][:, c * P:(c + 1) * P], headsT[:, c * P:(c + 1) * P],
                                                 w_o[:], start=True, stop=True)
                        t.then_inc(s["outs"], 1)

            @block.scalar
            def _(act):
                begin(act, "qvs toks keyT exps probTs headTc")
                with act.Fori(0, PAIRS) as hp:
                    act.wait_ge(w_loaded, hp * 16 + 16)
                    wait(act, "outs", hp * B, 0)
                    nc.scalar.copy(w_qvk[:], staged[:, 0:3 * P])
                    nc.scalar.copy(w_tok[:, 2 * P:3 * P], staged[:, 4 * P:5 * P])
                    nc.scalar.copy(w_tok[:, 3 * P:4 * P], staged[:, P:2 * P])
                    nc.scalar.copy(w_o[:], staged[:, 5 * P:6 * P]).then_inc(w_act, 1)
                    with act.Fori(0, B) as b:
                        it = hp * B + b
                        for n in range(2):
                            wait(act, "proj", it, n + 1)
                            nc.scalar.copy(qv[:, :, 1 - n, :],
                                           ps_a[n][:].rearrange("p (c n) -> p c n", c=TILES)).then_inc(s["qvs"], 1)
                        for c in range(TILES):
                            wait(act, "proj", it, c + 3)
                            nc.scalar.copy(tok[:, c, :], ps_a[c % 2][:]).then_inc(s["toks"], 1)
                        for h in range(2):
                            wait(act, "kadd", it, h + 1)
                            nc.scalar.copy(keys[h][(1 - h) * HD:(2 - h) * HD, :],
                                           keys[h][h * HD:(h + 1) * HD, :]).then_inc(s["keyT"], 1)

                        def exp(u):
                            h, c = divmod(u, TILES)
                            k = 2 * c + h
                            wait(act, "shifts", it, u + 1)
                            nc.scalar.activation(prob[u % 2][:, 0:(c + 1) * P], ps_s[u % 2][:, 0:(c + 1) * P],
                                                 ACT.Exp, bias=shift[:, k:k + 1], scale=scale[:, k:k + 1],
                                                 accum_out=row_sum[:, k:k + 1]).then_inc(s["exps"], 1)

                        def copy_turned(u):
                            c = u % TILES
                            wait(act, "turns", it, u + 1)
                            if u >= 2:
                                wait(act, "pvs", it, u - 1)
                            nc.scalar.copy(probT[u % 2][:, 0:(c + 1) * P],
                                           ps_a[u % 2][:, 0:(c + 1) * P]).then_inc(s["probTs"], 1)

                        exp(0)
                        for u in range(1, 2 * TILES):
                            exp(u)
                            copy_turned(u - 1)
                        copy_turned(2 * TILES - 1)
                        wait(act, "headT", it, 1)
                        nc.scalar.copy(headsT[:], ps_y[0][:]).then_inc(s["headTc"], 1)

            @block.vector
            def _(dve):
                nc.vector.tensor_copy(state[:, 0, :], mem["state0"][:]).then_inc(s["statec"], 1)
                begin(dve, "kmul masked zkm incs n2 n8 scales queries negs shifts inv headn xadd")
                with dve.Fori(0, PAIRS) as hp, dve.Fori(0, B) as b:
                    it = hp * B + b

                    def mask(half):
                        for h in range(2):
                            wait(dve, "lins", it, 2 * half + h + 1)
                            nc.vector.tensor_tensor(
                                lin[h][:, 2 * half:2 * half + 2, :, :].rearrange("p c a n -> p c (a n)"),
                                ps_s[h][:].rearrange("p (c n) -> p c n", c=2),
                                mem["lin_mask"][:].unsqueeze(1).broadcast_to([P, 2, 2 * P]),
                                ALU.mult).then_inc(s["masked"], 1)

                    for n, (dst, table) in enumerate(((kcos, mem["cos2"]), (ksin, mem["sin2"]))):
                        wait(dve, "proj", it, 7 + n)
                        nc.vector.tensor_tensor(dst[:], ps_a[n][:], table[:], ALU.mult).then_inc(s["kmul"], 1)
                    mask(0)
                    wait(dve, "states", it, 1)
                    for c in range(TILES - 1):
                        if c:
                            wait(dve, "statec", it, c)
                        nc.vector.tensor_tensor(state[:, c + 1, :], ps_d[:, c * P:(c + 1) * P],
                                                mem["state0"][:] if c == 0 else state[:, c, :],
                                                ALU.add).then_inc(s["statec"], 1)
                    mask(1)
                    wait(dve, "zs", it, 1)
                    for h in range(2):
                        nc.vector.tensor_tensor(
                            zk[:, :, h, :], (ps_z, ps_y[1])[h][:, 0:TILES * HD].rearrange("p (c d) -> p c d", c=TILES),
                            tok[:, :, h * P:h * P + HD], ALU.mult).then_inc(s["zkm"], 1)
                    wait(dve, "zkm", it, 2)
                    nc.vector.reduce_sum(inc[:], zk[:].rearrange("p c h d -> p (c h) d"),
                                         AX.X).then_inc(s["incs"], 1)
                    wait(dve, "ys", it, 1)
                    nc.vector.tensor_tensor(query[0][:], ps_y[0][:], mem["cos_sin"][:],
                                            ALU.mult).then_inc(s["queries"], 1)
                    wait(dve, "cum", it, 1)
                    nc.vector.tensor_scalar(norm2[:], ps_d[:, 3 * P:3 * P + 2 * TILES], float(HD * HD), 0.0,
                                            ALU.add, ALU.max).then_inc(s["n2"], 1)
                    wait(dve, "ys", it, 2)
                    nc.vector.tensor_tensor(query[1][:], ps_y[1][:], mem["cos_sin"][:],
                                            ALU.mult).then_inc(s["queries"], 1)
                    wait(dve, "pows", it, 1)
                    nc.vector.tensor_scalar(norm8[:], norm[:], EPS, float(HD) ** 0.5,
                                            ALU.add, ALU.mult).then_inc(s["n8"], 1)
                    wait(dve, "n8", it, 1)
                    nc.vector.reciprocal(scale[:], norm8[:]).then_inc(s["scales"], 1)
                    wait(dve, "scales", it, 1)
                    for u in range(2 * TILES):
                        h, c = divmod(u, TILES)
                        k = 2 * c + h
                        wait(dve, "scores", it, u + 1)
                        nc.vector.tensor_reduce(neg_max[:, k:k + 1], ps_s[u % 2][:, 0:(c + 1) * P], AX.X, ALU.max,
                                                negate=True).then_inc(s["negs"], 1)
                        wait(dve, "negs", it, u + 1)
                        nc.vector.tensor_scalar(shift[:, k:k + 1], neg_max[:, k:k + 1], scale[:, k:k + 1], None,
                                                ALU.mult).then_inc(s["shifts"], 1)
                    wait(dve, "exps", it, 2 * TILES)
                    nc.vector.reciprocal(inv_sum[:], row_sum[:]).then_inc(s["inv"], 1)
                    wait(dve, "pvs", it, 2 * TILES)
                    wait(dve, "inv", it, 1)
                    nc.vector.tensor_tensor(heads[:].rearrange("p c (h d) -> p (c h) d", h=2),
                                            ps_z[:].rearrange("p (k d) -> p k d", d=HD),
                                            inv_sum[:].unsqueeze(2).broadcast_to([P, 2 * TILES, HD]),
                                            ALU.mult).then_inc(s["headn"], 1)
                    wait(dve, "outs", it, 1)
                    x4 = mem["x"][:, bass.ds(b * SEQ, SEQ)]
                    nc.vector.tensor_tensor(x4, ps_y[1][:], x4, ALU.add).then_inc(s["xadd"], 1)

def transformer_block(nc, mem, ins, B):
    L, H, D, FEAT, FT = 6, 16, 8, 16, 4
    V = D + 1
    EPS = 1e-6 * FEAT
    SETS = 2
    TURNS = B // SETS
    ORDER = [("in", 0), ("mix", 0), ("in", 1), ("out", 0), ("mix", 1), ("ffn", 0), ("out", 1), ("ffn", 1)]
    FILLS = {"in": dict(w0=6, w1=6), "mix": dict(s0=4, s1=4, s2=4, s3=4, n0=1, n1=1),
             "out": dict(w0=1, w1=1), "ffn": dict(w0=3, w1=3)}
    BANKS = ["w0", "w1", "s0", "s1", "s2", "s3", "n0", "n1"]
    PER_TURN = {k: sum(FILLS[p].get(k, 0) for p, _ in ORDER) for k in BANKS}

    def place(bank, phase, z, n):
        return sum(FILLS[p].get(bank, 0) for p, _ in ORDER[:ORDER.index((phase, z))]) + n

    with ExitStack() as ctx:
        def sb(name, shape, dt=F32):
            return ctx.enter_context(nc.sbuf_tensor("t_" + name, shape, dt))

        def sem(name):
            return ctx.enter_context(nc.semaphore("t_" + name))

        w_sq = sb("w_sq", [P, 4, P])
        w_1 = sb("w_1", [P, FT * P])
        w_2 = sb("w_2", [P, FT, P])
        omega = sb("omega", [P, 2 * P])
        omega_s = sb("omega_s", [P, 2 * P])
        cols = sb("cols", [P, 4 + FT])
        rows = sb("rows", [P, 7, P])
        be1_bf2 = sb("be1_bf2", [P, P])
        o_now = sb("o_now", [P, TILES, P])
        o_bias = [sb(f"o_bias{z}", [P, TILES, P]) for z in range(SETS)]
        oT = sb("oT", [P, SEQ])
        proj = [sb(n, [P, SEQ]) for n in ("qT", "kT")]
        square = [sb(n, [P, SEQ]) for n in ("q2", "k2")]
        phi_q = [sb(f"phi_q{t}", [P, SEQ]) for t in range(2)]
        phi_k = [sb(f"phi_k{t}", [P, SEQ]) for t in range(2)]
        phi_kz = [[sb(f"phi_k{t}z{p}", [P, SEQ]) for p in range(2)] for t in range(2)]
        k_tok = sb("k_tok", [P, 2, TILES - 1, P])
        v_tok = sb("v_tok", [P, TILES, H, V])
        kv = sb("kv", [P, TILES - 1, 2, H * V])
        mixed = [[sb(f"mixed{i}_{r}", [P, 4, P]) for r in range(4)] for i in range(2)]
        den = sb("den", [P, TILES * H])
        inv = sb("inv", [P, TILES * H])
        att = sb("att", [P, TILES, P])
        attT = sb("attT", [P, SEQ])
        res = sb("res", [P, TILES, P])
        m = {"stats": sb("stats", [P, TILES, 6]), "mean_var": sb("mean_var", [P, TILES, 2]),
             "var_eps": sb("var_eps", [P, TILES]), "rstd": sb("rstd", [P, TILES]), "xn": sb("xn", [P, TILES, P])}
        h1T = sb("h1T", [P, SEQ])
        h1g = sb("h1g", [P, TILES, P])
        h1b = sb("h1b", [P, TILES, P])
        og = sb("og", [P, TILES, P])
        hid = [sb(f"hid{f}", [P, SEQ]) for f in range(FT)]
        ps = {k: ctx.enter_context(nc.psum_tensor("t_" + k, [P, 512], F32)) for k in BANKS}

        filled = {k: sem("filled_" + k) for k in BANKS}
        emptied = {k: sem("emptied_" + k) for k in BANKS}
        NAMES = dict(o_now=1, o_bias=1, kz=4, kv_sum=2, den=2, inv=2,
                     stats=8, mv=8, eps=2, rstd=2, xn=8, h1g=1, h1b=1, og=1, o_new=1)
        s = {n: sem(n) for n in NAMES}
        w_loaded, w_made, layer_done = sem("w_loaded"), sem("w_made"), sem("layer_done")
        ones_set = sem("ones_set")
        LOADS = 6

        with nc.Block() as block:
            @block.sync
            def _(sp):
                sp.sem_inc(layer_done, 1)
                with sp.Fori(0, L) as l:
                    sp.wait_ge(layer_done, l + 1)
                    for dst, name in ((w_sq[:].rearrange("p a n -> p (a n)"), "t_sq"), (w_1[:], "t_w1"),
                                      (w_2[:].rearrange("p a n -> p (a n)"), "t_w2"), (omega[:], "t_omega"),
                                      (cols[:], "t_cols")):
                        sp.dma_start(dst, ins[name][bass.ds(l, 1), :, :].squeeze(0)).then_inc(w_loaded, 16)
                    sp.dma_start(rows[:].rearrange("p a n -> p (a n)"),
                                 ins["t_rows"][bass.ds(l, 1), :].squeeze(0).partition_broadcast(P)).then_inc(w_loaded, 16)

            def turns(e, names, body):
                for n in names.split():
                    e.sem_inc(s[n], 1)
                with e.Fori(0, L) as l:
                    e.wait_ge(w_loaded, (l + 1) * (16 * LOADS))
                    e.wait_ge(w_made, l + 2)
                    e.nop(nofuse=True)
                    with e.Fori(0, TURNS) as tn:
                        it = l * TURNS + tn
                        for phase, z in ORDER:
                            body(phase, z, it, tn)

            def wait(e, name, it, z, n):
                e.wait_ge(s[name], (it * SETS) * NAMES[name] + (z * NAMES[name] + n + 1))

            def wait_filled(e, bank, it, phase, z, n):
                e.wait_ge(filled[bank], it * PER_TURN[bank] + (place(bank, phase, z, n) + 2))

            def wait_emptied(e, bank, it, phase, z, n):
                e.wait_ge(emptied[bank], it * PER_TURN[bank] + (place(bank, phase, z, n) + 2))

            def wait_free(e, bank, it, phase, z, n):
                e.wait_ge(emptied[bank], it * PER_TURN[bank] + (place(bank, phase, z, n) + 1))

            def chunk(c):
                return slice(c * P, (c + 1) * P)

            @block.gpsimd
            def _(pool):
                pool.sem_inc(w_made, 1)
                for n in "o_now o_bias kz kv_sum rstd h1g h1b og o_new".split():
                    pool.sem_inc(s[n], 1)
                with pool.Fori(0, L) as l:
                    pool.wait_ge(w_loaded, (l + 1) * (16 * LOADS))
                    nc.gpsimd.tensor_tensor(omega_s[:], omega[:], mem["omega_scale"][:], ALU.mult)
                    nc.gpsimd.tensor_tensor(be1_bf2[:], rows[:, 3, :], rows[:, 4, :], ALU.add).then_inc(w_made, 1)
                    with pool.Fori(0, TURNS) as tn:
                        it = l * TURNS + tn

                        def row(n):
                            return rows[:, n, :].unsqueeze(1).broadcast_to([P, TILES, P])

                        for phase, z in ORDER:
                            tokens = mem["o"][:, bass.ds((tn * SETS + z) * SEQ, SEQ)].rearrange(
                                "p (c d) -> p c d", c=TILES)
                            if phase == "in":
                                nc.gpsimd.tensor_copy(o_now[:], tokens).then_inc(s["o_now"], 1)
                                nc.gpsimd.tensor_tensor(o_bias[z][:], tokens, row(1), ALU.add).then_inc(s["o_bias"], 1)
                                for t in range(2):
                                    wait_emptied(pool, ("w0", "w1")[t], it, "in", z, 3)
                                    pool.nop(nofuse=True)
                                    for p in range(2):
                                        nc.gpsimd.tensor_scalar(phi_kz[t][p][:], phi_k[t][:],
                                                                mem["strip_head"][:, p:p + 1], None,
                                                                ALU.mult).then_inc(s["kz"], 1)
                                for bank in ("w0", "w1"):
                                    wait_emptied(pool, bank, it, "in", z, 5)
                                for c in range(1, TILES - 1):
                                    if c > 1:
                                        wait(pool, "kv_sum", it, z, c - 1)
                                    nc.gpsimd.tensor_tensor(kv[:, c, :, :], kv[:, c, :, :], kv[:, c - 1, :, :],
                                                            ALU.add).then_inc(s["kv_sum"], 1)
                            elif phase in ("out", "ffn"):
                                k = ("out", "ffn").index(phase)
                                wait(pool, "eps", it, z, k + 1)
                                nc.gpsimd.tensor_tensor(m["rstd"][:], m["var_eps"][:],
                                                        mem["minus_half"][:, 0:TILES], ALU.pow).then_inc(s["rstd"], 1)
                                wait(pool, "xn", it, z, TILES * (k + 1))
                                g, b, mid, out, one, two = (
                                    (row(2), be1_bf2[:].unsqueeze(1).broadcast_to([P, TILES, P]), h1g, h1b[:],
                                     "h1g", "h1b"),
                                    (row(5), row(6), og, tokens, "og", "o_new"))[k]
                                nc.gpsimd.tensor_tensor(mid[:], m["xn"][:], g, ALU.mult).then_inc(s[one], 1)
                                wait(pool, one, it, z, 1)
                                pool.nop(nofuse=True)
                                nc.gpsimd.tensor_tensor(out, mid[:], b, ALU.add).then_inc(s[two], 1)
                    wait(pool, "o_new", l * TURNS + (TURNS - 1), SETS - 1, 1)
                    pool.nop(nofuse=True)
                    nc.gpsimd.tensor_copy(be1_bf2[:, 0:1], be1_bf2[:, 0:1]).then_inc(layer_done, 1)

            @block.tensor
            def _(pe):
                for k in BANKS:
                    pe.sem_inc(filled[k], 1)

                def body(phase, z, it, tn):
                    def free(bank, n):
                        wait_free(pe, bank, it, phase, z, n)

                    def ready(bank, n, of=phase):
                        wait_emptied(pe, bank, it, of, z, n)

                    if phase == "in":
                        wait(pe, "o_now", it, z, 1)
                        free("w0", 0)
                        for c in range(TILES):
                            t = nc.tensor.transpose(ps["w0"][:, chunk(c)], o_now[:, c, :], mem["ident"][:])
                        t.then_inc(filled["w0"], 1)
                        ready("w0", 0)
                        free("w1", 0)
                        nc.tensor.matmul(ps["w1"][:], w_sq[:, 0, :], oT[:], start=True,
                                         stop=True).then_inc(filled["w1"], 1)
                        nc.tensor.matmul(ps["w0"][:], w_sq[:, 1, :], oT[:], start=True,
                                         stop=True).then_inc(filled["w0"], 1)
                        free("w1", 1)
                        for c in range(TILES):
                            t = nc.tensor.matmul(ps["w1"][:, chunk(c)], oT[:, chunk(c)], w_sq[:, 2, :],
                                                 start=True, stop=True)
                        t.then_inc(filled["w1"], 1)
                        for j in range(2):
                            ready(("w1", "w0")[j], (0, 1)[j])
                            for t_ in range(2):
                                bank = ("w0", "w1")[t_]
                                free(bank, 2 + j)
                                nc.tensor.matmul(ps[bank][:], omega_s[:, chunk(t_)], proj[j][:], start=True,
                                                 stop=False)
                                nc.tensor.matmul(ps[bank][:], mem["half_norm"][:, chunk(t_)], square[j][:],
                                                 start=False, stop=True).then_inc(filled[bank], 1)
                        for t_ in range(2):
                            bank = ("w0", "w1")[t_]
                            ready(bank, 3)
                            for c in range(TILES - 1):
                                t = nc.tensor.transpose(ps[bank][:, chunk(c)], phi_k[t_][:, chunk(c)],
                                                        mem["ident"][:])
                            t.then_inc(filled[bank], 1)
                        ready("w1", 1)
                        for t_ in range(2):
                            bank = ("w0", "w1")[t_]
                            ready(bank, 4)
                            for c in range(TILES - 1):
                                t = nc.tensor.matmul(ps[bank][:, c * H * V:(c + 1) * H * V], k_tok[:, t_, c, :],
                                                     v_tok[:, c, :, :].rearrange("p h d -> p (h d)"),
                                                     start=True, stop=True)
                            t.then_inc(filled[bank], 1)
                    elif phase == "mix":
                        def scores(c):
                            for r in range(4):
                                bank = f"s{r}"
                                free(bank, c)
                            for k in range(4):
                                t_, p = divmod(k, 2)
                                for r in range(4):
                                    rs = slice(32 * r, 32 * r + 32)
                                    t = nc.tensor.matmul(ps[f"s{r}"][:, chunk(k)], phi_kz[t_][p][rs, chunk(c)],
                                                         phi_q[t_][rs, chunk(c)], start=k == 0,
                                                         stop=r < 2 and k == 3, skip_group_check=True,
                                                         tile_position=(32 * r, 0))
                                    if r < 2 and k == 3:
                                        t.then_inc(filled[f"s{r}"], 1)
                            for r in (2, 3):
                                for k in range(4):
                                    t = nc.tensor.matmul(ps[f"s{r}"][:, chunk(k)], mem["ident16"][:],
                                                         mem["future16T"][:], start=False, stop=k == 3,
                                                         skip_group_check=True)
                                t.then_inc(filled[f"s{r}"], 1)

                        def weigh(c):
                            bank = f"n{c // 2}"
                            if c % 2 == 0:
                                free(bank, 0)
                            o = ps[bank][:, (c % 2) * H * V:(c % 2 + 1) * H * V]
                            if c:
                                if c > 1:
                                    wait(pe, "kv_sum", it, z, c - 1)
                                else:
                                    ready("w0", 5, "in")
                                    ready("w1", 5, "in")
                                for t_ in range(2):
                                    nc.tensor.matmul(o, phi_q[t_][:, chunk(c)], kv[:, c - 1, t_, :],
                                                     start=t_ == 0, stop=False, skip_group_check=True)
                            first = c == 0
                            for r in range(4):
                                ready(f"s{r}", c)
                                for k in range(4):
                                    t_, p = divmod(k, 2)
                                    h = 8 * t_ + 2 * r + p
                                    t = nc.tensor.matmul(o[:, h * V:(h + 1) * V], mixed[c % 2][r][:, k, :],
                                                         v_tok[:, c, h, :], start=first,
                                                         stop=r == 3 and k == 3, skip_group_check=True)
                                    first = False
                            if c % 2:
                                t.then_inc(filled[bank], 1)

                        wait(pe, "kz", it, z, 4)
                        for c in range(TILES):
                            scores(c)
                            if c >= 1:
                                weigh(c - 1)
                        weigh(TILES - 1)
                    elif phase == "out":
                        ready("n0", 0, "mix")
                        ready("n1", 0, "mix")
                        free("w0", 0)
                        for c in range(TILES):
                            t = nc.tensor.transpose(ps["w0"][:, chunk(c)], att[:, c, :], mem["ident"][:])
                        t.then_inc(filled["w0"], 1)
                        ready("w0", 0)
                        free("w1", 0)
                        for c in range(TILES):
                            t = nc.tensor.matmul(ps["w1"][:, chunk(c)], attT[:, chunk(c)], w_sq[:, 3, :],
                                                 start=True, stop=True)
                        t.then_inc(filled["w1"], 1)
                    else:
                        wait(pe, "xn", it, z, TILES)
                        free("w0", 0)
                        for c in range(TILES):
                            t = nc.tensor.transpose(ps["w0"][:, chunk(c)], m["xn"][:, c, :], mem["ident"][:])
                        t.then_inc(filled["w0"], 1)
                        ready("w0", 0)
                        for f in range(FT):
                            bank, n = (("w1", 0), ("w0", 1), ("w1", 1), ("w0", 2))[f]
                            free(bank, n)
                            nc.tensor.matmul(ps[bank][:], w_1[:, chunk(f)], h1T[:], start=True,
                                             stop=True).then_inc(filled[bank], 1)
                        free("w1", 2)
                        ready("w0", 1)
                        ready("w0", 2)
                        for c in range(TILES):
                            for f in range(FT):
                                t = nc.tensor.matmul(ps["w1"][:, chunk(c)], hid[f][:, chunk(c)], w_2[:, f, :],
                                                     start=f == 0, stop=f == FT - 1)
                        t.then_inc(filled["w1"], 1)

                turns(pe, "", body)

            @block.scalar
            def _(act):
                for k in BANKS:
                    act.sem_inc(emptied[k], 1)

                def body(phase, z, it, tn):
                    def full(bank, n):
                        wait_filled(act, bank, it, phase, z, n)

                    if phase == "in":
                        full("w0", 0)
                        nc.scalar.copy(oT[:], ps["w0"][:]).then_inc(emptied["w0"], 1)
                        for j, (bank, n) in enumerate((("w1", 0), ("w0", 1))):
                            full(bank, n)
                            nc.scalar.activation(proj[j][:], ps[bank][:], ACT.Identity, bias=cols[:, j:j + 1])
                            nc.scalar.activation(square[j][:], ps[bank][:], ACT.Square,
                                                 bias=cols[:, j:j + 1]).then_inc(emptied[bank], 1)
                        for j, phi in enumerate((phi_q, phi_k)):
                            for t_ in range(2):
                                bank = ("w0", "w1")[t_]
                                full(bank, 2 + j)
                                nc.scalar.activation(phi[t_][:], ps[bank][:], ACT.Exp).then_inc(emptied[bank], 1)
                    elif phase == "mix":
                        for c in range(TILES):
                            for r in (2, 3):
                                full(f"s{r}", c)
                                nc.scalar.activation(mixed[c % 2][r][:].rearrange("p k n -> p (k n)"), ps[f"s{r}"][:],
                                                     ACT.Relu).then_inc(emptied[f"s{r}"], 1)
                    elif phase == "out":
                        full("w0", 0)
                        nc.scalar.copy(attT[:], ps["w0"][:]).then_inc(emptied["w0"], 1)
                    else:
                        full("w0", 0)
                        nc.scalar.activation(h1T[:], ps["w0"][:], ACT.Identity, bias=cols[:, 3:4],
                                             scale=cols[:, 2:3]).then_inc(emptied["w0"], 1)
                        for f in (0, 2):
                            full("w1", f // 2)
                            nc.scalar.activation(hid[f][:], ps["w1"][:], ACT.Relu,
                                                 bias=cols[:, 4 + f:5 + f]).then_inc(emptied["w1"], 1)

                turns(act, "", body)

            @block.vector
            def _(dve):
                nc.vector.memset(v_tok[:].rearrange("p c h d -> p (c h d)"), 1.0).then_inc(ones_set, 1)
                dve.wait_ge(ones_set, 1)

                def norm(it, z, k):
                    for c in range(TILES):
                        nc.vector.bn_stats(m["stats"][:, c, :], res[:, c, :]).then_inc(s["stats"], 1)
                    wait(dve, "stats", it, z, TILES * (k + 1))
                    dve.nop(nofuse=True)
                    for c in range(TILES):
                        nc.vector.bn_aggr(m["mean_var"][:, c, :], m["stats"][:, c, :]).then_inc(s["mv"], 1)
                    wait(dve, "mv", it, z, TILES * (k + 1))
                    nc.vector.tensor_scalar(m["var_eps"][:], m["mean_var"][:, :, 1], LN_EPS, None,
                                            ALU.add).then_inc(s["eps"], 1)
                    wait(dve, "rstd", it, z, k + 1)
                    for c in range(TILES):
                        nc.vector.tensor_scalar(m["xn"][:, c, :], res[:, c, :], m["mean_var"][:, c, 0:1],
                                                m["rstd"][:, c:c + 1], ALU.subtract,
                                                ALU.mult).then_inc(s["xn"], 1)

                def body(phase, z, it, tn):
                    def full(bank, n):
                        wait_filled(dve, bank, it, phase, z, n)

                    if phase == "in":
                        full("w1", 1)
                        nc.vector.tensor_tensor(v_tok[:, :, :, 0:D],
                                                ps["w1"][:].rearrange("p (c h d) -> p c h d", c=TILES, h=H),
                                                rows[:, 0, :].rearrange("p (h d) -> p h d", h=H).unsqueeze(1)
                                                .broadcast_to([P, TILES, H, D]),
                                                ALU.add).then_inc(emptied["w1"], 1)
                        for t_ in range(2):
                            bank = ("w0", "w1")[t_]
                            full(bank, 4)
                            nc.vector.tensor_copy(k_tok[:, t_, :, :].rearrange("p c n -> p (c n)"),
                                                  ps[bank][:, 0:3 * P]).then_inc(emptied[bank], 1)
                        for t_ in range(2):
                            bank = ("w0", "w1")[t_]
                            full(bank, 5)
                            nc.vector.tensor_tensor(
                                kv[:, :, t_, :], ps[bank][:, 0:3 * H * V].rearrange("p (c n) -> p c n", c=3),
                                mem["own_head"][:, t_ * H * V:(t_ + 1) * H * V].unsqueeze(1)
                                .broadcast_to([P, 3, H * V]), ALU.mult).then_inc(emptied[bank], 1)
                    elif phase == "mix":
                        def divide(half):
                            bank = f"n{half}"
                            full(bank, 0)
                            hs = slice(2 * H * half, 2 * H * (half + 1))
                            nums = ps[bank][:, 0:2 * H * V].rearrange("p (h d) -> p h d", d=V)
                            nc.vector.tensor_scalar(den[:, hs], nums[:, :, D], EPS, None,
                                                    ALU.add).then_inc(s["den"], 1)
                            wait(dve, "den", it, z, half + 1)
                            nc.vector.reciprocal(inv[:, hs], den[:, hs]).then_inc(s["inv"], 1)
                            wait(dve, "inv", it, z, half + 1)
                            nc.vector.tensor_tensor(
                                att[:, 2 * half:2 * half + 2, :].rearrange("p c (h d) -> p (c h) d", h=H),
                                nums[:, :, 0:D], inv[:, hs].unsqueeze(2).broadcast_to([P, 2 * H, D]),
                                ALU.mult).then_inc(emptied[bank], 1)

                        for c in range(TILES):
                            for r in (0, 1):
                                full(f"s{r}", c)
                                nc.vector.tensor_tensor(mixed[c % 2][r][:], ps[f"s{r}"][:].rearrange("p (k n) -> p k n", k=4),
                                                        mem["upto"][:].unsqueeze(1).broadcast_to([P, 4, P]),
                                                        ALU.mult).then_inc(emptied[f"s{r}"], 1)
                            if c == 2:
                                divide(0)
                        divide(1)
                    elif phase == "out":
                        wait(dve, "xn", it, z, 0)
                        wait(dve, "o_bias", it, z, 1)
                        full("w1", 0)
                        nc.vector.tensor_tensor(res[:].rearrange("p c d -> p (c d)"), ps["w1"][:],
                                                o_bias[z][:].rearrange("p c d -> p (c d)"),
                                                ALU.add).then_inc(emptied["w1"], 1)
                        wait_emptied(dve, "w1", it, "out", z, 0)
                        norm(it, z, 0)
                    else:
                        for f in (1, 3):
                            full("w0", (f + 1) // 2)
                            nc.vector.tensor_scalar(hid[f][:], ps["w0"][:], cols[:, 4 + f:5 + f], 0.0,
                                                    ALU.add, ALU.max).then_inc(emptied["w0"], 1)
                        wait(dve, "xn", it, z, TILES)
                        wait(dve, "h1b", it, z, 1)
                        full("w1", 2)
                        nc.vector.tensor_tensor(res[:].rearrange("p c d -> p (c d)"), ps["w1"][:],
                                                h1b[:].rearrange("p c d -> p (c d)"),
                                                ALU.add).then_inc(emptied["w1"], 1)
                        wait_emptied(dve, "w1", it, "ffn", z, 2)
                        norm(it, z, 1)

                turns(dve, "stats mv eps xn den inv", body)

        added = sem("added")
        with nc.Block() as block:
            @block.vector
            def _(dve):
                with dve.Fori(0, B) as b:
                    x4 = mem["x"][:, bass.ds(b * SEQ, SEQ)]
                    nc.vector.tensor_tensor(x4, x4, mem["o"][:, bass.ds(b * SEQ, SEQ)], ALU.add).then_inc(added, 1)


def moe_block(nc, mem, groups, tag):
    E, K, ROUTE_SCALE = mem["experts"], 8, 2.826
    x_all = mem["x"]
    w_gate, w_up, w_down = mem["moe_gate"], mem["moe_up"], mem["moe_down"]
    with ExitStack() as ctx:
        def sb(name, shape, dt=F32):
            return ctx.enter_context(nc.sbuf_tensor(tag + name, shape, dt))

        def bank(name):
            return ctx.enter_context(nc.psum_tensor(tag + name, [P, 512], F32))

        def sem(name):
            return ctx.enter_context(nc.semaphore(tag + name))

        stats = sb("stats", [P, TILES, 6])
        mean_var = sb("mean_var", [P, TILES, 2])
        var_eps = sb("var_eps", [P, TILES])
        rstd = sb("rstd", [P, TILES])
        xn = sb("xn", [P, TILES, P])
        xT = sb("xT", [P, SEQ])
        score = sb("score", [P, TILES, E])
        select = sb("select", [P, TILES, E])
        top8 = sb("top8", [P, TILES, 8])
        rest = sb("rest", [P, TILES, E])
        chosen = sb("chosen", [P, TILES, E])
        picked = sb("picked", [P, TILES, E])
        total = sb("total", [P, TILES])
        inv_total = sb("inv_total", [P, TILES])
        combine = sb("combine", [P, TILES, E])
        silu = [sb(f"silu{i}", [P, SEQ]) for i in range(2)]
        hidden = [sb(f"hidden{i}", [P, SEQ]) for i in range(2)]
        acc = sb("acc", [P, TILES, P])
        ps_g = [bank(f"ps_g{i}") for i in range(2)]
        ps_u = [bank(f"ps_u{i}") for i in range(2)]
        ps_y = [bank(f"ps_y{i}") for i in range(2)]
        ps_t = bank("ps_t")
        ps_gate = bank("ps_gate")

        stats_done, mv_done, eps_done = sem("stats_done"), sem("mv_done"), sem("eps_done")
        rstd_done, xn_done, turned, xT_done = sem("rstd_done"), sem("xn_done"), sem("turned"), sem("xT_done")
        gates_done, score_done, route_step = sem("gates_done"), sem("score_done"), sem("route_step")
        g_done, u_done, silu_done, hid_done = sem("g_done"), sem("u_done"), sem("silu_done"), sem("hid_done")
        y_done, acc_done, group_done = sem("y_done"), sem("acc_done"), sem("group_done")
        N = E + 1
        ROUTE = 3 + 3 * TILES
        with nc.Block() as block:

            @block.tensor
            def _(pe):
                with pe.Fori(0, groups) as g:
                    pe.wait_ge(xn_done, g * TILES + TILES)
                    for c in range(TILES):
                        t = nc.tensor.transpose(ps_t[:, c * P:(c + 1) * P], xn[:, c, :], mem["ident"][:])
                    t.then_inc(turned, 1)
                    pe.wait_ge(xT_done, g + 1)
                    for c in range(TILES):
                        t = nc.tensor.matmul(ps_gate[:, c * E:(c + 1) * E], xT[:, c * P:(c + 1) * P],
                                             mem["router"][:], start=True, stop=True)
                    t.then_inc(gates_done, 1)

                    def down(e):
                        pe.wait_ge(hid_done, g * N + e + 1)
                        if e >= 2:
                            pe.wait_ge(acc_done, g * N + e - 1)
                        else:
                            pe.wait_ge(group_done, g + 1)
                        for c in range(TILES):
                            t = nc.tensor.matmul(ps_y[e % 2][:, c * P:(c + 1) * P],
                                                 hidden[e % 2][:, c * P:(c + 1) * P],
                                                 w_down[:, e * P:(e + 1) * P], start=True, stop=True)
                        t.then_inc(y_done, 1)

                    for e in range(N):
                        if e >= 2:
                            pe.wait_ge(silu_done, g * N + e - 1)
                        nc.tensor.matmul(ps_g[e % 2][:], w_gate[:, e * P:(e + 1) * P], xT[:],
                                         start=True, stop=True).then_inc(g_done, 1)
                        if e >= 2:
                            pe.wait_ge(hid_done, g * N + e - 1)
                        nc.tensor.matmul(ps_u[e % 2][:], w_up[:, e * P:(e + 1) * P], xT[:],
                                         start=True, stop=True).then_inc(u_done, 1)
                        if e >= 1:
                            down(e - 1)
                    down(N - 1)

            @block.scalar
            def _(act):
                with act.Fori(0, groups) as g:
                    act.wait_ge(turned, g + 1)
                    nc.scalar.copy(xT[:], ps_t[:]).then_inc(xT_done, 1)
                    act.wait_ge(gates_done, g + 1)
                    act.wait_ge(route_step, g * ROUTE + 1)
                    nc.scalar.activation(score[:].rearrange("p c e -> p (c e)"), ps_gate[:, 0:TILES * E],
                                         ACT.Sigmoid).then_inc(score_done, 1)
                    for e in range(N):
                        act.wait_ge(g_done, g * N + e + 1)
                        if e >= 2:
                            act.wait_ge(hid_done, g * N + e - 1)
                        nc.scalar.activation(silu[e % 2][:], ps_g[e % 2][:], ACT.Silu).then_inc(silu_done, 1)

            @block.gpsimd
            def _(pool):
                with pool.Fori(0, groups) as g:
                    pool.wait_ge(eps_done, g + 1)
                    nc.gpsimd.tensor_tensor(rstd[:], var_eps[:], mem["minus_half"][:, 0:TILES],
                                            ALU.pow).then_inc(rstd_done, 1)

            @block.vector
            def _(dve):
                dve.sem_inc(group_done, 1)
                dve.sem_inc(route_step, 1)
                with dve.Fori(0, groups) as g:
                    def x_tile(c, n=1):
                        return x_all[:, bass.ds(g * SEQ + c * P, n * P)]

                    for c in range(TILES):
                        nc.vector.bn_stats(stats[:, c, :], x_tile(c)).then_inc(stats_done, 1)
                    dve.wait_ge(stats_done, (g + 1) * TILES)
                    dve.nop(nofuse=True)
                    for c in range(TILES):
                        nc.vector.bn_aggr(mean_var[:, c, :], stats[:, c, :]).then_inc(mv_done, 1)
                    dve.wait_ge(mv_done, (g + 1) * TILES)
                    nc.vector.tensor_scalar(var_eps[:], mean_var[:, :, 1], LN_EPS, None,
                                            ALU.add).then_inc(eps_done, 1)
                    dve.wait_ge(rstd_done, g + 1)
                    for c in range(TILES):
                        nc.vector.tensor_scalar(xn[:, c, :], x_tile(c), mean_var[:, c, 0:1], rstd[:, c:c + 1],
                                                ALU.subtract, ALU.mult).then_inc(xn_done, 1)

                    dve.wait_ge(score_done, g + 1)
                    nc.vector.tensor_tensor(select[:], score[:],
                                            mem["expert_bias"][:].unsqueeze(1).broadcast_to([P, TILES, E]),
                                            ALU.add).then_inc(route_step, 1)
                    dve.wait_ge(route_step, g * ROUTE + 2)
                    dve.nop(nofuse=True)
                    for c in range(TILES):
                        nc.vector.max(top8[:, c, :], select[:, c, :]).then_inc(route_step, 1)
                    dve.wait_ge(route_step, g * ROUTE + 2 + TILES)
                    dve.nop(nofuse=True)
                    for c in range(TILES):
                        nc.vector.match_replace(rest[:, c, :], top8[:, c, :], select[:, c, :],
                                                -3.0e38).then_inc(route_step, 1)
                    dve.wait_ge(route_step, g * ROUTE + 2 + 2 * TILES)
                    nc.vector.tensor_tensor(chosen[:], rest[:], select[:], ALU.not_equal).then_inc(route_step, 1)
                    dve.wait_ge(route_step, g * ROUTE + 3 + 2 * TILES)
                    nc.vector.tensor_tensor(picked[:], chosen[:], score[:], ALU.mult).then_inc(route_step, 1)
                    dve.wait_ge(route_step, g * ROUTE + 4 + 2 * TILES)
                    nc.vector.reduce_sum(total[:], picked[:], AX.X).then_inc(route_step, 1)
                    dve.wait_ge(route_step, g * ROUTE + 5 + 2 * TILES)
                    nc.vector.reciprocal(inv_total[:], total[:]).then_inc(route_step, 1)
                    dve.wait_ge(route_step, g * ROUTE + 6 + 2 * TILES)
                    nc.vector.scalar_tensor_tensor(combine[:], picked[:], ROUTE_SCALE,
                                                   inv_total[:].unsqueeze(2).broadcast_to([P, TILES, E]),
                                                   ALU.mult, ALU.mult).then_inc(route_step, TILES - 2)

                    def gather(e):
                        dve.wait_ge(y_done, g * N + e + 1)
                        if e == 0:
                            dve.wait_ge(route_step, g * ROUTE + (ROUTE + 1))
                        elif e >= 1:
                            dve.wait_ge(acc_done, g * N + e)
                        for c in range(TILES):
                            y = ps_y[e % 2][:, c * P:(c + 1) * P]
                            if e == 0:
                                t = nc.vector.tensor_scalar(acc[:, c, :], y, combine[:, c, 0:1], None, ALU.mult)
                            elif e < E:
                                t = nc.vector.scalar_tensor_tensor(acc[:, c, :], y, combine[:, c, e:e + 1],
                                                                   acc[:, c, :], ALU.mult, ALU.add)
                        if e == E:
                            t = nc.vector.tensor_tensor(acc[:].rearrange("p c d -> p (c d)"), ps_y[e % 2][:],
                                                        acc[:].rearrange("p c d -> p (c d)"), ALU.add)
                        t.then_inc(acc_done, 1)

                    for e in range(N):
                        dve.wait_ge(silu_done, g * N + e + 1)
                        dve.wait_ge(u_done, g * N + e + 1)
                        if e >= 2:
                            dve.wait_ge(y_done, g * N + e - 1)
                        nc.vector.tensor_tensor(hidden[e % 2][:], silu[e % 2][:], ps_u[e % 2][:],
                                                ALU.mult).then_inc(hid_done, 1)
                        if e >= 1:
                            gather(e - 1)
                    gather(N - 1)
                    dve.wait_ge(acc_done, g * N + N)
                    nc.vector.tensor_tensor(x_tile(0, TILES), x_tile(0, TILES),
                                            acc[:].rearrange("p c d -> p (c d)"), ALU.add).then_inc(group_done, 1)


def build(nc, ins, out, stages):
    B = ins["x"].shape[0]
    with ExitStack() as ctx:
        mem = {}

        def keep(name, shape, dt=F32):
            mem[name] = ctx.enter_context(nc.sbuf_tensor(name, shape, dt))
            return mem[name]

        keep("x", [P, B * SEQ])
        keep("ident", [P, P])
        keep("minus_half", [P, 16])
        E = ins["router"].shape[1]
        mem["experts"] = E
        for n in ("moe_gate", "moe_up", "moe_down"):
            keep(n, [P, (E + 1) * P])
        keep("plus_half", [P, 16])
        keep("xT", [P, B * SEQ])
        mem["o"] = mem["xT"]
        names = ["ident", "router", "moe_gate", "moe_up", "moe_down"]
        for n in ("twos_upto", "twos", "state0", "lin_mask", "cos2", "sin2", "cos_sin", "ident16", "future16",
                  "future16T", "upto", "omega_scale", "half_norm", "own_head", "strip_head"):
            keep(n, list(ins[n].shape), ins[n].dtype)
            names.append(n)
        keep("b_out4", [P, SEQ])
        keep("router", [P, E])
        keep("expert_bias", [P, E])
        loaded = ctx.enter_context(nc.semaphore("loaded"))
        consts = ctx.enter_context(nc.semaphore("consts"))
        stored = ctx.enter_context(nc.semaphore("stored"))
        loads = [(mem["x"][:].rearrange("p (t d) -> p t d", d=P),
                  ins["x"].rearrange("b (c p) d -> p (b c) d", p=P))]
        for n in names:
            loads.append((mem[n][:], ins[n]))
        loads.append((mem["expert_bias"][:], ins["expert_bias"].partition_broadcast(P)))
        for c in range(TILES):
            loads.append((mem["b_out4"][:, c * P:(c + 1) * P], ins["b_out"].partition_broadcast(P)))
        with nc.Block() as block:
            @block.sync
            def _(sp):
                for dst, src in loads:
                    sp.dma_start(dst, src).then_inc(loaded, 16)
                sp.wait_ge(loaded, 16 * len(loads))

            @block.vector
            def _(dve):
                nc.vector.memset(mem["minus_half"][:], -0.5).then_inc(consts, 1)
                nc.vector.memset(mem["plus_half"][:], 0.5).then_inc(consts, 1)
                dve.wait_ge(consts, 2)
        for n, s in enumerate(stages):
            tag = f"{s}{n}_"
            if s == "a":
                norm_block(nc, mem, B, attention=True, tag=tag)
                attention_block(nc, mem, ins, B)
            if s == "b":
                norm_block(nc, mem, B, attention=False, tag=tag)
                transformer_block(nc, mem, ins, B)
            if s == "ffn":
                moe_block(nc, mem, B, tag)
        with nc.Block() as block:
            @block.sync
            def _(sp):
                sp.dma_start(out.rearrange("b (c p) d -> p (b c) d", p=P),
                             mem["x"][:].rearrange("p (t d) -> p t d", d=P)).then_inc(stored, 16)
                sp.wait_ge(stored, 16)


def lay_out(t):
    f = "L0_ffn_"
    a = {"x": t["L0_attn_a_X"], "expert_bias": t[f + "expert_bias"],
         "router": t[f + "gate_w"].T, "ident": np.eye(P, dtype=np.float32)}
    for name, experts, shared in (("moe_gate", "w_gate", "shared_gate_w"), ("moe_up", "w_up", "shared_up_w"),
                                  ("moe_down", "w_down", "shared_down_w")):
        w = np.concatenate([t[f + experts], t[f + shared][None]], axis=0)
        a[name] = w.transpose(2, 0, 1).reshape(P, -1)
    f = "L0_attn_a_"
    HHD = t[f + "w_out"].shape[0]
    HD, pairs = 64, HHD // P
    q, k, v = (t[f + "w_qkv"][:, i * HHD:(i + 1) * HHD] for i in range(3))
    kk, vk = (t[f + "w_kvkv"][:, i * HHD:(i + 1) * HHD] for i in range(2))
    blocks = [w.reshape(P, pairs, P).transpose(1, 0, 2) for w in (q, vk, k, kk, v)]
    a["pairs"] = np.concatenate(blocks + [t[f + "w_out"].reshape(pairs, P, P)], axis=2)
    a["b_out"] = t[f + "b_out"]
    a.update(tables(HD))
    f = "L0_attn_b_"
    L = t[f + "Wq"].shape[0]
    a["t_sq"] = np.concatenate([t[f + n] for n in ("Wq", "Wk", "Wv", "Wo")], axis=2)
    a["t_w1"] = t[f + "W1"]
    a["t_w2"] = t[f + "W2"].reshape(L, -1, P, P).transpose(0, 2, 1, 3).reshape(L, P, -1)
    heads, _, at = feature_places()
    omega = np.zeros((L, P, 2 * P), np.float32)
    for col in range(2 * P):
        omega[:, heads[col] * 8:heads[col] * 8 + 8, col] = t[f + "omega"][:, :, at[col]]
    a["t_omega"] = omega
    columns = [t[f + n][:, :, None] for n in ("bq", "bk", "g1", "be1")]
    a["t_cols"] = np.concatenate(columns + [t[f + "bf1"].reshape(L, -1, P).transpose(0, 2, 1)], axis=2)
    a["t_rows"] = np.concatenate([t[f + n] for n in ("bv", "bo", "g1", "be1", "bf2", "g2", "be2")], axis=1)
    return a


def feature_places():
    col = np.arange(2 * P)
    half, strip, head, sign, m = col // P, col // 32 % 4, col // 16 % 2, 1 - 2 * (col // 8 % 2), col % 8
    return 8 * half + 2 * strip + head, sign, m


def tables(HD):
    f32 = np.float32
    i, j = np.arange(P)[:, None], np.arange(P)[None, :]
    freq = (f32(1.0) / f32(10000.0) ** (np.arange(0, HD, 2, dtype=f32) / f32(HD))).astype(f32)
    angle = np.repeat(np.arange(SEQ, dtype=f32)[:, None] * freq[None, :], 2, axis=1).T
    cos, sin = np.cos(angle).astype(f32), np.sin(angle).astype(f32)
    eye = np.eye(HD, dtype=f32) * f32(HD ** 0.5)
    turned = np.zeros((HD, HD), f32)
    turned[1::2, 0::2] = -eye[0::2, 0::2]
    turned[0::2, 1::2] = eye[0::2, 0::2]
    state0 = np.concatenate([eye, turned], axis=1)
    bf16 = mybir.dt.np(BF16)
    heads, sign, _ = feature_places()
    root = 8 ** -0.25
    of_head = (np.arange(P)[:, None] // 8 == heads[None, :]).astype(f32)
    own = (heads.reshape(2, P, 1) == np.arange(16 * 9)[None, None, :] // 9).astype(f32)
    return {
        "future16T": np.where(i > j, -1e30, 0.0).astype(bf16), "upto": (i <= j).astype(f32),
        "omega_scale": np.tile((sign * root).astype(f32), (P, 1)),
        "half_norm": (of_head * f32(-0.5 * root * root)).astype(f32),
        "own_head": own.transpose(1, 0, 2).reshape(P, -1),
        "strip_head": np.stack([(np.arange(P) // 16 % 2 == p) for p in range(2)], axis=1).astype(f32),
        "twos_upto": 2.0 * (i <= j).astype(f32), "twos": np.full((P, P), 2.0, f32),
        "state0": np.concatenate([state0, state0], axis=0),
        "lin_mask": np.concatenate([(i <= j), (i < j) + 0.5 * (i == j)], axis=1).astype(f32),
        "cos2": np.concatenate([cos, cos]), "sin2": np.concatenate([sin, sin]),
        "cos_sin": np.concatenate([cos, sin]),
        "ident16": np.eye(P).astype(bf16), "future16": np.where(j > i, -1e30, 0.0).astype(bf16),
    }


def kernel(**inputs):
    import concourse.bacc as bacc
    from concourse.bass_utils import run_bass_kernel_spmd

    t = {k: np.asarray(v) for k, v in inputs.items()}
    arrays = {k: np.ascontiguousarray(v) for k, v in lay_out(t).items()}
    nc = bacc.Bacc("TRN2", target_bir_lowering=False, num_devices=1)
    ins = {k: nc.dram_tensor("in_" + k, list(v.shape), mybir.dt.from_np(v.dtype), kind="ExternalInput").ap()
           for k, v in arrays.items()}
    out = nc.dram_tensor("out", list(arrays["x"].shape), F32, kind="ExternalOutput").ap()
    build(nc, ins, out, STAGES)
    r = run_bass_kernel_spmd(nc, [{"in_" + k: v for k, v in arrays.items()}], core_ids=[0])
    return r.results[0]["out"]
```

```python
from contextlib import ExitStack

import concourse.bass as bass
import concourse.mybir as mybir
import numpy as np

F32 = mybir.dt.float32
BF16 = mybir.dt.bfloat16
ALU = mybir.AluOpType
ACT = mybir.ActivationFunctionType
AX = mybir.AxisListType
P = 128
TILES = 4
SEQ = TILES * P
LN_EPS = 1e-5

STAGES = ("a", "ffn", "b", "ffn")

def layernorm_steps(nc, dve, m, s, g, read):
    for c in range(TILES):
        nc.vector.bn_stats(m["stats"][:, c, :], read(c)).then_inc(s["stats_done"], 1)
    dve.wait_ge(s["stats_done"], (g + 1) * TILES)
    dve.nop(nofuse=True)
    for c in range(TILES):
        nc.vector.bn_aggr(m["mean_var"][:, c, :], m["stats"][:, c, :]).then_inc(s["mv_done"], 1)
    dve.wait_ge(s["mv_done"], (g + 1) * TILES)
    nc.vector.tensor_scalar(m["var_eps"][:], m["mean_var"][:, :, 1], LN_EPS, None,
                            ALU.add).then_inc(s["eps_done"], 1)
    dve.wait_ge(s["rstd_done"], g + 1)
    for c in range(TILES):
        nc.vector.tensor_scalar(m["xn"][:, c, :], read(c), m["mean_var"][:, c, 0:1], m["rstd"][:, c:c + 1],
                                ALU.subtract, ALU.mult).then_inc(s["xn_done"], 1)


def norm_block(nc, mem, groups, attention, tag):
    with ExitStack() as ctx:
        def sb(name, shape, dt=F32):
            return ctx.enter_context(nc.sbuf_tensor(tag + name, shape, dt))

        def sem(name):
            return ctx.enter_context(nc.semaphore(tag + name))

        m = {"stats": sb("stats", [P, TILES, 6]), "mean_var": sb("mean_var", [P, TILES, 2]),
             "var_eps": sb("var_eps", [P, TILES]), "rstd": sb("rstd", [P, TILES]),
             "xn": sb("xn", [P, TILES, P])}
        s = {n: sem(n) for n in ("stats_done", "mv_done", "eps_done", "rstd_done", "xn_done")}
        turned, xT_done, out_done = sem("turned"), sem("xT_done"), sem("out_done")
        ps_t = ctx.enter_context(nc.psum_tensor(tag + "ps_t", [P, 512], F32))
        with nc.Block() as block:
            @block.vector
            def _(dve):
                with dve.Fori(0, groups) as g:
                    x4 = mem["x"][:, bass.ds(g * SEQ, SEQ)]
                    layernorm_steps(nc, dve, m, s, g, lambda c: mem["x"][:, bass.ds(g * SEQ + c * P, P)])
                    dve.wait_ge(s["xn_done"], (g + 1) * TILES)
                    if attention:
                        nc.vector.tensor_tensor(
                            x4, x4, mem["b_out4"][:], ALU.add).then_inc(out_done, 1)
                        dve.wait_ge(turned, g + 1)
                    else:
                        nc.vector.tensor_copy(mem["o"][:, bass.ds(g * SEQ, SEQ)],
                                              m["xn"][:].rearrange("p c d -> p (c d)")).then_inc(out_done, 1)

            @block.gpsimd
            def _(pool):
                with pool.Fori(0, groups) as g:
                    pool.wait_ge(s["eps_done"], g + 1)
                    nc.gpsimd.tensor_tensor(m["rstd"][:], m["var_eps"][:], mem["minus_half"][:, 0:TILES],
                                            ALU.pow).then_inc(s["rstd_done"], 1)

            if attention:
                @block.tensor
                def _(pe):
                    with pe.Fori(0, groups) as g:
                        pe.wait_ge(s["xn_done"], g * TILES + TILES)
                        pe.wait_ge(xT_done, g + 1)
                        for c in range(TILES):
                            t = nc.tensor.transpose(ps_t[:, c * P:(c + 1) * P], m["xn"][:, c, :], mem["ident"][:])
                        t.then_inc(turned, 1)

                @block.scalar
                def _(act):
                    act.sem_inc(xT_done, 1)
                    with act.Fori(0, groups) as g:
                        act.wait_ge(turned, g + 1)
                        nc.scalar.copy(mem["xT"][:, bass.ds(g * SEQ, SEQ)], ps_t[:]).then_inc(xT_done, 1)


def attention_block(nc, mem, ins, B):
    H, HD, EPS = 16, 64, 1e-8
    PAIRS = H // 2
    with ExitStack() as ctx:
        def sb(name, shape, dt=F32):
            return ctx.enter_context(nc.sbuf_tensor("a_" + name, shape, dt))

        def bank(name):
            return ctx.enter_context(nc.psum_tensor("a_" + name, [P, 512], F32))

        def sem(name):
            return ctx.enter_context(nc.semaphore("a_" + name))

        staged = sb("staged", [P, 6 * P])
        w_qvk = sb("w_qvk", [P, 3 * P])
        w_rk = sb("w_rk", [P, P])
        w_tok = sb("w_tok", [P, 4 * P])
        w_o = sb("w_o", [P, P])
        xTb = sb("xTb", [P, SEQ])
        qv = sb("qv", [P, TILES, 2, P])
        tok = sb("tok", [P, TILES, 4 * P])
        kcos, ksin = sb("kcos", [P, SEQ]), sb("ksin", [P, SEQ])
        keys = [sb(f"keys{h}", [P, SEQ]) for h in range(2)]
        state = sb("state", [P, TILES, P])
        lin = [sb(f"lin{h}", [P, TILES, 2, P]) for h in range(2)]
        zk = sb("zk", [P, TILES, 2, HD])
        inc = sb("inc", [P, 2 * TILES])
        norm2 = sb("norm2", [P, 2 * TILES])
        norm = sb("norm", [P, 2 * TILES])
        norm8 = sb("norm8", [P, 2 * TILES])
        scale = sb("scale", [P, 2 * TILES])
        query = [sb(f"query{h}", [P, SEQ]) for h in range(2)]
        neg_max = sb("neg_max", [P, 2 * TILES])
        shift = sb("shift", [P, 2 * TILES])
        row_sum = sb("row_sum", [P, 2 * TILES])
        inv_sum = sb("inv_sum", [P, 2 * TILES])
        prob = [sb(f"prob{i}", [P, SEQ]) for i in range(2)]
        probT = [sb(f"probT{i}", [P, SEQ]) for i in range(2)]
        heads = sb("heads", [P, TILES, 2 * HD])
        headsT = sb("headsT", [P, SEQ])
        ps_a = [bank(f"ps_a{i}") for i in range(2)]
        ps_s = [bank(f"ps_s{i}") for i in range(2)]
        ps_y = [bank(f"ps_y{i}") for i in range(2)]
        ps_z = bank("ps_z")
        ps_d = bank("ps_d")

        NAMES = dict(proj=8, states=1, lins=4, zs=1, cum=1, ys=2, scores=8, turns=8, pvs=8, headT=1, outs=1,
                     qvs=2, toks=4, keyT=2, exps=8, probTs=8, headTc=1,
                     kmul=2, statec=3, masked=4, zkm=2, incs=1, n2=1, n8=1, scales=1, queries=2, negs=8,
                     shifts=8, inv=1, headn=1, xadd=1, xcopy=1, kadd=2, pows=1)
        s = {n: sem(n) for n in NAMES}
        w_loaded, w_act, w_pool = sem("w_loaded"), sem("w_act"), sem("w_pool")

        def begin(e, names):
            for n in names.split():
                e.sem_inc(s[n], 1)

        def wait(e, name, it, n):
            e.wait_ge(s[name], it * NAMES[name] + (n + 1))

        def flat(ap):
            return ap.rearrange("p a b c -> p (a b c)") if len(ap.shape) == 4 else ap.rearrange("p a b -> p (a b)")

        with nc.Block() as block:
            @block.sync
            def _(sp):
                sp.sem_inc(w_act, 1)
                sp.sem_inc(w_pool, 1)
                with sp.Fori(0, PAIRS) as hp:
                    sp.wait_ge(w_act, hp + 1)
                    sp.wait_ge(w_pool, hp + 1)
                    sp.dma_start(staged[:], ins["pairs"][bass.ds(hp, 1), :, :].squeeze(0)).then_inc(w_loaded, 16)

            @block.gpsimd
            def _(pool):
                begin(pool, "xcopy kadd pows")
                with pool.Fori(0, PAIRS) as hp:
                    pool.wait_ge(w_loaded, hp * 16 + 16)
                    wait(pool, "outs", hp * B, 0)
                    pool.nop(nofuse=True)
                    k_, kk_ = staged[:, 2 * P:3 * P], staged[:, 3 * P:4 * P]
                    nc.gpsimd.tensor_scalar(w_rk[:, 0:P:2], k_[:, 1:P:2], -1.0, None, ALU.mult)
                    nc.gpsimd.tensor_copy(w_rk[:, 1:P:2], k_[:, 0:P:2])
                    for h in range(2):
                        kk_h = kk_[:, h * HD:(h + 1) * HD]
                        at = h * P
                        nc.gpsimd.tensor_copy(w_tok[:, at:at + HD], kk_h)
                        nc.gpsimd.tensor_scalar(w_tok[:, at + HD:at + P:2], kk_h[:, 1:HD:2], -1.0, None, ALU.mult)
                        t = nc.gpsimd.tensor_copy(w_tok[:, at + HD + 1:at + P:2], kk_h[:, 0:HD:2])
                    t.then_inc(w_pool, 1)
                    with pool.Fori(0, B) as b:
                        it = hp * B + b
                        wait(pool, "proj", it, 0)
                        pool.nop(nofuse=True)
                        nc.gpsimd.tensor_copy(xTb[:], mem["xT"][:, bass.ds(b * SEQ, SEQ)]).then_inc(s["xcopy"], 1)
                        wait(pool, "kmul", it, 2)
                        for h in range(2):
                            r = slice(h * HD, (h + 1) * HD)
                            nc.gpsimd.tensor_tensor(keys[h][r, :], kcos[r, :], ksin[r, :],
                                                    ALU.add).then_inc(s["kadd"], 1)
                            wait(pool, "kadd", it, h + 1)
                        wait(pool, "n2", it, 1)
                        nc.gpsimd.tensor_tensor(norm[:], norm2[:], mem["plus_half"][:, 0:2 * TILES],
                                                ALU.pow).then_inc(s["pows"], 1)

            @block.tensor
            def _(pe):
                begin(pe, "proj states lins zs cum ys scores turns pvs headT outs")
                with pe.Fori(0, PAIRS) as hp:
                    pe.wait_ge(w_act, hp + 2)
                    pe.wait_ge(w_pool, hp + 2)
                    pe.nop(nofuse=True)
                    with pe.Fori(0, B) as b:
                        it = hp * B + b
                        wait(pe, "xcopy", it, 1)
                        for n in range(8):
                            if n == 0:
                                wait(pe, "probTs", it, 0)
                            elif n in (2, 3):
                                wait(pe, "qvs", it, n - 1)
                            elif n >= 4:
                                wait(pe, "toks", it, n - 3)
                            o = ps_a[n % 2][:]
                            if n in (0, 1, 6, 7):
                                w = {0: w_qvk[:, P:2 * P], 1: w_qvk[:, 0:P], 6: w_qvk[:, 2 * P:3 * P],
                                     7: w_rk[:]}[n]
                                t = nc.tensor.matmul(o, w, xTb[:], start=True, stop=True)
                            else:
                                t = nc.tensor.matmul(o, xTb[:, (n - 2) * P:(n - 1) * P], w_tok[:],
                                                     start=True, stop=True)
                            t.then_inc(s["proj"], 1)

                        def rows(h):
                            return slice(h * HD, (h + 1) * HD)

                        def lin_scores(half):
                            for h in range(2):
                                if half:
                                    wait(pe, "masked", it, 1 + h)
                                for c in (2 * half, 2 * half + 1):
                                    t = nc.tensor.matmul(ps_s[h][:, (c % 2) * 2 * P:(c % 2 + 1) * 2 * P],
                                                         qv[rows(h), c, 1, :],
                                                         qv[rows(h), c, :, :].rearrange("p a n -> p (a n)"),
                                                         start=True, stop=True)
                                t.then_inc(s["lins"], 1)

                        wait(pe, "qvs", it, 2)
                        lin_scores(0)
                        wait(pe, "toks", it, 4)
                        for c in range(TILES - 1):
                            for h in range(2):
                                t = nc.tensor.matmul(ps_d[rows(h), c * P:(c + 1) * P],
                                                     tok[:, c, 3 * P + h * HD:3 * P + (h + 1) * HD],
                                                     tok[:, c, h * P:(h + 1) * P], start=True, stop=True)
                        t.then_inc(s["states"], 1)
                        lin_scores(1)
                        wait(pe, "statec", it, 3)
                        wait(pe, "masked", it, 4)
                        wait(pe, "xadd", it, 0)
                        for c in range(TILES):
                            for h in range(2):
                                o = (ps_z, ps_y[1])[h][:, c * HD:(c + 1) * HD]
                                nc.tensor.matmul(o, lin[h][:, c, 1, :], tok[:, c, h * P:h * P + HD],
                                                 start=True, stop=False)
                                t = nc.tensor.matmul(o, qv[rows(h), c, 1, :], state[rows(h), c, 0:HD],
                                                     start=False, stop=True)
                        t.then_inc(s["zs"], 1)

                        def ys(h):
                            for c in range(TILES):
                                o = ps_y[h][:, c * P:(c + 1) * P]
                                nc.tensor.matmul(o, tok[:, c, h * P:(h + 1) * P], lin[h][:, c, 0, :],
                                                 start=True, stop=False)
                                t = nc.tensor.matmul(o, state[rows(h), c, :], qv[rows(h), c, 0, :],
                                                     start=False, stop=True)
                            t.then_inc(s["ys"], 1)

                        ys(0)
                        wait(pe, "incs", it, 1)
                        N2 = 2 * TILES
                        o = ps_d[:, 3 * P:3 * P + N2]
                        nc.tensor.matmul(o, mem["twos_upto"][:], inc[:], start=True, stop=False)
                        for back in range(1, TILES):
                            t = nc.tensor.matmul(o[:, 2 * back:N2], mem["twos"][:], inc[:, 0:N2 - 2 * back],
                                                 start=False, stop=back == TILES - 1)
                        t.then_inc(s["cum"], 1)
                        ys(1)

                        def scores(u):
                            h, c = divmod(u, TILES)
                            if c == 0:
                                wait(pe, "queries", it, h + 1)
                                wait(pe, "keyT", it, h + 1)
                                wait(pe, "kadd", it, 2)
                            if u >= 2:
                                wait(pe, "exps", it, u - 1)
                            o = ps_s[u % 2]
                            nc.tensor.matmul(o[:, 0:(c + 1) * P], query[h][:, c * P:(c + 1) * P],
                                             keys[h][:, 0:(c + 1) * P], start=True, stop=False)
                            nc.tensor.matmul(o[:, c * P:(c + 1) * P], mem["ident16"][:], mem["future16"][:],
                                             start=False, stop=True).then_inc(s["scores"], 1)

                        def turn(u):
                            c = u % TILES
                            wait(pe, "exps", it, u + 1)
                            if u < 2:
                                wait(pe, "kmul", it, u + 1)
                            else:
                                wait(pe, "probTs", it, u - 1)
                            for j in range(c + 1):
                                t = nc.tensor.transpose(ps_a[u % 2][:, j * P:(j + 1) * P],
                                                        prob[u % 2][:, j * P:(j + 1) * P], mem["ident"][:])
                            t.then_inc(s["turns"], 1)

                        def weigh(u):
                            h, c = divmod(u, TILES)
                            wait(pe, "probTs", it, u + 1)
                            for j in range(c + 1):
                                t = nc.tensor.matmul(ps_z[:, (2 * c + h) * HD:(2 * c + h + 1) * HD],
                                                     probT[u % 2][:, j * P:(j + 1) * P],
                                                     tok[:, j, 2 * P + h * HD:2 * P + (h + 1) * HD],
                                                     start=j == 0, stop=j == c)
                            t.then_inc(s["pvs"], 1)

                        U = 2 * TILES
                        for u in range(U + 2):
                            if u < U:
                                scores(u)
                            if 1 <= u <= U:
                                turn(u - 1)
                            if u >= 2:
                                weigh(u - 2)
                        wait(pe, "headn", it, 1)
                        for c in range(TILES):
                            t = nc.tensor.transpose(ps_y[0][:, c * P:(c + 1) * P], heads[:, c, :], mem["ident"][:])
                        t.then_inc(s["headT"], 1)
                        wait(pe, "headTc", it, 1)
                        for c in range(TILES):
                            t = nc.tensor.matmul(ps_y[1][:, c * P:(c + 1) * P], headsT[:, c * P:(c + 1) * P],
                                                 w_o[:], start=True, stop=True)
                        t.then_inc(s["outs"], 1)

            @block.scalar
            def _(act):
                begin(act, "qvs toks keyT exps probTs headTc")
                with act.Fori(0, PAIRS) as hp:
                    act.wait_ge(w_loaded, hp * 16 + 16)
                    wait(act, "outs", hp * B, 0)
                    nc.scalar.copy(w_qvk[:], staged[:, 0:3 * P])
                    nc.scalar.copy(w_tok[:, 2 * P:3 * P], staged[:, 4 * P:5 * P])
                    nc.scalar.copy(w_tok[:, 3 * P:4 * P], staged[:, P:2 * P])
                    nc.scalar.copy(w_o[:], staged[:, 5 * P:6 * P]).then_inc(w_act, 1)
                    with act.Fori(0, B) as b:
                        it = hp * B + b
                        for n in range(2):
                            wait(act, "proj", it, n + 1)
                            nc.scalar.copy(qv[:, :, 1 - n, :],
                                           ps_a[n][:].rearrange("p (c n) -> p c n", c=TILES)).then_inc(s["qvs"], 1)
                        for c in range(TILES):
                            wait(act, "proj", it, c + 3)
                            nc.scalar.copy(tok[:, c, :], ps_a[c % 2][:]).then_inc(s["toks"], 1)
                        for h in range(2):
                            wait(act, "kadd", it, h + 1)
                            nc.scalar.copy(keys[h][(1 - h) * HD:(2 - h) * HD, :],
                                           keys[h][h * HD:(h + 1) * HD, :]).then_inc(s["keyT"], 1)

                        def exp(u):
                            h, c = divmod(u, TILES)
                            k = 2 * c + h
                            wait(act, "shifts", it, u + 1)
                            nc.scalar.activation(prob[u % 2][:, 0:(c + 1) * P], ps_s[u % 2][:, 0:(c + 1) * P],
                                                 ACT.Exp, bias=shift[:, k:k + 1], scale=scale[:, k:k + 1],
                                                 accum_out=row_sum[:, k:k + 1]).then_inc(s["exps"], 1)

                        def copy_turned(u):
                            c = u % TILES
                            wait(act, "turns", it, u + 1)
                            if u >= 2:
                                wait(act, "pvs", it, u - 1)
                            nc.scalar.copy(probT[u % 2][:, 0:(c + 1) * P],
                                           ps_a[u % 2][:, 0:(c + 1) * P]).then_inc(s["probTs"], 1)

                        exp(0)
                        for u in range(1, 2 * TILES):
                            exp(u)
                            copy_turned(u - 1)
                        copy_turned(2 * TILES - 1)
                        wait(act, "headT", it, 1)
                        nc.scalar.copy(headsT[:], ps_y[0][:]).then_inc(s["headTc"], 1)

            @block.vector
            def _(dve):
                nc.vector.tensor_copy(state[:, 0, :], mem["state0"][:]).then_inc(s["statec"], 1)
                begin(dve, "kmul masked zkm incs n2 n8 scales queries negs shifts inv headn xadd")
                with dve.Fori(0, PAIRS) as hp, dve.Fori(0, B) as b:
                    it = hp * B + b

                    def mask(half):
                        for h in range(2):
                            wait(dve, "lins", it, 2 * half + h + 1)
                            nc.vector.tensor_tensor(
                                lin[h][:, 2 * half:2 * half + 2, :, :].rearrange("p c a n -> p c (a n)"),
                                ps_s[h][:].rearrange("p (c n) -> p c n", c=2),
                                mem["lin_mask"][:].unsqueeze(1).broadcast_to([P, 2, 2 * P]),
                                ALU.mult).then_inc(s["masked"], 1)

                    for n, (dst, table) in enumerate(((kcos, mem["cos2"]), (ksin, mem["sin2"]))):
                        wait(dve, "proj", it, 7 + n)
                        nc.vector.tensor_tensor(dst[:], ps_a[n][:], table[:], ALU.mult).then_inc(s["kmul"], 1)
                    mask(0)
                    wait(dve, "states", it, 1)
                    for c in range(TILES - 1):
                        if c:
                            wait(dve, "statec", it, c)
                        nc.vector.tensor_tensor(state[:, c + 1, :], ps_d[:, c * P:(c + 1) * P],
                                                mem["state0"][:] if c == 0 else state[:, c, :],
                                                ALU.add).then_inc(s["statec"], 1)
                    mask(1)
                    wait(dve, "zs", it, 1)
                    for h in range(2):
                        nc.vector.tensor_tensor(
                            zk[:, :, h, :], (ps_z, ps_y[1])[h][:, 0:TILES * HD].rearrange("p (c d) -> p c d", c=TILES),
                            tok[:, :, h * P:h * P + HD], ALU.mult).then_inc(s["zkm"], 1)
                    wait(dve, "zkm", it, 2)
                    nc.vector.reduce_sum(inc[:], zk[:].rearrange("p c h d -> p (c h) d"),
                                         AX.X).then_inc(s["incs"], 1)
                    wait(dve, "ys", it, 1)
                    nc.vector.tensor_tensor(query[0][:], ps_y[0][:], mem["cos_sin"][:],
                                            ALU.mult).then_inc(s["queries"], 1)
                    wait(dve, "cum", it, 1)
                    nc.vector.tensor_scalar(norm2[:], ps_d[:, 3 * P:3 * P + 2 * TILES], float(HD * HD), 0.0,
                                            ALU.add, ALU.max).then_inc(s["n2"], 1)
                    wait(dve, "ys", it, 2)
                    nc.vector.tensor_tensor(query[1][:], ps_y[1][:], mem["cos_sin"][:],
                                            ALU.mult).then_inc(s["queries"], 1)
                    wait(dve, "pows", it, 1)
                    nc.vector.tensor_scalar(norm8[:], norm[:], EPS, float(HD) ** 0.5,
                                            ALU.add, ALU.mult).then_inc(s["n8"], 1)
                    wait(dve, "n8", it, 1)
                    nc.vector.reciprocal(scale[:], norm8[:]).then_inc(s["scales"], 1)
                    wait(dve, "scales", it, 1)
                    for u in range(2 * TILES):
                        h, c = divmod(u, TILES)
                        k = 2 * c + h
                        wait(dve, "scores", it, u + 1)
                        nc.vector.tensor_reduce(neg_max[:, k:k + 1], ps_s[u % 2][:, 0:(c + 1) * P], AX.X, ALU.max,
                                                negate=True).then_inc(s["negs"], 1)
                        wait(dve, "negs", it, u + 1)
                        nc.vector.tensor_scalar(shift[:, k:k + 1], neg_max[:, k:k + 1], scale[:, k:k + 1], None,
                                                ALU.mult).then_inc(s["shifts"], 1)
                    wait(dve, "exps", it, 2 * TILES)
                    nc.vector.reciprocal(inv_sum[:], row_sum[:]).then_inc(s["inv"], 1)
                    wait(dve, "pvs", it, 2 * TILES)
                    wait(dve, "inv", it, 1)
                    nc.vector.tensor_tensor(heads[:].rearrange("p c (h d) -> p (c h) d", h=2),
                                            ps_z[:].rearrange("p (k d) -> p k d", d=HD),
                                            inv_sum[:].unsqueeze(2).broadcast_to([P, 2 * TILES, HD]),
                                            ALU.mult).then_inc(s["headn"], 1)
                    wait(dve, "outs", it, 1)
                    x4 = mem["x"][:, bass.ds(b * SEQ, SEQ)]
                    nc.vector.tensor_tensor(x4, ps_y[1][:], x4, ALU.add).then_inc(s["xadd"], 1)

def transformer_block(nc, mem, ins, B):
    L, H, D, FEAT, FT = 6, 16, 8, 16, 4
    V = D + 1
    EPS = 1e-6 * FEAT
    HALF = H // 2 * V
    SPAN, SPANS = P // 2, 2 * TILES
    DIAGONAL = HALF + 2 * V
    ROOT = float(D) ** -0.25
    UNROLLED = 2
    LEAD = "turn project values mapq mapk keys sums".split()
    FIRST = "turn S00 project S01 values W00 W01 S10 S11 mapq W10 mapk W11 keys sums".split()
    SLOT = ("S00 turn S01 nums W00 project W01 S10 att values S11 Wo mapq W10 mapk W11 h1 keys W1 sums "
            "W2").split()
    LAST = "S00 nums S01 W00 att W01 Wo S10 S11 W10 W11 h1 W1 W2".split()
    EDGE = "turn nums project att values Wo mapq mapk keys h1 sums W1 W2".split()
    FILLS = dict(turn="w0", project="w1 w0", values="w1", mapq="w0 w1", mapk="s0 s1", keys="w0 w1", sums="w0 s3",
                 S00="s0 s1", S01="s2 s3", S10="s0 s1", S11="s2 s3", W00="", W01="", W10="n0", W11="n1",
                 nums="w0 w1", att="w0", Wo="w1", h1="s2", W1="s0 s1 s2 s3", W2="w1")
    BANKS = ["w0", "w1", "s0", "s1", "s2", "s3", "n0", "n1"]

    def fills(steps, bank):
        return sum(FILLS[step].split().count(bank) for step in steps)

    class Slot:

        def __init__(self, steps, group, shift, before, parity):
            self.steps = steps
            self.group = group
            self.shift = shift
            self.before = before
            self.parity = parity

        def of(self, phase):
            return self.group + {"in": self.shift, "mix": 0, "out": -1}[phase]

        def fill(self, bank, step):
            layers, slots, patterns = self.before
            n = sum(fills(p, bank) for p in patterns) + fills(self.steps[:self.steps.index(step)], bank)
            layer = sum(fills(p, bank) for p in (FIRST, LAST, EDGE)) + (B - 2) * fills(SLOT, bank)
            return layers * layer + (slots * fills(SLOT, bank) + n)

    with ExitStack() as ctx:
        def sb(name, shape, dt=F32):
            return ctx.enter_context(nc.sbuf_tensor("t_" + name, shape, dt))

        def sem(name):
            return ctx.enter_context(nc.semaphore("t_" + name))

        w_in = sb("w_in", [P, 3, P])
        omega = sb("omega", [P, 2 * P])
        cols_in = sb("cols_in", [P, 2])
        bv = sb("bv", [P, P])
        w_o = sb("w_o", [P, P])
        w_1 = sb("w_1", [P, FT * P])
        w_2 = sb("w_2", [P, FT, P])
        cols = sb("cols", [P, 2 + FT])
        cols_v = sb("cols_v", [P, 2 + FT])
        rows = sb("rows", [P, 6, P])
        be1_bf2 = sb("be1_bf2", [P, P])
        next_sq, next_1 = sb("next_sq", [P, 4 * P]), sb("next_1", [P, FT * P])
        next_2, next_omega = sb("next_2", [P, FT * P]), sb("next_omega", [P // 2, 2 * P])
        next_cols, next_rows = sb("next_cols", [P, 4 + FT]), sb("next_rows", [P, 7 * P])
        o_now = sb("o_now", [P, TILES, P])
        oT = sb("oT", [P, SEQ])
        proj = [[sb(f"{n}{t}", [P, SEQ]) for t in range(2)] for n in ("qq", "kk")]
        phi_q = [[sb(f"phi_q{t}_{i}", [P, SEQ]) for t in range(2)] for i in range(2)]
        phi_k = [sb(f"phi_k{t}", [P, SEQ]) for t in range(2)]
        kz = [sb(f"kz{t}", [P, SPANS, 2, SPAN]) for t in range(2)]
        qz = [sb(f"qz{t}", [P, SPANS, 4, SPAN]) for t in range(2)]
        k_tok = sb("k_tok", [P, 2, TILES, P])
        v_tok = sb("v_tok", [P, TILES, 2, H, V])
        v_pad = sb("v_pad", [P, SPANS, H // 2 * DIAGONAL])
        kv = sb("kv", [P, 2, SPANS - 1, HALF])
        mixed = [[sb(f"mixed{i}_{n}", [P, 2, 4, SPAN]) for n in range(4)] for i in range(2)]
        num = [sb(f"num{t}", [HALF, SEQ]) for t in range(2)]
        o_bias = sb("o_bias", [P, TILES, P])
        den = sb("den", [P, 2, TILES, 8])
        inv = sb("inv", [P, 2, TILES, 8])
        att = sb("att", [P, TILES, P])
        attT = sb("attT", [P, SEQ])
        res = sb("res", [P, TILES, P])
        m = {"stats": sb("stats", [P, TILES, 6]), "mean_var": sb("mean_var", [P, TILES, 2]),
             "var_eps": sb("var_eps", [P, TILES]), "rstd": sb("rstd", [P, TILES]), "xn": sb("xn", [P, TILES, P])}
        h1T = oT
        scaled = sb("scaled", [P, TILES, P])
        h1b = sb("h1b", [P, TILES, P])
        hid = [sb(f"hid{f}", [P, SEQ]) for f in range(FT)]
        ps = {k: ctx.enter_context(nc.psum_tensor("t_" + k, [P, 512], F32)) for k in BANKS}

        filled = {k: sem("filled_" + k) for k in BANKS}
        emptied = {k: sem("emptied_" + k) for k in BANKS}
        EVENTS = dict(o_now=1, o_bias=1, qz=2, kz=4, kv_sum=3, v_tok=1, v_pad=1, den=2, inv=2,
                      stats=8, mv=8, eps=2, rstd=2, xn=8, scaled=2, h1b=1, o_new=1)
        PHASE = {n: "in" if n in ("o_now", "qz", "kz", "kv_sum", "v_tok", "v_pad") else "out" for n in EVENTS}
        s = {n: sem(n) for n in EVENTS}
        w_loaded = sem("w_loaded")
        made_in = {n: sem("made_in_" + n) for n in ("act", "dve")}
        made_out = {n: sem("made_out_" + n) for n in ("act", "dve", "pool")}
        ones_set = sem("ones_set")
        LOADS = 6

        with nc.Block() as block:
            @block.sync
            def _(sp):
                with sp.Fori(0, L + 1) as l:
                    for made in list(made_in.values()) + list(made_out.values()):
                        sp.wait_ge(made, l + 1)
                    for dst, name in ((next_sq, "t_sq"), (next_1, "t_w1"), (next_2, "t_w2"),
                                      (next_omega, "t_omega"), (next_cols, "t_cols")):
                        sp.dma_start(dst[:], ins[name][bass.ds(l, 1), :, :].squeeze(0)).then_inc(w_loaded, 16)
                    sp.dma_start(next_rows[:], ins["t_rows"][bass.ds(l, 1), :].squeeze(0)
                                 .partition_broadcast(P)).then_inc(w_loaded, 16)
                sp.wait_ge(w_loaded, (L + 1) * 16 * LOADS)

            def pipeline(e, names, weights_in, weights_out, body):
                for n in names.split():
                    e.sem_inc(s[n], B + 1 if n == "o_new" else 1)

                def run(slot, sequence):
                    for step in slot.steps:
                        body(step, slot, sequence)

                weights_in(0, None)
                run(Slot(LEAD, 0, 0, (0, 0, []), 0), {"in": 0})
                with e.Fori(0, L) as l:
                    g = l * B
                    run(Slot(FIRST, g, 1, (l, 0, [LEAD]), 0), {"in": 1})
                    slot = Slot(SLOT, None, None, (l, 0, [LEAD, FIRST]), None)
                    weights_out(l, slot)
                    with e.Fori(0, (B - 2) // UNROLLED) as tn:
                        for u in range(UNROLLED):
                            z = tn * UNROLLED + (1 + u)
                            run(Slot(SLOT, g + z, 1, (l, tn * UNROLLED + u, [LEAD, FIRST]), (1 + u) % 2),
                                {"in": z + 1, "out": z - 1})
                    slot = Slot(LAST, g + (B - 1), None, (l, B - 2, [LEAD, FIRST]), 1)
                    weights_in(l + 1, slot)
                    run(slot, {"out": B - 2})
                    run(Slot(EDGE, g + B, 0, (l, B - 2, [LEAD, FIRST, LAST]), 0), {"in": 0, "out": B - 1})

            def wait_staged(e, l, slot):
                e.wait_ge(w_loaded, (l + 1) * (16 * LOADS))
                if slot is not None:
                    for bank in ("w0", "w1"):
                        e.wait_ge(filled[bank], slot.fill(bank, slot.steps[0]) + 1)
                e.nop(nofuse=True)

            def wait(e, name, slot, n):
                e.wait_ge(s[name], slot.of(PHASE[name]) * EVENTS[name] + (n + 1 + (B if name == "o_new" else 0)))

            def wait_filled(e, bank, slot, step, n=0):
                e.wait_ge(filled[bank], slot.fill(bank, step) + (n + 2))

            def wait_emptied(e, bank, slot, step, n=0):
                e.wait_ge(emptied[bank], slot.fill(bank, step) + (n + 2))

            def wait_free(e, bank, slot, step, n=0):
                e.wait_ge(emptied[bank], slot.fill(bank, step) + (n + 1))

            def chunk(c):
                return slice(c * P, (c + 1) * P)

            def tokens_of(z):
                return mem["o"][:, bass.ds(z * SEQ, SEQ)] if not isinstance(z, int) \
                    else mem["o"][:, z * SEQ:(z + 1) * SEQ]

            @block.gpsimd
            def _(pool):
                pool.sem_inc(made_out["pool"], 1)

                def weights_in(l, slot):
                    pass

                def weights_out(l, slot):
                    wait_staged(pool, l, slot)
                    pool.wait_ge(s["o_new"], l * B + (B + 1))
                    pool.nop(nofuse=True)
                    nc.gpsimd.tensor_copy(rows[:].rearrange("p a n -> p (a n)"), next_rows[:, P:7 * P])
                    nc.gpsimd.tensor_tensor(be1_bf2[:], next_rows[:, 3 * P:4 * P], next_rows[:, 4 * P:5 * P],
                                            ALU.add).then_inc(made_out["pool"], 1)
                    pool.wait_ge(made_out["pool"], l + 2)
                    pool.nop(nofuse=True)

                def row(n):
                    return rows[:, n, :].unsqueeze(1).broadcast_to([P, TILES, P])

                def body(step, slot, sequence):
                    if step == "nums":
                        tokens = tokens_of(sequence["out"]).rearrange("p (c d) -> p c d", c=TILES)
                        nc.gpsimd.tensor_tensor(o_bias[:], tokens, row(0), ALU.add).then_inc(s["o_bias"], 1)
                    elif step == "sums":
                        wait_emptied(pool, "w0", slot, "sums")
                        wait_emptied(pool, "s3", slot, "sums")
                        for c in range(1, TILES):
                            if c > 1:
                                wait(pool, "kv_sum", slot, c - 1)
                                pool.nop(nofuse=True)
                            own = kv[:, :, 2 * c:min(2 * c + 2, SPANS - 1), :]
                            n = own.shape[2]
                            nc.gpsimd.tensor_tensor(own, own, kv[:, :, 2 * c - 1:2 * c, :]
                                                    .broadcast_to([P, 2, n, HALF]), ALU.add).then_inc(s["kv_sum"], 1)
                    elif step in ("Wo", "W2"):
                        k = ("Wo", "W2").index(step)
                        wait(pool, "eps", slot, k + 1)
                        nc.gpsimd.tensor_tensor(m["rstd"][:], m["var_eps"][:],
                                                mem["minus_half"][:, 0:TILES], ALU.pow).then_inc(s["rstd"], 1)
                        wait(pool, "xn", slot, TILES * (k + 1))
                        pool.nop(nofuse=True)
                        g, b, out, name = (
                            (row(1), be1_bf2[:].unsqueeze(1).broadcast_to([P, TILES, P]), h1b[:], "h1b"),
                            (row(4), row(5), tokens_of(sequence["out"]).rearrange("p (c d) -> p c d", c=TILES),
                             "o_new"))[k]
                        nc.gpsimd.tensor_tensor(scaled[:], m["xn"][:], g, ALU.mult).then_inc(s["scaled"], 1)
                        wait(pool, "scaled", slot, k + 1)
                        pool.nop(nofuse=True)
                        nc.gpsimd.tensor_tensor(out, scaled[:], b, ALU.add).then_inc(s[name], 1)

                pipeline(pool, "o_bias kv_sum rstd scaled h1b o_new", weights_in, weights_out, body)

            @block.tensor
            def _(pe):
                for k in BANKS:
                    pe.sem_inc(filled[k], 1)

                def weights_in(l, slot):
                    if slot is None:
                        for made in made_in.values():
                            pe.wait_ge(made, 2)
                        pe.nop(nofuse=True)

                def weights_out(l, slot):
                    for made in (made_out["act"], made_out["dve"]):
                        pe.wait_ge(made, l + 2)
                    pe.nop(nofuse=True)

                def scores(slot, i, t):
                    if i == 0 and t == 0:
                        pe.wait_ge(s["kz"], slot.of("mix") * 4 + 5)
                        pe.wait_ge(s["qz"], slot.of("mix") * 2 + 3)
                    for n in range(2):
                        bank = f"s{2 * t + n}"
                        wait_free(pe, bank, slot, f"S{i}{t}")
                        for k in range(2):
                            u = 4 * i + 2 * n + k
                            mm = nc.tensor.matmul(ps[bank][:, k * 4 * SPAN:(k + 1) * 4 * SPAN],
                                                  kz[t][:, u, :, :].rearrange("p h n -> p (h n)"),
                                                  qz[t][:, u, :, :].rearrange("p r n -> p (r n)"),
                                                  start=True, stop=True)
                        mm.then_inc(filled[bank], 1)

                def weigh(slot, i, t):
                    bank = f"n{t}"
                    if i == 0:
                        if t == 0:
                            pe.wait_ge(s["v_pad"], slot.of("mix") + 2)
                            pe.wait_ge(s["kv_sum"], slot.of("mix") * 3 + 4)
                        pe.wait_ge(emptied[bank], slot.of("mix") + 1)
                    for n in range(2):
                        wait_emptied(pe, f"s{2 * t + n}", slot, f"S{i}{t}")
                    for uu in range(4):
                        u = 4 * i + uu
                        o = ps[bank][0:HALF, u * SPAN:(u + 1) * SPAN]
                        if u:
                            nc.tensor.matmul(o, kv[:, t, u - 1, :], phi_q[slot.parity][t][:, u * SPAN:(u + 1) * SPAN],
                                             start=True, stop=False)
                        for r in range(4):
                            at = t * 4 * DIAGONAL + r * HALF
                            mm = nc.tensor.matmul(o, v_pad[:, u, at:at + HALF], mixed[i][2 * t + uu // 2][:, uu % 2, r, :],
                                                  start=u == 0 and r == 0, stop=r == 3)
                    if i == 1:
                        mm.then_inc(filled[bank], 1)

                def body(step, slot, sequence):
                    def free(bank, n=0):
                        wait_free(pe, bank, slot, step, n)

                    def ready(bank, of, n=0):
                        wait_emptied(pe, bank, slot, of, n)

                    if step == "turn":
                        wait(pe, "o_now", slot, 1)
                        free("w0")
                        for c in range(TILES):
                            t = nc.tensor.transpose(ps["w0"][:, chunk(c)], o_now[:, c, :], mem["ident"][:])
                        t.then_inc(filled["w0"], 1)
                    elif step == "project":
                        if slot.steps is EDGE:
                            for made in made_in.values():
                                pe.wait_ge(made, (slot.before[0] + 1) + 2)
                            pe.nop(nofuse=True)
                        ready("w0", "turn")
                        for bank, n in (("w1", 0), ("w0", 1)):
                            free(bank)
                            nc.tensor.matmul(ps[bank][:], w_in[:, n, :], oT[:], start=True,
                                             stop=True).then_inc(filled[bank], 1)
                    elif step == "values":
                        free("w1")
                        for c in range(TILES):
                            t = nc.tensor.matmul(ps["w1"][:, chunk(c)], oT[:, chunk(c)], w_in[:, 2, :],
                                                 start=True, stop=True)
                        t.then_inc(filled["w1"], 1)
                    elif step in ("mapq", "mapk"):
                        j = ("mapq", "mapk").index(step)
                        ready(("w1", "w0")[j], "project")
                        for t_, bank in enumerate((("w0", "w1"), ("s0", "s1"))[j]):
                            free(bank)
                            nc.tensor.matmul(ps[bank][:], omega[:, chunk(t_)], proj[j][t_][:], start=True,
                                             stop=True).then_inc(filled[bank], 1)
                    elif step == "keys":
                        for t_, bank in enumerate(("w0", "w1")):
                            ready(f"s{t_}", "mapk")
                            free(bank)
                            for c in range(TILES):
                                t = nc.tensor.transpose(ps[bank][:, chunk(c)], phi_k[t_][:, chunk(c)],
                                                        mem["ident"][:])
                            t.then_inc(filled[bank], 1)
                    elif step == "sums":
                        wait(pe, "v_tok", slot, 1)
                        for t_, bank in enumerate(("w0", "s3")):
                            ready(("w0", "w1")[t_], "keys")
                            free(bank)
                            for c in range(TILES):
                                n = 2 if c < TILES - 1 else 1
                                t = nc.tensor.matmul(
                                    ps[bank][:, 2 * c * HALF:(2 * c + n) * HALF].rearrange("p (s n) -> p s n", s=n),
                                    k_tok[:, t_, c, :],
                                    v_tok[:, c, 0:n, 8 * t_:8 * t_ + 8, :].rearrange("p s h d -> p s (h d)"),
                                    start=True, stop=True)
                            t.then_inc(filled[bank], 1)
                    elif step[0] == "S":
                        scores(slot, int(step[1]), int(step[2]))
                    elif step in ("W00", "W01", "W10", "W11"):
                        weigh(slot, int(step[1]), int(step[2]))
                    elif step == "nums":
                        for t_, bank in enumerate(("w0", "w1")):
                            pe.wait_ge(emptied[f"n{t_}"], slot.of("out") + 2)
                            free(bank)
                            for c in range(TILES):
                                t = nc.tensor.transpose(ps[bank][:, c * HALF:(c + 1) * HALF], num[t_][:, chunk(c)],
                                                        mem["ident"][0:HALF, 0:HALF])
                            t.then_inc(filled[bank], 1)
                    elif step == "att":
                        for bank in ("w0", "w1"):
                            ready(bank, "nums")
                        free("w0")
                        for c in range(TILES):
                            t = nc.tensor.transpose(ps["w0"][:, chunk(c)], att[:, c, :], mem["ident"][:])
                        t.then_inc(filled["w0"], 1)
                    elif step == "Wo":
                        ready("w0", "att")
                        free("w1")
                        for c in range(TILES):
                            t = nc.tensor.matmul(ps["w1"][:, chunk(c)], attT[:, chunk(c)], w_o[:],
                                                 start=True, stop=True)
                        t.then_inc(filled["w1"], 1)
                    elif step == "h1":
                        wait(pe, "xn", slot, TILES)
                        free("s2")
                        for c in range(TILES):
                            t = nc.tensor.transpose(ps["s2"][:, chunk(c)], m["xn"][:, c, :], mem["ident"][:])
                        t.then_inc(filled["s2"], 1)
                    elif step == "W1":
                        ready("s2", "h1")
                        for f in range(FT):
                            free(f"s{f}")
                            nc.tensor.matmul(ps[f"s{f}"][:], w_1[:, chunk(f)], h1T[:], start=True,
                                             stop=True).then_inc(filled[f"s{f}"], 1)
                    elif step == "W2":
                        for f in range(FT):
                            ready(f"s{f}", "W1")
                        free("w1")
                        for c in range(TILES):
                            for f in range(FT):
                                t = nc.tensor.matmul(ps["w1"][:, chunk(c)], hid[f][:, chunk(c)], w_2[:, f, :],
                                                     start=f == 0, stop=f == FT - 1)
                        t.then_inc(filled["w1"], 1)

                pipeline(pe, "", weights_in, weights_out, body)

            @block.scalar
            def _(act):
                for k in BANKS:
                    act.sem_inc(emptied[k], 1)

                def weights_in(l, slot):
                    if slot is None:
                        act.wait_ge(ones_set, 11)
                        act.nop(nofuse=True)
                    wait_staged(act, l, slot)
                    nc.scalar.copy(w_in[:].rearrange("p a n -> p (a n)"), next_sq[:, 0:3 * P])
                    nc.scalar.copy(cols_in[:], next_cols[:, 0:2])
                    for sign in range(2):
                        def signed(ap):
                            return ap.rearrange("p (g s m) -> p g s m", s=2, m=8)[:, :, sign, :]

                        t = nc.scalar.mul(signed(omega[0:64, :]), signed(next_omega[:]), (ROOT, -ROOT)[sign])
                    t.then_inc(made_in["act"], 1)
                    act.wait_ge(made_in["act"], l + 2)
                    act.nop(nofuse=True)

                def weights_out(l, slot):
                    wait_staged(act, l, slot)
                    nc.scalar.copy(w_o[:], next_sq[:, 3 * P:4 * P])
                    nc.scalar.copy(cols[:], next_cols[:, 2:4 + FT]).then_inc(made_out["act"], 1)
                    act.wait_ge(made_out["act"], l + 2)
                    act.nop(nofuse=True)

                def body(step, slot, sequence):
                    def full(bank):
                        wait_filled(act, bank, slot, step)

                    if step == "turn":
                        act.wait_ge(s["o_new"], slot.of("in") + 2)
                        act.nop(nofuse=True)
                        nc.scalar.copy(o_now[:].rearrange("p c d -> p (c d)"),
                                       tokens_of(sequence["in"])).then_inc(s["o_now"], 1)
                        full("w0")
                        nc.scalar.copy(oT[:], ps["w0"][:]).then_inc(emptied["w0"], 1)
                    elif step == "project":
                        for j, bank in enumerate(("w1", "w0")):
                            full(bank)
                            for t_ in range(2):
                                half = slice(64 * t_, 64 * t_ + 64)
                                nc.scalar.activation(proj[j][t_][0:64, :], ps[bank][half, :], ACT.Identity,
                                                     bias=cols_in[half, j:j + 1])
                                t = nc.scalar.activation(proj[j][t_][64:P, :], ps[bank][half, :], ACT.Square,
                                                         bias=cols_in[half, j:j + 1])
                            t.then_inc(emptied[bank], 1)
                    elif step in ("mapq", "mapk"):
                        j = ("mapq", "mapk").index(step)
                        maps = (phi_q[1 - slot.parity if slot.shift else 0], phi_k)[j]
                        for t_, bank in enumerate((("w0", "w1"), ("s0", "s1"))[j]):
                            full(bank)
                            if j == 0:
                                for r in range(4):
                                    rs = slice(32 * r, 32 * r + 32)
                                    t = nc.scalar.activation(
                                        qz[t_][rs, :, r, :], ps[bank][rs, :].rearrange("p (u n) -> p u n", u=SPANS),
                                        ACT.Exp)
                                t.then_inc(s["qz"], 1)
                            nc.scalar.activation(maps[t_][:], ps[bank][:], ACT.Exp).then_inc(emptied[bank], 1)
                    elif step in ("W10", "W11"):
                        t_ = int(step[2])
                        full(f"n{t_}")
                        nc.scalar.copy(num[t_][:], ps[f"n{t_}"][0:HALF, :]).then_inc(emptied[f"n{t_}"], 1)
                    elif step == "att":
                        full("w0")
                        nc.scalar.copy(attT[:], ps["w0"][:]).then_inc(emptied["w0"], 1)
                    elif step == "h1":
                        full("s2")
                        nc.scalar.activation(h1T[:], ps["s2"][:], ACT.Identity, bias=cols[:, 1:2],
                                             scale=cols[:, 0:1]).then_inc(emptied["s2"], 1)
                    elif step == "W1":
                        for f in (0, 2):
                            full(f"s{f}")
                            nc.scalar.activation(hid[f][:], ps[f"s{f}"][:], ACT.Relu,
                                                 bias=cols[:, 2 + f:3 + f]).then_inc(emptied[f"s{f}"], 1)

                act.sem_inc(made_in["act"], 1)
                act.sem_inc(made_out["act"], 1)
                pipeline(act, "o_now qz", weights_in, weights_out, body)

            @block.vector
            def _(dve):
                flat = v_tok[:].rearrange("p c s h d -> p c s (h d)")
                nc.vector.memset(flat[:, :, 1, :], 1.0).then_inc(ones_set, 1)
                nc.vector.memset(flat[0:SPAN, :, 0, :], 1.0).then_inc(ones_set, 1)
                nc.vector.memset(flat[SPAN:P, :, 0, :], 0.0).then_inc(ones_set, 1)
                nc.vector.memset(v_pad[:].rearrange("p u n -> p (u n)"), 0.0).then_inc(ones_set, 1)
                nc.vector.tensor_copy(omega[64:P, :], mem["half_norm"][64:P, :]).then_inc(ones_set, 1)
                for t_ in range(2):
                    nc.vector.memset(qz[t_][:].rearrange("p u r n -> p (u r n)"), 0.0).then_inc(ones_set, 1)
                dve.wait_ge(ones_set, 7)
                own = [v_pad[SPAN * p:SPAN * (p + 1)].rearrange("p (c s) (k n) -> p c s k n", s=2, n=DIAGONAL)
                       [:, :, :, :, p * V:(p + 1) * V] for p in range(2)]
                for p in range(2):
                    for span in range(2):
                        nc.vector.memset(own[p][:, :, span, :, D:V], 1.0).then_inc(ones_set, 1)
                dve.wait_ge(ones_set, 11)

                def weights_in(l, slot):
                    wait_staged(dve, l, slot)
                    nc.vector.tensor_copy(bv[:], next_rows[:, 0:P]).then_inc(made_in["dve"], 1)
                    dve.wait_ge(made_in["dve"], l + 2)
                    dve.nop(nofuse=True)

                def weights_out(l, slot):
                    wait_staged(dve, l, slot)
                    nc.vector.tensor_copy(cols_v[:], next_cols[:, 2:4 + FT])
                    nc.vector.tensor_copy(w_1[:], next_1[:])
                    nc.vector.tensor_copy(w_2[:].rearrange("p a n -> p (a n)"),
                                          next_2[:]).then_inc(made_out["dve"], 1)
                    dve.wait_ge(made_out["dve"], l + 2)
                    dve.nop(nofuse=True)

                def norm(slot, k):
                    for c in range(TILES):
                        nc.vector.bn_stats(m["stats"][:, c, :], res[:, c, :]).then_inc(s["stats"], 1)
                    wait(dve, "stats", slot, TILES * (k + 1))
                    dve.nop(nofuse=True)
                    for c in range(TILES):
                        nc.vector.bn_aggr(m["mean_var"][:, c, :], m["stats"][:, c, :]).then_inc(s["mv"], 1)
                    wait(dve, "mv", slot, TILES * (k + 1))
                    nc.vector.tensor_scalar(m["var_eps"][:], m["mean_var"][:, :, 1], LN_EPS, None,
                                            ALU.add).then_inc(s["eps"], 1)
                    wait(dve, "rstd", slot, k + 1)
                    for c in range(TILES):
                        nc.vector.tensor_scalar(m["xn"][:, c, :], res[:, c, :], m["mean_var"][:, c, 0:1],
                                                m["rstd"][:, c:c + 1], ALU.subtract,
                                                ALU.mult).then_inc(s["xn"], 1)

                def body(step, slot, sequence):
                    def full(bank):
                        wait_filled(dve, bank, slot, step)

                    if step == "values":
                        wait(dve, "v_pad", slot, 0)
                        full("w1")
                        for span, size in ((1, P), (0, SPAN)):
                            t = nc.vector.tensor_tensor(
                                v_tok[0:size, :, span, :, 0:D],
                                ps["w1"][0:size, :].rearrange("p (c h d) -> p c h d", c=TILES, h=H),
                                bv[0:size, :].rearrange("p (h d) -> p h d", h=H).unsqueeze(1)
                                .broadcast_to([size, TILES, H, D]), ALU.add)
                            t.then_inc(*((s["v_tok"], 1) if span else (emptied["w1"], 1)))
                    elif step == "mapk":
                        for t_ in range(2):
                            wait_emptied(dve, f"s{t_}", slot, "mapk")
                            for p in range(2):
                                nc.vector.tensor_scalar(kz[t_][:, :, p, :],
                                                        phi_k[t_][:].rearrange("p (u n) -> p u n", u=SPANS),
                                                        mem["strip_head"][:, p:p + 1], None,
                                                        ALU.mult).then_inc(s["kz"], 1)
                    elif step == "keys":
                        for t_, bank in enumerate(("w0", "w1")):
                            full(bank)
                            nc.vector.tensor_copy(k_tok[:, t_, :, :].rearrange("p c n -> p (c n)"),
                                                  ps[bank][:]).then_inc(emptied[bank], 1)
                    elif step == "sums":
                        for t_, bank in enumerate(("w0", "s3")):
                            full(bank)
                            nc.vector.tensor_tensor(
                                kv[:, t_, :, :],
                                ps[bank][:, 0:(SPANS - 1) * HALF].rearrange("p (c n) -> p c n", c=SPANS - 1),
                                mem["own_head"][:].unsqueeze(1).broadcast_to([P, SPANS - 1, HALF]),
                                ALU.mult).then_inc(emptied[bank], 1)
                        dve.wait_ge(filled["n1"], slot.of("in") + 1)
                        wait(dve, "v_tok", slot, 1)
                        for p in range(2):
                            for span in range(2):
                                rows_ = slice(SPAN * span, SPAN * (span + 1))
                                t = nc.vector.tensor_copy(
                                    own[p][:, :, span, :, 0:D],
                                    v_tok[rows_, :, 1, :, 0:D].rearrange("p c (k q) d -> p c k q d", q=2)
                                    [:, :, :, p, :])
                        t.then_inc(s["v_pad"], 1)
                    elif step[0] == "S":
                        i, t_ = int(step[1]), int(step[2])
                        for n in (2 * t_, 2 * t_ + 1):
                            full(f"s{n}")
                            nc.vector.tensor_tensor(mixed[i][n][:].rearrange("p u r n -> p (u r) n"),
                                                    ps[f"s{n}"][:].rearrange("p (k n) -> p k n", k=8),
                                                    mem["upto"][:].unsqueeze(1).broadcast_to([P, 8, SPAN]),
                                                    ALU.mult).then_inc(emptied[f"s{n}"], 1)
                    elif step == "nums":
                        for t_, bank in enumerate(("w0", "w1")):
                            full(bank)
                            nums = ps[bank][:, 0:TILES * HALF].rearrange("p (c k d) -> p c k d", c=TILES, d=V)
                            nc.vector.tensor_scalar(den[:, t_, :, :], nums[:, :, :, D], EPS, None,
                                                    ALU.add).then_inc(s["den"], 1)
                            wait(dve, "den", slot, t_ + 1)
                            nc.vector.reciprocal(inv[:, t_, :, :], den[:, t_, :, :]).then_inc(s["inv"], 1)
                            wait(dve, "inv", slot, t_ + 1)
                            nc.vector.tensor_tensor(
                                att[:].rearrange("p c (t k d) -> p c t k d", t=2, k=8)[:, :, t_, :, :],
                                nums[:, :, :, 0:D], inv[:, t_, :, :].unsqueeze(3).broadcast_to([P, TILES, 8, D]),
                                ALU.mult).then_inc(emptied[bank], 1)
                    elif step == "Wo":
                        wait(dve, "xn", slot, 0)
                        wait(dve, "o_bias", slot, 1)
                        full("w1")
                        nc.vector.tensor_tensor(res[:].rearrange("p c d -> p (c d)"), ps["w1"][:],
                                                o_bias[:].rearrange("p c d -> p (c d)"),
                                                ALU.add).then_inc(emptied["w1"], 1)
                        wait_emptied(dve, "w1", slot, "Wo")
                        norm(slot, 0)
                    elif step == "W1":
                        for f in (1, 3):
                            full(f"s{f}")
                            nc.vector.tensor_scalar(hid[f][:], ps[f"s{f}"][:], cols_v[:, 2 + f:3 + f], 0.0,
                                                    ALU.add, ALU.max).then_inc(emptied[f"s{f}"], 1)
                    elif step == "W2":
                        wait(dve, "xn", slot, TILES)
                        wait(dve, "h1b", slot, 1)
                        full("w1")
                        nc.vector.tensor_tensor(res[:].rearrange("p c d -> p (c d)"), ps["w1"][:],
                                                h1b[:].rearrange("p c d -> p (c d)"),
                                                ALU.add).then_inc(emptied["w1"], 1)
                        wait_emptied(dve, "w1", slot, "W2")
                        norm(slot, 1)

                dve.sem_inc(made_in["dve"], 1)
                dve.sem_inc(made_out["dve"], 1)
                pipeline(dve, "stats mv eps xn den inv kz v_tok v_pad", weights_in, weights_out, body)

        added = sem("added")
        with nc.Block() as block:
            @block.vector
            def _(dve):
                with dve.Fori(0, B) as b:
                    x4 = mem["x"][:, bass.ds(b * SEQ, SEQ)]
                    nc.vector.tensor_tensor(x4, x4, mem["o"][:, bass.ds(b * SEQ, SEQ)], ALU.add).then_inc(added, 1)


def moe_block(nc, mem, groups, tag):
    E, K, ROUTE_SCALE = mem["experts"], 8, 2.826
    x_all = mem["x"]
    w_gate, w_up, w_down = mem["moe_gate"], mem["moe_up"], mem["moe_down"]
    with ExitStack() as ctx:
        def sb(name, shape, dt=F32):
            return ctx.enter_context(nc.sbuf_tensor(tag + name, shape, dt))

        def bank(name):
            return ctx.enter_context(nc.psum_tensor(tag + name, [P, 512], F32))

        def sem(name):
            return ctx.enter_context(nc.semaphore(tag + name))

        stats = sb("stats", [P, TILES, 6])
        mean_var = sb("mean_var", [P, TILES, 2])
        var_eps = sb("var_eps", [P, TILES])
        rstd = sb("rstd", [P, TILES])
        xn = sb("xn", [P, TILES, P])
        xT = sb("xT", [P, SEQ])
        score = sb("score", [P, TILES, E])
        select = sb("select", [P, TILES, E])
        top8 = sb("top8", [P, TILES, 8])
        rest = sb("rest", [P, TILES, E])
        chosen = sb("chosen", [P, TILES, E])
        picked = sb("picked", [P, TILES, E])
        total = sb("total", [P, TILES])
        inv_total = sb("inv_total", [P, TILES])
        combine = sb("combine", [P, TILES, E])
        silu = [sb(f"silu{i}", [P, SEQ]) for i in range(2)]
        hidden = [sb(f"hidden{i}", [P, SEQ]) for i in range(2)]
        acc = sb("acc", [P, TILES, P])
        ps_g = [bank(f"ps_g{i}") for i in range(2)]
        ps_u = [bank(f"ps_u{i}") for i in range(2)]
        ps_y = [bank(f"ps_y{i}") for i in range(2)]
        ps_t = bank("ps_t")
        ps_gate = bank("ps_gate")

        stats_done, mv_done, eps_done = sem("stats_done"), sem("mv_done"), sem("eps_done")
        rstd_done, xn_done, turned, xT_done = sem("rstd_done"), sem("xn_done"), sem("turned"), sem("xT_done")
        gates_done, score_done, route_step = sem("gates_done"), sem("score_done"), sem("route_step")
        g_done, u_done, silu_done, hid_done = sem("g_done"), sem("u_done"), sem("silu_done"), sem("hid_done")
        y_done, acc_done, group_done = sem("y_done"), sem("acc_done"), sem("group_done")
        N = E + 1
        ROUTE = 3 + 3 * TILES
        with nc.Block() as block:

            @block.tensor
            def _(pe):
                with pe.Fori(0, groups) as g:
                    pe.wait_ge(xn_done, g * TILES + TILES)
                    for c in range(TILES):
                        t = nc.tensor.transpose(ps_t[:, c * P:(c + 1) * P], xn[:, c, :], mem["ident"][:])
                    t.then_inc(turned, 1)
                    pe.wait_ge(xT_done, g + 1)
                    for c in range(TILES):
                        t = nc.tensor.matmul(ps_gate[:, c * E:(c + 1) * E], xT[:, c * P:(c + 1) * P],
                                             mem["router"][:], start=True, stop=True)
                    t.then_inc(gates_done, 1)

                    def down(e):
                        pe.wait_ge(hid_done, g * N + e + 1)
                        if e >= 2:
                            pe.wait_ge(acc_done, g * N + e - 1)
                        else:
                            pe.wait_ge(group_done, g + 1)
                        for c in range(TILES):
                            t = nc.tensor.matmul(ps_y[e % 2][:, c * P:(c + 1) * P],
                                                 hidden[e % 2][:, c * P:(c + 1) * P],
                                                 w_down[:, e * P:(e + 1) * P], start=True, stop=True)
                        t.then_inc(y_done, 1)

                    for e in range(N):
                        if e >= 2:
                            pe.wait_ge(silu_done, g * N + e - 1)
                        nc.tensor.matmul(ps_g[e % 2][:], w_gate[:, e * P:(e + 1) * P], xT[:],
                                         start=True, stop=True).then_inc(g_done, 1)
                        if e >= 2:
                            pe.wait_ge(hid_done, g * N + e - 1)
                        nc.tensor.matmul(ps_u[e % 2][:], w_up[:, e * P:(e + 1) * P], xT[:],
                                         start=True, stop=True).then_inc(u_done, 1)
                        if e >= 1:
                            down(e - 1)
                    down(N - 1)

            @block.scalar
            def _(act):
                with act.Fori(0, groups) as g:
                    act.wait_ge(turned, g + 1)
                    nc.scalar.copy(xT[:], ps_t[:]).then_inc(xT_done, 1)
                    act.wait_ge(gates_done, g + 1)
                    act.wait_ge(route_step, g * ROUTE + 1)
                    nc.scalar.activation(score[:].rearrange("p c e -> p (c e)"), ps_gate[:, 0:TILES * E],
                                         ACT.Sigmoid).then_inc(score_done, 1)
                    for e in range(N):
                        act.wait_ge(g_done, g * N + e + 1)
                        if e >= 2:
                            act.wait_ge(hid_done, g * N + e - 1)
                        nc.scalar.activation(silu[e % 2][:], ps_g[e % 2][:], ACT.Silu).then_inc(silu_done, 1)

            @block.gpsimd
            def _(pool):
                with pool.Fori(0, groups) as g:
                    pool.wait_ge(eps_done, g + 1)
                    nc.gpsimd.tensor_tensor(rstd[:], var_eps[:], mem["minus_half"][:, 0:TILES],
                                            ALU.pow).then_inc(rstd_done, 1)

            @block.vector
            def _(dve):
                dve.sem_inc(group_done, 1)
                dve.sem_inc(route_step, 1)
                with dve.Fori(0, groups) as g:
                    def x_tile(c, n=1):
                        return x_all[:, bass.ds(g * SEQ + c * P, n * P)]

                    for c in range(TILES):
                        nc.vector.bn_stats(stats[:, c, :], x_tile(c)).then_inc(stats_done, 1)
                    dve.wait_ge(stats_done, (g + 1) * TILES)
                    dve.nop(nofuse=True)
                    for c in range(TILES):
                        nc.vector.bn_aggr(mean_var[:, c, :], stats[:, c, :]).then_inc(mv_done, 1)
                    dve.wait_ge(mv_done, (g + 1) * TILES)
                    nc.vector.tensor_scalar(var_eps[:], mean_var[:, :, 1], LN_EPS, None,
                                            ALU.add).then_inc(eps_done, 1)
                    dve.wait_ge(rstd_done, g + 1)
                    for c in range(TILES):
                        nc.vector.tensor_scalar(xn[:, c, :], x_tile(c), mean_var[:, c, 0:1], rstd[:, c:c + 1],
                                                ALU.subtract, ALU.mult).then_inc(xn_done, 1)

                    dve.wait_ge(score_done, g + 1)
                    nc.vector.tensor_tensor(select[:], score[:],
                                            mem["expert_bias"][:].unsqueeze(1).broadcast_to([P, TILES, E]),
                                            ALU.add).then_inc(route_step, 1)
                    dve.wait_ge(route_step, g * ROUTE + 2)
                    dve.nop(nofuse=True)
                    for c in range(TILES):
                        nc.vector.max(top8[:, c, :], select[:, c, :]).then_inc(route_step, 1)
                    dve.wait_ge(route_step, g * ROUTE + 2 + TILES)
                    dve.nop(nofuse=True)
                    for c in range(TILES):
                        nc.vector.match_replace(rest[:, c, :], top8[:, c, :], select[:, c, :],
                                                -3.0e38).then_inc(route_step, 1)
                    dve.wait_ge(route_step, g * ROUTE + 2 + 2 * TILES)
                    nc.vector.tensor_tensor(chosen[:], rest[:], select[:], ALU.not_equal).then_inc(route_step, 1)
                    dve.wait_ge(route_step, g * ROUTE + 3 + 2 * TILES)
                    nc.vector.tensor_tensor(picked[:], chosen[:], score[:], ALU.mult).then_inc(route_step, 1)
                    dve.wait_ge(route_step, g * ROUTE + 4 + 2 * TILES)
                    nc.vector.reduce_sum(total[:], picked[:], AX.X).then_inc(route_step, 1)
                    dve.wait_ge(route_step, g * ROUTE + 5 + 2 * TILES)
                    nc.vector.reciprocal(inv_total[:], total[:]).then_inc(route_step, 1)
                    dve.wait_ge(route_step, g * ROUTE + 6 + 2 * TILES)
                    nc.vector.scalar_tensor_tensor(combine[:], picked[:], ROUTE_SCALE,
                                                   inv_total[:].unsqueeze(2).broadcast_to([P, TILES, E]),
                                                   ALU.mult, ALU.mult).then_inc(route_step, TILES - 2)

                    def gather(e):
                        dve.wait_ge(y_done, g * N + e + 1)
                        if e == 0:
                            dve.wait_ge(route_step, g * ROUTE + (ROUTE + 1))
                        elif e >= 1:
                            dve.wait_ge(acc_done, g * N + e)
                        for c in range(TILES):
                            y = ps_y[e % 2][:, c * P:(c + 1) * P]
                            if e == 0:
                                t = nc.vector.tensor_scalar(acc[:, c, :], y, combine[:, c, 0:1], None, ALU.mult)
                            elif e < E:
                                t = nc.vector.scalar_tensor_tensor(acc[:, c, :], y, combine[:, c, e:e + 1],
                                                                   acc[:, c, :], ALU.mult, ALU.add)
                        if e == E:
                            t = nc.vector.tensor_tensor(acc[:].rearrange("p c d -> p (c d)"), ps_y[e % 2][:],
                                                        acc[:].rearrange("p c d -> p (c d)"), ALU.add)
                        t.then_inc(acc_done, 1)

                    for e in range(N):
                        dve.wait_ge(silu_done, g * N + e + 1)
                        dve.wait_ge(u_done, g * N + e + 1)
                        if e >= 2:
                            dve.wait_ge(y_done, g * N + e - 1)
                        nc.vector.tensor_tensor(hidden[e % 2][:], silu[e % 2][:], ps_u[e % 2][:],
                                                ALU.mult).then_inc(hid_done, 1)
                        if e >= 1:
                            gather(e - 1)
                    gather(N - 1)
                    dve.wait_ge(acc_done, g * N + N)
                    nc.vector.tensor_tensor(x_tile(0, TILES), x_tile(0, TILES),
                                            acc[:].rearrange("p c d -> p (c d)"), ALU.add).then_inc(group_done, 1)


def build(nc, ins, out, stages):
    B = ins["x"].shape[0]
    with ExitStack() as ctx:
        mem = {}

        def keep(name, shape, dt=F32):
            mem[name] = ctx.enter_context(nc.sbuf_tensor(name, shape, dt))
            return mem[name]

        keep("x", [P, B * SEQ])
        keep("ident", [P, P])
        keep("minus_half", [P, 16])
        E = ins["router"].shape[1]
        mem["experts"] = E
        for n in ("moe_gate", "moe_up", "moe_down"):
            keep(n, [P, (E + 1) * P])
        keep("plus_half", [P, 16])
        keep("router", [P, E])
        keep("expert_bias", [P, E])
        keep("xT", [P, B * SEQ])
        mem["o"] = mem["xT"]
        names = ["ident", "router", "moe_gate", "moe_up", "moe_down"]
        for n in ("ident16", "future16", "upto", "half_norm", "own_head", "strip_head"):
            keep(n, list(ins[n].shape), ins[n].dtype)
            names.append(n)
        tables_a = ctx.enter_context(ExitStack())
        for n in ("twos_upto", "twos", "state0", "lin_mask", "cos2", "sin2", "cos_sin"):
            mem[n] = tables_a.enter_context(nc.sbuf_tensor(n, list(ins[n].shape), ins[n].dtype))
            names.append(n)
        mem["b_out4"] = tables_a.enter_context(nc.sbuf_tensor("b_out4", [P, SEQ], F32))
        loaded = ctx.enter_context(nc.semaphore("loaded"))
        consts = ctx.enter_context(nc.semaphore("consts"))
        stored = ctx.enter_context(nc.semaphore("stored"))
        loads = [(mem["x"][:].rearrange("p (t d) -> p t d", d=P),
                  ins["x"].rearrange("b (c p) d -> p (b c) d", p=P))]
        for n in names:
            loads.append((mem[n][:], ins[n]))
        loads.append((mem["expert_bias"][:], ins["expert_bias"].partition_broadcast(P)))
        for c in range(TILES):
            loads.append((mem["b_out4"][:, c * P:(c + 1) * P], ins["b_out"].partition_broadcast(P)))
        with nc.Block() as block:
            @block.sync
            def _(sp):
                for dst, src in loads:
                    sp.dma_start(dst, src).then_inc(loaded, 16)
                sp.wait_ge(loaded, 16 * len(loads))

            @block.vector
            def _(dve):
                nc.vector.memset(mem["minus_half"][:], -0.5).then_inc(consts, 1)
                nc.vector.memset(mem["plus_half"][:], 0.5).then_inc(consts, 1)
                dve.wait_ge(consts, 2)
        for n, s in enumerate(stages):
            tag = f"{s}{n}_"
            if s == "a":
                norm_block(nc, mem, B, attention=True, tag=tag)
                attention_block(nc, mem, ins, B)
                tables_a.close()
            if s == "b":
                tables_a.close()
                norm_block(nc, mem, B, attention=False, tag=tag)
                transformer_block(nc, mem, ins, B)
            if s == "ffn":
                moe_block(nc, mem, B, tag)
        with nc.Block() as block:
            @block.sync
            def _(sp):
                sp.dma_start(out.rearrange("b (c p) d -> p (b c) d", p=P),
                             mem["x"][:].rearrange("p (t d) -> p t d", d=P)).then_inc(stored, 16)
                sp.wait_ge(stored, 16)


def lay_out(t):
    f = "L0_ffn_"
    a = {"x": t["L0_attn_a_X"], "expert_bias": t[f + "expert_bias"],
         "router": t[f + "gate_w"].T, "ident": np.eye(P, dtype=np.float32)}
    for name, experts, shared in (("moe_gate", "w_gate", "shared_gate_w"), ("moe_up", "w_up", "shared_up_w"),
                                  ("moe_down", "w_down", "shared_down_w")):
        w = np.concatenate([t[f + experts], t[f + shared][None]], axis=0)
        a[name] = w.transpose(2, 0, 1).reshape(P, -1)
    f = "L0_attn_a_"
    HHD = t[f + "w_out"].shape[0]
    HD, pairs = 64, HHD // P
    q, k, v = (t[f + "w_qkv"][:, i * HHD:(i + 1) * HHD] for i in range(3))
    kk, vk = (t[f + "w_kvkv"][:, i * HHD:(i + 1) * HHD] for i in range(2))
    blocks = [w.reshape(P, pairs, P).transpose(1, 0, 2) for w in (q, vk, k, kk, v)]
    a["pairs"] = np.concatenate(blocks + [t[f + "w_out"].reshape(pairs, P, P)], axis=2)
    a["b_out"] = t[f + "b_out"]
    a.update(tables(HD))
    f = "L0_attn_b_"
    L = t[f + "Wq"].shape[0]
    a["t_sq"] = np.concatenate([t[f + n] for n in ("Wq", "Wk", "Wv", "Wo")], axis=2)
    a["t_w1"] = t[f + "W1"]
    a["t_w2"] = t[f + "W2"].reshape(L, -1, P, P).transpose(0, 2, 1, 3).reshape(L, P, -1)
    heads, _, at = feature_places()
    omega = np.zeros((L, P // 2, 2 * P), np.float32)
    for col in range(2 * P):
        row = heads[col] % 8 * 8
        omega[:, row:row + 8, col] = t[f + "omega"][:, :, at[col]]
    a["t_omega"] = omega
    columns = [t[f + n][:, :, None] for n in ("bq", "bk", "g1", "be1")]
    a["t_cols"] = np.concatenate(columns + [t[f + "bf1"].reshape(L, -1, P).transpose(0, 2, 1)], axis=2)
    a["t_rows"] = np.concatenate([t[f + n] for n in ("bv", "bo", "g1", "be1", "bf2", "g2", "be2")], axis=1)
    for n in ("t_sq", "t_w1", "t_w2", "t_omega", "t_cols", "t_rows"):
        a[n] = np.concatenate([a[n], np.zeros_like(a[n][:1])])
    return a


def feature_places():
    col = np.arange(2 * P)
    half, strip, head, sign, m = col // P, col // 32 % 4, col // 16 % 2, 1 - 2 * (col // 8 % 2), col % 8
    return 8 * half + 2 * strip + head, sign, m


def tables(HD):
    f32 = np.float32
    i, j = np.arange(P)[:, None], np.arange(P)[None, :]
    freq = (f32(1.0) / f32(10000.0) ** (np.arange(0, HD, 2, dtype=f32) / f32(HD))).astype(f32)
    angle = np.repeat(np.arange(SEQ, dtype=f32)[:, None] * freq[None, :], 2, axis=1).T
    cos, sin = np.cos(angle).astype(f32), np.sin(angle).astype(f32)
    eye = np.eye(HD, dtype=f32) * f32(HD ** 0.5)
    turned = np.zeros((HD, HD), f32)
    turned[1::2, 0::2] = -eye[0::2, 0::2]
    turned[0::2, 1::2] = eye[0::2, 0::2]
    state0 = np.concatenate([eye, turned], axis=1)
    bf16 = mybir.dt.np(BF16)
    key, query = i % (P // 2), j[:, :P // 2]
    heads, _, _ = feature_places()
    root = 8 ** -0.25
    squares = (np.arange(P)[:, None] - P // 2) // 8 == heads[None, :] % 8
    return {
        "upto": (key <= query).astype(f32),
        "half_norm": (squares * f32(-0.5 * root * root)).astype(f32),
        "own_head": (heads[:P, None] == np.arange(8 * 9)[None, :] // 9).astype(f32),
        "strip_head": np.stack([(np.arange(P) // 16 % 2 == p) for p in range(2)], axis=1).astype(f32),
        "twos_upto": 2.0 * (i <= j).astype(f32), "twos": np.full((P, P), 2.0, f32),
        "state0": np.concatenate([state0, state0], axis=0),
        "lin_mask": np.concatenate([(i <= j), (i < j) + 0.5 * (i == j)], axis=1).astype(f32),
        "cos2": np.concatenate([cos, cos]), "sin2": np.concatenate([sin, sin]),
        "cos_sin": np.concatenate([cos, sin]),
        "ident16": np.eye(P).astype(bf16), "future16": np.where(j > i, -1e30, 0.0).astype(bf16),
    }


def kernel(**inputs):
    import concourse.bacc as bacc
    from concourse.bass_utils import run_bass_kernel_spmd

    t = {k: np.asarray(v) for k, v in inputs.items()}
    arrays = {k: np.ascontiguousarray(v) for k, v in lay_out(t).items()}
    nc = bacc.Bacc("TRN2", target_bir_lowering=False, num_devices=1)
    ins = {k: nc.dram_tensor("in_" + k, list(v.shape), mybir.dt.from_np(v.dtype), kind="ExternalInput").ap()
           for k, v in arrays.items()}
    out = nc.dram_tensor("out", list(arrays["x"].shape), F32, kind="ExternalOutput").ap()
    build(nc, ins, out, STAGES)
    r = run_bass_kernel_spmd(nc, [{"in_" + k: v for k, v in arrays.items()}], core_ids=[0])
    return r.results[0]["out"]
```

```python
from contextlib import ExitStack

import concourse.bass as bass
import concourse.mybir as mybir
import numpy as np

F32 = mybir.dt.float32
BF16 = mybir.dt.bfloat16
F32R = mybir.dt.float32r
ALU = mybir.AluOpType
ACT = mybir.ActivationFunctionType
AX = mybir.AxisListType
P = 128
TILES = 4
SEQ = TILES * P
LN_EPS = 1e-5

UNROLLED = 2
STAGES = ("a", "ffn", "b", "ffn")

def layernorm_steps(nc, dve, m, s, g, read):
    for c in range(TILES):
        nc.vector.bn_stats(m["stats"][:, c, :], read(c)).then_inc(s["stats_done"], 1)
    dve.wait_ge(s["stats_done"], (g + 1) * TILES)
    dve.nop(nofuse=True)
    for c in range(TILES):
        nc.vector.bn_aggr(m["mean_var"][:, c, :], m["stats"][:, c, :]).then_inc(s["mv_done"], 1)
    dve.wait_ge(s["mv_done"], (g + 1) * TILES)
    nc.vector.tensor_scalar(m["var_eps"][:], m["mean_var"][:, :, 1], LN_EPS, None,
                            ALU.add).then_inc(s["eps_done"], 1)
    dve.wait_ge(s["rstd_done"], g + 1)
    for c in range(TILES):
        nc.vector.tensor_scalar(m["xn"][:, c, :], read(c), m["mean_var"][:, c, 0:1], m["rstd"][:, c:c + 1],
                                ALU.subtract, ALU.mult).then_inc(s["xn_done"], 1)


def norm_block(nc, mem, groups, attention, tag):
    with ExitStack() as ctx:
        def sb(name, shape, dt=F32):
            return ctx.enter_context(nc.sbuf_tensor(tag + name, shape, dt))

        def sem(name):
            return ctx.enter_context(nc.semaphore(tag + name))

        m = {"stats": sb("stats", [P, TILES, 6]), "mean_var": sb("mean_var", [P, TILES, 2]),
             "var_eps": sb("var_eps", [P, TILES]), "rstd": sb("rstd", [P, TILES]),
             "xn": sb("xn", [P, TILES, P])}
        s = {n: sem(n) for n in ("stats_done", "mv_done", "eps_done", "rstd_done", "xn_done")}
        turned, xT_done, out_done = sem("turned"), sem("xT_done"), sem("out_done")
        ps_t = ctx.enter_context(nc.psum_tensor(tag + "ps_t", [P, 512], F32))
        with nc.Block() as block:
            @block.vector
            def _(dve):
                with dve.Fori(0, groups) as g:
                    x4 = mem["x"][:, bass.ds(g * SEQ, SEQ)]
                    layernorm_steps(nc, dve, m, s, g, lambda c: mem["x"][:, bass.ds(g * SEQ + c * P, P)])
                    dve.wait_ge(s["xn_done"], (g + 1) * TILES)
                    if attention:
                        nc.vector.tensor_tensor(
                            x4, x4, mem["b_out4"][:], ALU.add).then_inc(out_done, 1)
                        dve.wait_ge(turned, g + 1)
                    else:
                        nc.vector.tensor_copy(mem["o"][:, bass.ds(g * SEQ, SEQ)],
                                              m["xn"][:].rearrange("p c d -> p (c d)")).then_inc(out_done, 1)

            @block.gpsimd
            def _(pool):
                with pool.Fori(0, groups) as g:
                    pool.wait_ge(s["eps_done"], g + 1)
                    nc.gpsimd.tensor_tensor(m["rstd"][:], m["var_eps"][:], mem["minus_half"][:, 0:TILES],
                                            ALU.pow).then_inc(s["rstd_done"], 1)

            if attention:
                @block.tensor
                def _(pe):
                    with pe.Fori(0, groups) as g:
                        pe.wait_ge(s["xn_done"], g * TILES + TILES)
                        pe.wait_ge(xT_done, g + 1)
                        for c in range(TILES):
                            t = nc.tensor.transpose(ps_t[:, c * P:(c + 1) * P], m["xn"][:, c, :], mem["ident"][:])
                        t.then_inc(turned, 1)

                @block.scalar
                def _(act):
                    act.sem_inc(xT_done, 1)
                    with act.Fori(0, groups) as g:
                        act.wait_ge(turned, g + 1)
                        nc.scalar.copy(mem["xT"][:, bass.ds(g * SEQ, SEQ)], ps_t[:]).then_inc(xT_done, 1)


def fills(plan, steps, bank):
    return sum(plan.FILLS[step].split().count(bank) for step in steps)


class Slot:

    def __init__(self, plan, steps, passed, slots, group, layer, parity, new_weights=False):
        self.plan = plan
        self.steps = steps
        self.passed, self.slots = passed, slots
        self.group = group
        self.layer = layer
        self.new_weights = new_weights
        self.shift = 0 if steps is plan.LEAD else 1
        self.parity = parity
        self.parity_in = (parity + self.shift) % 2

    def of(self, phase):
        return self.group + {"in": self.shift, "mix": 0, "out": -1}[phase]

    def fill(self, bank, step):
        plan = self.plan
        n = sum(fills(plan, p, bank) for p in self.passed) + fills(plan, self.steps[:self.steps.index(step)], bank)
        return self.slots * fills(plan, plan.SLOT, bank) + n


def pipeline(e, plan, weights_in, weights_out, body):
    def run(slot, sequence):
        for step in slot.steps:
            body(step, slot, sequence)

    B, once = plan.B, [plan.LEAD, plan.FIRST]
    weights_in(0, None)
    run(Slot(plan, plan.LEAD, [], 0, 0, 0, 0, new_weights=True), {"in": 0, "next": 1})
    run(Slot(plan, plan.FIRST, once[:1], 0, 0, 0, 0), {"in": 1, "next": 2})
    with e.Fori(0, plan.LAYERS) as l:
        g = l * B
        weights_out(l, Slot(plan, plan.SLOT, once, g, g + 1, l, 1))
        with e.Fori(0, (B - 2) // UNROLLED) as tn:
            for u in range(UNROLLED):
                z = tn * UNROLLED + (1 + u)
                run(Slot(plan, plan.SLOT, once, g + (z - 1), g + z, l, (1 + u) % 2),
                    {"in": z + 1, "next": z + 2, "out": z - 1})
        slot = Slot(plan, plan.SLOT, once, g + (B - 2), g + (B - 1), l, 1, new_weights=True)
        weights_in(l + 1, slot)
        run(slot, {"in": 0, "next": 1, "out": B - 2})
        run(Slot(plan, plan.SLOT, once, g + (B - 1), g + B, l, 0), {"in": 1, "next": 2, "out": B - 1})


def sequence_of(tokens, z):
    return tokens[:, z * SEQ:(z + 1) * SEQ] if isinstance(z, int) else tokens[:, bass.ds(z * SEQ, SEQ)]


class AttentionPlan:
    LEAD = "X P0 P1 P2 P3 Xn L0 St L1 Z Y0 keys cum Y1".split()
    SLOT = ("P0 S0 S1 headT P1 outs T0 P2 S2 W0 T1 S3 P3 W1 Xn T2 S4 L0 W2 T3 S5 St L1 W3 T4 S6 Z W4 T5 S7 Y0 keys W5 T6 "
            "cum W6 T7 Y1 W7").split()
    FIRST = [step for step in SLOT if step not in ("headT", "outs")]
    FILLS = dict(X="", Xn="", keys="", P0="a1 a0", P1="a2 a1", P2="a0 a2", P3="a1 a0", L0="a2 a0", St="d", L1="a1 a2", Z="a0 a1",
                 Y0="a2", cum="d", Y1="a0", headT="t", outs="s0",
                 **{f"S{u}": f"s{u % 2}" for u in range(8)}, **{f"T{u}": "t" for u in range(8)},
                 **{f"W{u}": "z" if u == 7 else "" for u in range(8)})
    BANKS = ["a0", "a1", "a2", "d", "s0", "s1", "t", "z"]


def attention_block(nc, mem, ins, B):
    H, HD, EPS = 16, 64, 1e-8
    PAIRS = H // 2
    U = 2 * TILES
    plan = AttentionPlan()
    plan.B, plan.LAYERS = B, PAIRS
    with ExitStack() as ctx:
        def sb(name, shape, dt=F32):
            return ctx.enter_context(nc.sbuf_tensor("a_" + name, shape, dt))

        def sem(name):
            return ctx.enter_context(nc.semaphore("a_" + name))

        staged = sb("staged", [P, 6 * P])
        w_in = sb("w_in", [P, 5 * P])
        w_rk, w_tok = w_in[:, 0:P], w_in[:, P:5 * P]
        w_hi, w_lo = sb("w_hi", [P, 8 * P], F32R), sb("w_lo", [P, 8 * P], F32R)
        w_o = sb("w_o", [P, P])
        x_hi, x_lo = sb("x_hi", [P, SEQ], F32R), sb("x_lo", [P, SEQ], F32R)
        qv = sb("qv", [P, TILES, 2, P])
        kcos, ksin = sb("kcos", [P, SEQ]), sb("ksin", [P, SEQ])
        state = sb("state", [P, TILES, P])
        lin = [sb(f"lin{h}", [P, TILES, 2, P]) for h in range(2)]
        zk = sb("zk", [P, TILES, 2, HD])
        inc = sb("inc", [P, U])
        norm2 = sb("norm2", [P, U])
        norm = sb("norm", [P, U])
        norm8 = sb("norm8", [P, U])
        tok = [sb(f"tok{i}", [P, TILES, 4 * P]) for i in range(2)]
        keys = [[sb(f"keys{i}_{h}", [P, SEQ]) for h in range(2)] for i in range(2)]
        query = [[sb(f"query{i}_{h}", [P, SEQ]) for h in range(2)] for i in range(2)]
        scale = [sb(f"scale{i}", [P, U]) for i in range(2)]
        neg_max = sb("neg_max", [P, U])
        shift = sb("shift", [P, U])
        row_sum = sb("row_sum", [P, U])
        inv_sum = sb("inv_sum", [P, U])
        prob = [sb(f"prob{i}", [P, SEQ]) for i in range(2)]
        probT = [sb(f"probT{i}", [P, SEQ]) for i in range(2)]
        heads = sb("heads", [P, TILES, 2 * HD])
        headsT = sb("headsT", [P, SEQ])
        ps = {k: ctx.enter_context(nc.psum_tensor("a_" + k, [P, 512], F32)) for k in plan.BANKS}

        filled = {k: sem("filled_" + k) for k in plan.BANKS}
        emptied = {k: sem("emptied_" + k) for k in plan.BANKS}
        EVENTS = dict(xcopy=2, keys=4, statec=2, incs=1, pows=1, n8=1, scales=1, negs=8, shifts=8, inv=1)
        PHASE = {n: "mix" if n in ("negs", "shifts", "inv") else "in" for n in EVENTS}
        s = {n: sem(n) for n in EVENTS}
        w_loaded, state_set = sem("w_loaded"), sem("state_set")
        made_in = {n: sem("made_in_" + n) for n in ("act", "dve")}
        made_out, made_qvk, w_built, wrapped = sem("made_out"), sem("made_qvk"), sem("w_built"), sem("wrapped")

        def begin(e, names):
            for n in names.split():
                e.sem_inc(s[n], 1)

        def wait(e, name, slot, n):
            e.wait_ge(s[name], slot.of(PHASE[name]) * EVENTS[name] + (n + 1))

        def wait_filled(e, bank, slot, step):
            e.wait_ge(filled[bank], slot.fill(bank, step) + 2)

        def wait_emptied(e, bank, slot, step):
            e.wait_ge(emptied[bank], slot.fill(bank, step) + 2)

        def wait_free(e, bank, slot, step):
            e.wait_ge(emptied[bank], slot.fill(bank, step) + 1)

        def wait_staged(e, hp, slot):
            e.wait_ge(w_loaded, (hp + 1) * 16)
            if slot is not None:
                for bank in ("a0", "a1", "s0"):
                    e.wait_ge(filled[bank], slot.fill(bank, slot.steps[0]) + 1)
            e.nop(nofuse=True)

        with nc.Block() as block:
            @block.sync
            def _(sp):
                with sp.Fori(0, PAIRS + 1) as hp:
                    for made in (made_in["act"], made_in["dve"], made_out):
                        sp.wait_ge(made, hp + 1)
                    sp.dma_start(staged[:], ins["pairs"][bass.ds(hp, 1), :, :].squeeze(0)).then_inc(w_loaded, 16)
                sp.wait_ge(w_loaded, (PAIRS + 1) * 16)

            @block.gpsimd
            def _(pool):
                begin(pool, "xcopy pows")
                nc.gpsimd.tensor_copy(mem["xT"][:, B * SEQ:(B + 1) * SEQ], mem["xT"][:, 0:SEQ]).then_inc(wrapped, 1)
                pool.wait_ge(wrapped, 1)
                pool.nop(nofuse=True)

                def weights_in(hp, slot):
                    pass

                def weights_out(hp, slot):
                    pass

                def body(step, slot, sequence):
                    if step in ("X", "Xn"):
                        ahead = 2 * (step == "Xn")
                        if ahead:
                            wait_filled(pool, "a0", slot, "P3")
                            pool.nop(nofuse=True)
                        x_ = sequence_of(mem["xT"], sequence["in" if step == "X" else "next"])
                        nc.gpsimd.tensor_copy(x_hi[:], x_).then_inc(s["xcopy"], 1)
                        wait(pool, "xcopy", slot, ahead + 1)
                        pool.nop(nofuse=True)
                        nc.gpsimd.tensor_tensor(x_lo[:], x_, x_hi[:].bitcast(F32), ALU.subtract).then_inc(s["xcopy"], 1)
                    elif step == "cum":
                        wait_emptied(pool, "d", slot, "cum")
                        pool.nop(nofuse=True)
                        nc.gpsimd.tensor_tensor(norm[:], norm2[:], mem["plus_half"][:, 0:U],
                                                ALU.pow).then_inc(s["pows"], 1)

                pipeline(pool, plan, weights_in, weights_out, body)

            @block.tensor
            def _(pe):
                for k in plan.BANKS:
                    pe.sem_inc(filled[k], 1)

                def rows(h):
                    return slice(h * HD, (h + 1) * HD)

                def weights_in(hp, slot):
                    pass

                def weights_out(hp, slot):
                    pass

                def body(step, slot, sequence):
                    def free(bank):
                        wait_free(pe, bank, slot, step)

                    def ready(bank, of):
                        wait_emptied(pe, bank, slot, of)

                    def project(bank, operands):
                        free(bank)
                        for k, (w, x) in enumerate(((w_hi, x_hi), (w_hi, x_lo), (w_lo, x_hi))):
                            stationary, moving = operands(w, x)
                            t = nc.tensor.matmul(ps[bank][:], stationary, moving, start=k == 0, stop=k == 2)
                        t.then_inc(filled[bank], 1)

                    tokens = tok[slot.parity_in]
                    if step == "P0":
                        if slot.new_weights:
                            pe.wait_ge(made_qvk, slot.layer + (1 + slot.shift))
                            pe.nop(nofuse=True)
                        wait(pe, "xcopy", slot, 2)
                        for bank, n in (("a1", 1), ("a0", 0)):
                            project(bank, lambda w, x, n=n: (w[:, n * P:(n + 1) * P], x[:]))
                    elif step in ("P1", "P2"):
                        if slot.new_weights and step == "P1":
                            pe.wait_ge(made_in["dve"], slot.layer + (2 + slot.shift))
                            pe.nop(nofuse=True)
                        for n, bank in enumerate((("a2", "a1"), ("a0", "a2"))[step == "P2"]):
                            c = 2 * (step == "P2") + n
                            project(bank, lambda w, x, c=c: (x[:, c * P:(c + 1) * P], w[:, 4 * P:8 * P]))
                    elif step == "P3":
                        for bank, n in (("a1", 2), ("a0", 3)):
                            project(bank, lambda w, x, n=n: (w[:, n * P:(n + 1) * P], x[:]))
                    elif step in ("L0", "L1"):
                        half = int(step[1])
                        if half == 0:
                            ready("a0", "P0")
                            ready("a1", "P0")
                        for h, bank in enumerate((("a2", "a0"), ("a1", "a2"))[half]):
                            free(bank)
                            for c in (2 * half, 2 * half + 1):
                                t = nc.tensor.matmul(ps[bank][:, (c % 2) * 2 * P:(c % 2 + 1) * 2 * P],
                                                     qv[rows(h), c, 1, :],
                                                     qv[rows(h), c, :, :].rearrange("p a n -> p (a n)"),
                                                     start=True, stop=True)
                            t.then_inc(filled[bank], 1)
                    elif step == "St":
                        ready("a2", "P1")
                        ready("a1", "P1")
                        ready("a0", "P2")
                        free("d")
                        for c in range(TILES - 1):
                            for h in range(2):
                                t = nc.tensor.matmul(ps["d"][rows(h), c * P:(c + 1) * P],
                                                     tokens[:, c, 3 * P + h * HD:3 * P + (h + 1) * HD],
                                                     tokens[:, c, h * P:(h + 1) * P], start=True, stop=True)
                        t.then_inc(filled["d"], 1)
                    elif step == "Z":
                        ready("d", "St")
                        ready("a2", "L1")
                        ready("a1", "L1")
                        for h, bank in enumerate(("a0", "a1")):
                            free(bank)
                            for c in range(TILES):
                                o = ps[bank][:, c * HD:(c + 1) * HD]
                                nc.tensor.matmul(o, lin[h][:, c, 1, :], tokens[:, c, h * P:h * P + HD],
                                                 start=True, stop=False)
                                t = nc.tensor.matmul(o, qv[rows(h), c, 1, :], state[rows(h), c, 0:HD],
                                                     start=False, stop=True)
                            t.then_inc(filled[bank], 1)
                    elif step in ("Y0", "Y1"):
                        h = int(step[1])
                        bank = ("a2", "a0")[h]
                        free(bank)
                        for c in range(TILES):
                            o = ps[bank][:, c * P:(c + 1) * P]
                            nc.tensor.matmul(o, tokens[:, c, h * P:(h + 1) * P], lin[h][:, c, 0, :],
                                             start=True, stop=False)
                            t = nc.tensor.matmul(o, state[rows(h), c, :], qv[rows(h), c, 0, :],
                                                 start=False, stop=True)
                        t.then_inc(filled[bank], 1)
                    elif step == "cum":
                        wait(pe, "incs", slot, 1)
                        free("d")
                        o = ps["d"][:, 3 * P:3 * P + U]
                        nc.tensor.matmul(o, mem["twos_upto"][:], inc[:], start=True, stop=False)
                        for back in range(1, TILES):
                            t = nc.tensor.matmul(o[:, 2 * back:U], mem["twos"][:], inc[:, 0:U - 2 * back],
                                                 start=False, stop=back == TILES - 1)
                        t.then_inc(filled["d"], 1)
                    elif step == "headT":
                        pe.wait_ge(emptied["z"], slot.of("out") + 2)
                        free("t")
                        for c in range(TILES):
                            t = nc.tensor.transpose(ps["t"][:, c * P:(c + 1) * P], heads[:, c, :], mem["ident"][:])
                        t.then_inc(filled["t"], 1)
                    elif step == "outs":
                        ready("t", "headT")
                        pe.wait_ge(made_out, slot.layer + 2)
                        free("s0")
                        for c in range(TILES):
                            t = nc.tensor.matmul(ps["s0"][:, c * P:(c + 1) * P], headsT[:, c * P:(c + 1) * P],
                                                 w_o[:], start=True, stop=True)
                        t.then_inc(filled["s0"], 1)
                    elif step[0] == "S":
                        u = int(step[1])
                        h, c = divmod(u, TILES)
                        o, queries, k_ = ps[f"s{u % 2}"], query[slot.parity][h], keys[slot.parity][h]
                        if c == 0:
                            pe.wait_ge(s["keys"], slot.of("mix") * 4 + (2 * h + 3))
                            bank = ("a2", "a0")[h]
                            pe.wait_ge(emptied[bank], slot.fill(bank, "S0") + 1)
                        free(f"s{u % 2}")
                        nc.tensor.matmul(o[:, 0:(c + 1) * P], queries[:, c * P:(c + 1) * P],
                                         k_[:, 0:(c + 1) * P], start=True, stop=False)
                        nc.tensor.matmul(o[:, c * P:(c + 1) * P], mem["ident16"][:], mem["future16"][:],
                                         start=False, stop=True).then_inc(filled[f"s{u % 2}"], 1)
                    elif step[0] == "T":
                        u = int(step[1])
                        ready(f"s{u % 2}", f"S{u}")
                        free("t")
                        for j in range(u % TILES + 1):
                            t = nc.tensor.transpose(ps["t"][:, j * P:(j + 1) * P],
                                                    prob[u % 2][:, j * P:(j + 1) * P], mem["ident"][:])
                        t.then_inc(filled["t"], 1)
                    elif step[0] == "W":
                        u = int(step[1])
                        h, c = divmod(u, TILES)
                        ready("t", f"T{u}")
                        if u == 0:
                            pe.wait_ge(emptied["z"], slot.of("mix") + 1)
                        for j in range(c + 1):
                            t = nc.tensor.matmul(ps["z"][:, (2 * c + h) * HD:(2 * c + h + 1) * HD],
                                                 probT[u % 2][:, j * P:(j + 1) * P],
                                                 tok[slot.parity][:, j, 2 * P + h * HD:2 * P + (h + 1) * HD],
                                                 start=j == 0, stop=j == c)
                        if u == U - 1:
                            t.then_inc(filled["z"], 1)

                pipeline(pe, plan, weights_in, weights_out, body)

            @block.scalar
            def _(act):
                for k in plan.BANKS:
                    act.sem_inc(emptied[k], 1)
                act.sem_inc(made_in["act"], 1)
                act.sem_inc(made_out, 1)

                def weights_in(hp, slot):
                    wait_staged(act, hp, slot)
                    nc.scalar.copy(w_tok[:, 2 * P:3 * P], staged[:, 4 * P:5 * P])
                    nc.scalar.copy(w_tok[:, 3 * P:4 * P], staged[:, P:2 * P]).then_inc(made_in["act"], 1)

                def weights_out(hp, slot):
                    wait_staged(act, hp, slot)
                    nc.scalar.copy(w_o[:], staged[:, 5 * P:6 * P]).then_inc(made_out, 1)
                    act.wait_ge(made_out, hp + 2)
                    act.nop(nofuse=True)

                def body(step, slot, sequence):
                    def full(bank):
                        wait_filled(act, bank, slot, step)

                    if step == "P0":
                        for n, bank in enumerate(("a1", "a0")):
                            full(bank)
                            nc.scalar.copy(qv[:, :, 1 - n, :],
                                           ps[bank][:].rearrange("p (c n) -> p c n", c=TILES)).then_inc(emptied[bank], 1)
                    elif step in ("P1", "P2"):
                        for n, bank in enumerate((("a2", "a1"), ("a0", "a2"))[step == "P2"]):
                            full(bank)
                            nc.scalar.copy(tok[slot.parity_in][:, 2 * (step == "P2") + n, :],
                                           ps[bank][:]).then_inc(emptied[bank], 1)
                    elif step == "headT":
                        full("t")
                        nc.scalar.copy(headsT[:], ps["t"][:]).then_inc(emptied["t"], 1)
                    elif step[0] == "T":
                        u = int(step[1])
                        n = (u % TILES + 1) * P
                        full("t")
                        nc.scalar.copy(probT[u % 2][:, 0:n], ps["t"][:, 0:n]).then_inc(emptied["t"], 1)
                    elif step[0] == "S" and step != "St":
                        u = int(step[1])
                        h, c = divmod(u, TILES)
                        k = 2 * c + h
                        wait(act, "shifts", slot, u + 1)
                        if u == 0:
                            wait(act, "inv", slot, 0)
                            act.nop(nofuse=True)
                        nc.scalar.activation(prob[u % 2][:, 0:(c + 1) * P], ps[f"s{u % 2}"][:, 0:(c + 1) * P],
                                             ACT.Exp, bias=shift[:, k:k + 1], scale=scale[slot.parity][:, k:k + 1],
                                             accum_out=row_sum[:, k:k + 1]).then_inc(emptied[f"s{u % 2}"], 1)

                pipeline(act, plan, weights_in, weights_out, body)

            @block.vector
            def _(dve):
                dve.sem_inc(made_in["dve"], 1)
                begin(dve, "keys statec incs n8 scales negs shifts inv")
                nc.vector.tensor_copy(state[:, 0, :], mem["state0"][:]).then_inc(state_set, 1)
                dve.wait_ge(state_set, 1)

                def weights_in(hp, slot):
                    wait_staged(dve, hp, slot)
                    qvk = slice(0, 3 * P)
                    nc.vector.tensor_copy(w_hi[:, qvk], staged[:, qvk]).then_inc(w_built, 1)
                    dve.wait_ge(w_built, 3 * hp + 1)
                    nc.vector.tensor_tensor(w_lo[:, qvk], staged[:, qvk], w_hi[:, qvk].bitcast(F32),
                                            ALU.subtract).then_inc(made_qvk, 1)
                    k_, kk_ = staged[:, 2 * P:3 * P], staged[:, 3 * P:4 * P]
                    nc.vector.tensor_scalar(w_rk[:, 0:P:2], k_[:, 1:P:2], -1.0, None, ALU.mult)
                    nc.vector.tensor_copy(w_rk[:, 1:P:2], k_[:, 0:P:2])
                    for h in range(2):
                        kk_h = kk_[:, h * HD:(h + 1) * HD]
                        at = h * P
                        nc.vector.tensor_copy(w_tok[:, at:at + HD], kk_h)
                        nc.vector.tensor_scalar(w_tok[:, at + HD:at + P:2], kk_h[:, 1:HD:2], -1.0, None, ALU.mult)
                        t = nc.vector.tensor_copy(w_tok[:, at + HD + 1:at + P:2], kk_h[:, 0:HD:2])
                    t.then_inc(w_built, 1)
                    dve.wait_ge(w_built, 3 * hp + 2)
                    dve.wait_ge(made_in["act"], hp + 2)
                    dve.nop(nofuse=True)
                    others = slice(3 * P, 8 * P)
                    nc.vector.tensor_copy(w_hi[:, others], w_in[:]).then_inc(w_built, 1)
                    dve.wait_ge(w_built, 3 * hp + 3)
                    nc.vector.tensor_tensor(w_lo[:, others], w_in[:], w_hi[:, others].bitcast(F32),
                                            ALU.subtract).then_inc(made_in["dve"], 1)

                def weights_out(hp, slot):
                    pass

                def body(step, slot, sequence):
                    def full(bank):
                        wait_filled(dve, bank, slot, step)

                    if step == "P3":
                        for dst, table, bank in ((kcos, mem["cos2"], "a1"), (ksin, mem["sin2"], "a0")):
                            full(bank)
                            nc.vector.tensor_tensor(dst[:], ps[bank][:], table[:], ALU.mult).then_inc(emptied[bank], 1)
                    elif step == "keys":
                        for bank in ("a0", "a1"):
                            wait_emptied(dve, bank, slot, "P3")
                        for h in range(2):
                            own = slice(h * HD, (h + 1) * HD)
                            for rows in (own, slice((1 - h) * HD, (2 - h) * HD)):
                                nc.vector.tensor_tensor(keys[slot.parity_in][h][rows, :], kcos[own, :], ksin[own, :],
                                                        ALU.add).then_inc(s["keys"], 1)
                    elif step in ("L0", "L1"):
                        half = int(step[1])
                        for h, bank in enumerate((("a2", "a0"), ("a1", "a2"))[half]):
                            full(bank)
                            nc.vector.tensor_tensor(
                                lin[h][:, 2 * half:2 * half + 2, :, :].rearrange("p c a n -> p c (a n)"),
                                ps[bank][:].rearrange("p (c n) -> p c n", c=2),
                                mem["lin_mask"][:].unsqueeze(1).broadcast_to([P, 2, 2 * P]),
                                ALU.mult).then_inc(emptied[bank], 1)
                    elif step == "St":
                        full("d")
                        for c in range(TILES - 1):
                            if c:
                                wait(dve, "statec", slot, c)
                            t = nc.vector.tensor_tensor(state[:, c + 1, :], ps["d"][:, c * P:(c + 1) * P],
                                                        mem["state0"][:] if c == 0 else state[:, c, :], ALU.add)
                            t.then_inc(s["statec"] if c < TILES - 2 else emptied["d"], 1)
                    elif step == "Z":
                        for h, bank in enumerate(("a0", "a1")):
                            full(bank)
                            nc.vector.tensor_tensor(
                                zk[:, :, h, :], ps[bank][:, 0:TILES * HD].rearrange("p (c d) -> p c d", c=TILES),
                                tok[slot.parity_in][:, :, h * P:h * P + HD], ALU.mult).then_inc(emptied[bank], 1)
                        for bank in ("a0", "a1"):
                            wait_emptied(dve, bank, slot, "Z")
                        nc.vector.reduce_sum(inc[:], zk[:].rearrange("p c h d -> p (c h) d"),
                                             AX.X).then_inc(s["incs"], 1)
                    elif step in ("Y0", "Y1"):
                        h = int(step[1])
                        bank = ("a2", "a0")[h]
                        full(bank)
                        nc.vector.tensor_tensor(query[slot.parity_in][h][:], ps[bank][:], mem["cos_sin"][:],
                                                ALU.mult).then_inc(emptied[bank], 1)
                    elif step == "cum":
                        full("d")
                        nc.vector.tensor_scalar(norm2[:], ps["d"][:, 3 * P:3 * P + U], float(HD * HD), 0.0,
                                                ALU.add, ALU.max).then_inc(emptied["d"], 1)
                        wait(dve, "pows", slot, 1)
                        nc.vector.tensor_scalar(norm8[:], norm[:], EPS, float(HD) ** 0.5,
                                                ALU.add, ALU.mult).then_inc(s["n8"], 1)
                        wait(dve, "n8", slot, 1)
                        nc.vector.reciprocal(scale[slot.parity_in][:], norm8[:]).then_inc(s["scales"], 1)
                        wait(dve, "scales", slot, 1)
                        dve.nop(nofuse=True)
                    elif step[0] == "S":
                        u = int(step[1])
                        h, c = divmod(u, TILES)
                        k = 2 * c + h
                        full(f"s{u % 2}")
                        nc.vector.tensor_reduce(neg_max[:, k:k + 1], ps[f"s{u % 2}"][:, 0:(c + 1) * P], AX.X, ALU.max,
                                                negate=True).then_inc(s["negs"], 1)
                        wait(dve, "negs", slot, u + 1)
                        nc.vector.tensor_scalar(shift[:, k:k + 1], neg_max[:, k:k + 1],
                                                scale[slot.parity][:, k:k + 1], None,
                                                ALU.mult).then_inc(s["shifts"], 1)
                    elif step == "W7":
                        for u in (U - 2, U - 1):
                            wait_emptied(dve, f"s{u % 2}", slot, f"S{u}")
                        nc.vector.reciprocal(inv_sum[:], row_sum[:]).then_inc(s["inv"], 1)
                        full("z")
                        wait(dve, "inv", slot, 1)
                        nc.vector.tensor_tensor(heads[:].rearrange("p c (h d) -> p (c h) d", h=2),
                                                ps["z"][:].rearrange("p (k d) -> p k d", d=HD),
                                                inv_sum[:].unsqueeze(2).broadcast_to([P, U, HD]),
                                                ALU.mult).then_inc(emptied["z"], 1)
                    elif step == "outs":
                        full("s0")
                        x4 = sequence_of(mem["x"], sequence["out"])
                        nc.vector.tensor_tensor(x4, ps["s0"][:], x4, ALU.add).then_inc(emptied["s0"], 1)

                pipeline(dve, plan, weights_in, weights_out, body)


class TransformerPlan:
    LEAD = "turn project values mapq mapk keys sums".split()
    FIRST = "turn S00 project S01 values W00 W01 S10 S11 mapq W10 mapk W11 keys sums".split()
    SLOT = ("S00 turn S01 nums W00 project W01 S10 att values S11 Wo mapq W10 mapk W11 h1 keys W1 sums "
            "W2").split()
    FILLS = dict(turn="w0", project="w1 w0", values="w1", mapq="w0 w1", mapk="s0 s1", keys="w0 w1", sums="w0 s3",
                 S00="s0 s1", S01="s2 s3", S10="s0 s1", S11="s2 s3", W00="", W01="", W10="n0", W11="n1",
                 nums="w0 w1", att="w0", Wo="w1", h1="s2", W1="s0 s1 s2 s3", W2="w1")
    BANKS = ["w0", "w1", "s0", "s1", "s2", "s3", "n0", "n1"]


def transformer_block(nc, mem, ins, B):
    L, H, D, FEAT, FT = 6, 16, 8, 16, 4
    V = D + 1
    EPS = 1e-6 * FEAT
    HALF = H // 2 * V
    SPAN, SPANS = P // 2, 2 * TILES
    DIAGONAL = HALF + 2 * V
    ROOT = float(D) ** -0.25
    plan = TransformerPlan()
    plan.B, plan.LAYERS = B, L
    with ExitStack() as ctx:
        def sb(name, shape, dt=F32):
            return ctx.enter_context(nc.sbuf_tensor("t_" + name, shape, dt))

        def sem(name):
            return ctx.enter_context(nc.semaphore("t_" + name))

        w_in = sb("w_in", [P, 3, P])
        omega = sb("omega", [P, 2 * P])
        cols_in = sb("cols_in", [P, 2])
        bv = sb("bv", [P, P])
        w_o = sb("w_o", [P, P])
        w_1 = sb("w_1", [P, FT * P])
        w_2 = sb("w_2", [P, FT, P])
        cols = sb("cols", [P, 2 + FT])
        cols_v = sb("cols_v", [P, 2 + FT])
        rows = sb("rows", [P, 6, P])
        be1_bf2 = sb("be1_bf2", [P, P])
        next_sq, next_1 = sb("next_sq", [P, 4 * P]), sb("next_1", [P, FT * P])
        next_2, next_omega = sb("next_2", [P, FT * P]), sb("next_omega", [P // 2, 2 * P])
        next_cols, next_rows = sb("next_cols", [P, 4 + FT]), sb("next_rows", [P, 7 * P])
        o_now = sb("o_now", [P, TILES, P])
        oT = sb("oT", [P, SEQ])
        proj = [[sb(f"{n}{t}", [P, SEQ]) for t in range(2)] for n in ("qq", "kk")]
        phi_q = [[sb(f"phi_q{t}_{i}", [P, SEQ]) for t in range(2)] for i in range(2)]
        phi_k = [sb(f"phi_k{t}", [P, SEQ]) for t in range(2)]
        kz = [sb(f"kz{t}", [P, SPANS, 2, SPAN]) for t in range(2)]
        qz = [sb(f"qz{t}", [P, SPANS, 4, SPAN]) for t in range(2)]
        k_tok = sb("k_tok", [P, 2, TILES, P])
        v_tok = sb("v_tok", [P, TILES, 2, H, V])
        v_pad = sb("v_pad", [P, SPANS, H // 2 * DIAGONAL])
        kv = sb("kv", [P, 2, SPANS - 1, HALF])
        mixed = [[sb(f"mixed{i}_{n}", [P, 2, 4, SPAN]) for n in range(4)] for i in range(2)]
        num = [sb(f"num{t}", [HALF, SEQ]) for t in range(2)]
        o_bias = sb("o_bias", [P, TILES, P])
        den = sb("den", [P, 2, TILES, 8])
        inv = sb("inv", [P, 2, TILES, 8])
        att = sb("att", [P, TILES, P])
        attT = sb("attT", [P, SEQ])
        res = o_bias
        m = {"stats": sb("stats", [P, TILES, 6]), "mean_var": sb("mean_var", [P, TILES, 2]),
             "var_eps": sb("var_eps", [P, TILES]), "rstd": sb("rstd", [P, TILES]), "xn": sb("xn", [P, TILES, P])}
        h1T = oT
        scaled = sb("scaled", [P, TILES, P])
        h1b = sb("h1b", [P, TILES, P])
        hid = [sb(f"hid{f}", [P, SEQ]) for f in range(FT)]
        ps = {k: ctx.enter_context(nc.psum_tensor("t_" + k, [P, 512], F32)) for k in plan.BANKS}

        filled = {k: sem("filled_" + k) for k in plan.BANKS}
        emptied = {k: sem("emptied_" + k) for k in plan.BANKS}
        EVENTS = dict(o_now=1, o_bias=1, qz=2, kz=4, kv_sum=3, v_tok=1, v_pad=1, den=2, inv=2,
                      stats=8, mv=8, eps=2, rstd=2, xn=8, scaled=2, h1b=1, o_new=1)
        PHASE = {n: "in" if n in ("o_now", "qz", "kz", "kv_sum", "v_tok", "v_pad") else "out" for n in EVENTS}
        s = {n: sem(n) for n in EVENTS}
        w_loaded = sem("w_loaded")
        made_in = {n: sem("made_in_" + n) for n in ("act", "dve")}
        made_out = {n: sem("made_out_" + n) for n in ("act", "dve", "pool")}
        ones_set = sem("ones_set")
        LOADS = 6

        with nc.Block() as block:
            @block.sync
            def _(sp):
                with sp.Fori(0, L + 1) as l:
                    for made in list(made_in.values()) + list(made_out.values()):
                        sp.wait_ge(made, l + 1)
                    for dst, name in ((next_sq, "t_sq"), (next_1, "t_w1"), (next_2, "t_w2"),
                                      (next_omega, "t_omega"), (next_cols, "t_cols")):
                        sp.dma_start(dst[:], ins[name][bass.ds(l, 1), :, :].squeeze(0)).then_inc(w_loaded, 16)
                    sp.dma_start(next_rows[:], ins["t_rows"][bass.ds(l, 1), :].squeeze(0)
                                 .partition_broadcast(P)).then_inc(w_loaded, 16)
                sp.wait_ge(w_loaded, (L + 1) * 16 * LOADS)

            def begin(e, names):
                for n in names.split():
                    e.sem_inc(s[n], B + 1 if n == "o_new" else 1)

            def wait_staged(e, l, slot):
                e.wait_ge(w_loaded, (l + 1) * (16 * LOADS))
                if slot is not None:
                    for bank in ("w0", "w1"):
                        e.wait_ge(filled[bank], slot.fill(bank, slot.steps[0]) + 1)
                e.nop(nofuse=True)

            def wait(e, name, slot, n):
                e.wait_ge(s[name], slot.of(PHASE[name]) * EVENTS[name] + (n + 1 + (B if name == "o_new" else 0)))

            def wait_filled(e, bank, slot, step, n=0):
                e.wait_ge(filled[bank], slot.fill(bank, step) + (n + 2))

            def wait_emptied(e, bank, slot, step, n=0):
                e.wait_ge(emptied[bank], slot.fill(bank, step) + (n + 2))

            def wait_free(e, bank, slot, step, n=0):
                e.wait_ge(emptied[bank], slot.fill(bank, step) + (n + 1))

            def chunk(c):
                return slice(c * P, (c + 1) * P)

            @block.gpsimd
            def _(pool):
                pool.sem_inc(made_out["pool"], 1)

                def weights_in(l, slot):
                    pass

                def weights_out(l, slot):
                    wait_staged(pool, l, slot)
                    pool.wait_ge(s["o_new"], l * B + (B + 1))
                    pool.nop(nofuse=True)
                    nc.gpsimd.tensor_copy(rows[:].rearrange("p a n -> p (a n)"), next_rows[:, P:7 * P])
                    nc.gpsimd.tensor_tensor(be1_bf2[:], next_rows[:, 3 * P:4 * P], next_rows[:, 4 * P:5 * P],
                                            ALU.add).then_inc(made_out["pool"], 1)
                    pool.wait_ge(made_out["pool"], l + 2)
                    pool.nop(nofuse=True)

                def row(n):
                    return rows[:, n, :].unsqueeze(1).broadcast_to([P, TILES, P])

                def body(step, slot, sequence):
                    if step == "nums":
                        tokens = sequence_of(mem["o"], sequence["out"]).rearrange("p (c d) -> p c d", c=TILES)
                        nc.gpsimd.tensor_tensor(o_bias[:], tokens, row(0), ALU.add).then_inc(s["o_bias"], 1)
                    elif step in ("Wo", "W2"):
                        k = ("Wo", "W2").index(step)
                        wait(pool, "eps", slot, k + 1)
                        nc.gpsimd.tensor_tensor(m["rstd"][:], m["var_eps"][:],
                                                mem["minus_half"][:, 0:TILES], ALU.pow).then_inc(s["rstd"], 1)
                        wait(pool, "xn", slot, TILES * (k + 1))
                        pool.nop(nofuse=True)
                        g, b, out, name = (
                            (row(1), be1_bf2[:].unsqueeze(1).broadcast_to([P, TILES, P]), h1b[:], "h1b"),
                            (row(4), row(5), sequence_of(mem["o"], sequence["out"]).rearrange("p (c d) -> p c d", c=TILES),
                             "o_new"))[k]
                        nc.gpsimd.tensor_tensor(scaled[:], m["xn"][:], g, ALU.mult).then_inc(s["scaled"], 1)
                        wait(pool, "scaled", slot, k + 1)
                        pool.nop(nofuse=True)
                        nc.gpsimd.tensor_tensor(out, scaled[:], b, ALU.add).then_inc(s[name], 1)

                begin(pool, "o_bias rstd scaled h1b o_new")
                pipeline(pool, plan, weights_in, weights_out, body)

            @block.tensor
            def _(pe):
                for k in plan.BANKS:
                    pe.sem_inc(filled[k], 1)

                def weights_in(l, slot):
                    pass

                def weights_out(l, slot):
                    pass

                def scores(slot, i, t):
                    if i == 0 and t == 0:
                        pe.wait_ge(s["kz"], slot.of("mix") * 4 + 5)
                        pe.wait_ge(s["qz"], slot.of("mix") * 2 + 3)
                    for n in range(2):
                        bank = f"s{2 * t + n}"
                        wait_free(pe, bank, slot, f"S{i}{t}")
                        for k in range(2):
                            u = 4 * i + 2 * n + k
                            mm = nc.tensor.matmul(ps[bank][:, k * 4 * SPAN:(k + 1) * 4 * SPAN],
                                                  kz[t][:, u, :, :].rearrange("p h n -> p (h n)"),
                                                  qz[t][:, u, :, :].rearrange("p r n -> p (r n)"),
                                                  start=True, stop=True)
                        mm.then_inc(filled[bank], 1)

                def weigh(slot, i, t):
                    bank = f"n{t}"
                    if i == 0:
                        if t == 0:
                            pe.wait_ge(s["v_pad"], slot.of("mix") + 2)
                            pe.wait_ge(s["kv_sum"], slot.of("mix") * 3 + 4)
                        pe.wait_ge(emptied[bank], slot.of("mix") + 1)
                    for n in range(2):
                        wait_emptied(pe, f"s{2 * t + n}", slot, f"S{i}{t}")
                    for uu in range(4):
                        u = 4 * i + uu
                        o = ps[bank][0:HALF, u * SPAN:(u + 1) * SPAN]
                        if u:
                            nc.tensor.matmul(o, kv[:, t, u - 1, :], phi_q[slot.parity][t][:, u * SPAN:(u + 1) * SPAN],
                                             start=True, stop=False)
                        for r in range(4):
                            at = t * 4 * DIAGONAL + r * HALF
                            mm = nc.tensor.matmul(o, v_pad[:, u, at:at + HALF], mixed[i][2 * t + uu // 2][:, uu % 2, r, :],
                                                  start=u == 0 and r == 0, stop=r == 3)
                    if i == 1:
                        mm.then_inc(filled[bank], 1)

                def body(step, slot, sequence):
                    def free(bank, n=0):
                        wait_free(pe, bank, slot, step, n)

                    def ready(bank, of, n=0):
                        wait_emptied(pe, bank, slot, of, n)

                    if step == "turn":
                        wait(pe, "o_now", slot, 1)
                        free("w0")
                        for c in range(TILES):
                            t = nc.tensor.transpose(ps["w0"][:, chunk(c)], o_now[:, c, :], mem["ident"][:])
                        t.then_inc(filled["w0"], 1)
                    elif step == "project":
                        if slot.new_weights:
                            for made in made_in.values():
                                pe.wait_ge(made, slot.layer + (2 + slot.shift))
                            pe.nop(nofuse=True)
                        ready("w0", "turn")
                        for bank, n in (("w1", 0), ("w0", 1)):
                            free(bank)
                            nc.tensor.matmul(ps[bank][:], w_in[:, n, :], oT[:], start=True,
                                             stop=True).then_inc(filled[bank], 1)
                    elif step == "values":
                        free("w1")
                        for c in range(TILES):
                            t = nc.tensor.matmul(ps["w1"][:, chunk(c)], oT[:, chunk(c)], w_in[:, 2, :],
                                                 start=True, stop=True)
                        t.then_inc(filled["w1"], 1)
                    elif step in ("mapq", "mapk"):
                        j = ("mapq", "mapk").index(step)
                        ready(("w1", "w0")[j], "project")
                        for t_, bank in enumerate((("w0", "w1"), ("s0", "s1"))[j]):
                            free(bank)
                            nc.tensor.matmul(ps[bank][:], omega[:, chunk(t_)], proj[j][t_][:], start=True,
                                             stop=True).then_inc(filled[bank], 1)
                    elif step == "keys":
                        for t_, bank in enumerate(("w0", "w1")):
                            ready(f"s{t_}", "mapk")
                            free(bank)
                            for c in range(TILES):
                                t = nc.tensor.transpose(ps[bank][:, chunk(c)], phi_k[t_][:, chunk(c)],
                                                        mem["ident"][:])
                            t.then_inc(filled[bank], 1)
                    elif step == "sums":
                        wait(pe, "v_tok", slot, 1)
                        for t_, bank in enumerate(("w0", "s3")):
                            ready(("w0", "w1")[t_], "keys")
                            free(bank)
                            for c in range(TILES):
                                n = 2 if c < TILES - 1 else 1
                                t = nc.tensor.matmul(
                                    ps[bank][:, 2 * c * HALF:(2 * c + n) * HALF].rearrange("p (s n) -> p s n", s=n),
                                    k_tok[:, t_, c, :],
                                    v_tok[:, c, 0:n, 8 * t_:8 * t_ + 8, :].rearrange("p s h d -> p s (h d)"),
                                    start=True, stop=True)
                            t.then_inc(filled[bank], 1)
                    elif step[0] == "S":
                        scores(slot, int(step[1]), int(step[2]))
                    elif step in ("W00", "W01", "W10", "W11"):
                        weigh(slot, int(step[1]), int(step[2]))
                    elif step == "nums":
                        for t_, bank in enumerate(("w0", "w1")):
                            pe.wait_ge(emptied[f"n{t_}"], slot.of("out") + 2)
                            free(bank)
                            for c in range(TILES):
                                t = nc.tensor.transpose(ps[bank][:, c * HALF:(c + 1) * HALF], num[t_][:, chunk(c)],
                                                        mem["ident"][0:HALF, 0:HALF])
                            t.then_inc(filled[bank], 1)
                    elif step == "att":
                        for bank in ("w0", "w1"):
                            ready(bank, "nums")
                        free("w0")
                        for c in range(TILES):
                            t = nc.tensor.transpose(ps["w0"][:, chunk(c)], att[:, c, :], mem["ident"][:])
                        t.then_inc(filled["w0"], 1)
                    elif step == "Wo":
                        for made in (made_out["act"], made_out["dve"]):
                            pe.wait_ge(made, slot.layer + 2)
                        pe.nop(nofuse=True)
                        ready("w0", "att")
                        free("w1")
                        for c in range(TILES):
                            t = nc.tensor.matmul(ps["w1"][:, chunk(c)], attT[:, chunk(c)], w_o[:],
                                                 start=True, stop=True)
                        t.then_inc(filled["w1"], 1)
                    elif step == "h1":
                        wait(pe, "xn", slot, TILES)
                        free("s2")
                        for c in range(TILES):
                            t = nc.tensor.transpose(ps["s2"][:, chunk(c)], m["xn"][:, c, :], mem["ident"][:])
                        t.then_inc(filled["s2"], 1)
                    elif step == "W1":
                        ready("s2", "h1")
                        for f in range(FT):
                            free(f"s{f}")
                            nc.tensor.matmul(ps[f"s{f}"][:], w_1[:, chunk(f)], h1T[:], start=True,
                                             stop=True).then_inc(filled[f"s{f}"], 1)
                    elif step == "W2":
                        for f in range(FT):
                            ready(f"s{f}", "W1")
                        free("w1")
                        for c in range(TILES):
                            for f in range(FT):
                                t = nc.tensor.matmul(ps["w1"][:, chunk(c)], hid[f][:, chunk(c)], w_2[:, f, :],
                                                     start=f == 0, stop=f == FT - 1)
                        t.then_inc(filled["w1"], 1)

                pipeline(pe, plan, weights_in, weights_out, body)

            @block.scalar
            def _(act):
                for k in plan.BANKS:
                    act.sem_inc(emptied[k], 1)

                def weights_in(l, slot):
                    if slot is None:
                        act.wait_ge(ones_set, 11)
                        act.nop(nofuse=True)
                    wait_staged(act, l, slot)
                    nc.scalar.copy(w_in[:].rearrange("p a n -> p (a n)"), next_sq[:, 0:3 * P])
                    nc.scalar.copy(cols_in[:], next_cols[:, 0:2])
                    for sign in range(2):
                        def signed(ap):
                            return ap.rearrange("p (g s m) -> p g s m", s=2, m=8)[:, :, sign, :]

                        t = nc.scalar.mul(signed(omega[0:64, :]), signed(next_omega[:]), (ROOT, -ROOT)[sign])
                    t.then_inc(made_in["act"], 1)
                    act.wait_ge(made_in["act"], l + 2)
                    act.nop(nofuse=True)

                def weights_out(l, slot):
                    wait_staged(act, l, slot)
                    nc.scalar.copy(w_o[:], next_sq[:, 3 * P:4 * P])
                    nc.scalar.copy(cols[:], next_cols[:, 2:4 + FT]).then_inc(made_out["act"], 1)
                    act.wait_ge(made_out["act"], l + 2)
                    act.nop(nofuse=True)

                def body(step, slot, sequence):
                    def full(bank):
                        wait_filled(act, bank, slot, step)

                    if step == "turn":
                        act.wait_ge(s["o_new"], slot.of("in") + 2)
                        act.nop(nofuse=True)
                        nc.scalar.copy(o_now[:].rearrange("p c d -> p (c d)"),
                                       sequence_of(mem["o"], sequence["in"])).then_inc(s["o_now"], 1)
                        full("w0")
                        nc.scalar.copy(oT[:], ps["w0"][:]).then_inc(emptied["w0"], 1)
                    elif step == "project":
                        for j, bank in enumerate(("w1", "w0")):
                            full(bank)
                            for t_ in range(2):
                                half = slice(64 * t_, 64 * t_ + 64)
                                nc.scalar.activation(proj[j][t_][0:64, :], ps[bank][half, :], ACT.Identity,
                                                     bias=cols_in[half, j:j + 1])
                                t = nc.scalar.activation(proj[j][t_][64:P, :], ps[bank][half, :], ACT.Square,
                                                         bias=cols_in[half, j:j + 1])
                            t.then_inc(emptied[bank], 1)
                    elif step in ("mapq", "mapk"):
                        j = ("mapq", "mapk").index(step)
                        maps = (phi_q[slot.parity_in], phi_k)[j]
                        for t_, bank in enumerate((("w0", "w1"), ("s0", "s1"))[j]):
                            full(bank)
                            if j == 0:
                                for r in range(4):
                                    rs = slice(32 * r, 32 * r + 32)
                                    t = nc.scalar.activation(
                                        qz[t_][rs, :, r, :], ps[bank][rs, :].rearrange("p (u n) -> p u n", u=SPANS),
                                        ACT.Exp)
                                t.then_inc(s["qz"], 1)
                            nc.scalar.activation(maps[t_][:], ps[bank][:], ACT.Exp).then_inc(emptied[bank], 1)
                    elif step in ("W10", "W11"):
                        t_ = int(step[2])
                        full(f"n{t_}")
                        nc.scalar.copy(num[t_][:], ps[f"n{t_}"][0:HALF, :]).then_inc(emptied[f"n{t_}"], 1)
                    elif step == "att":
                        full("w0")
                        nc.scalar.copy(attT[:], ps["w0"][:]).then_inc(emptied["w0"], 1)
                    elif step == "h1":
                        full("s2")
                        nc.scalar.activation(h1T[:], ps["s2"][:], ACT.Identity, bias=cols[:, 1:2],
                                             scale=cols[:, 0:1]).then_inc(emptied["s2"], 1)
                    elif step == "W1":
                        for f in (0, 2):
                            full(f"s{f}")
                            nc.scalar.activation(hid[f][:], ps[f"s{f}"][:], ACT.Relu,
                                                 bias=cols[:, 2 + f:3 + f]).then_inc(emptied[f"s{f}"], 1)

                act.sem_inc(made_in["act"], 1)
                act.sem_inc(made_out["act"], 1)
                begin(act, "o_now qz")
                pipeline(act, plan, weights_in, weights_out, body)

            @block.vector
            def _(dve):
                flat = v_tok[:].rearrange("p c s h d -> p c s (h d)")
                nc.vector.memset(flat[:, :, 1, :], 1.0).then_inc(ones_set, 1)
                nc.vector.memset(flat[0:SPAN, :, 0, :], 1.0).then_inc(ones_set, 1)
                nc.vector.memset(flat[SPAN:P, :, 0, :], 0.0).then_inc(ones_set, 1)
                nc.vector.memset(v_pad[:].rearrange("p u n -> p (u n)"), 0.0).then_inc(ones_set, 1)
                nc.vector.tensor_copy(omega[64:P, :], mem["half_norm"][64:P, :]).then_inc(ones_set, 1)
                for t_ in range(2):
                    nc.vector.memset(qz[t_][:].rearrange("p u r n -> p (u r n)"), 0.0).then_inc(ones_set, 1)
                dve.wait_ge(ones_set, 7)
                own = [v_pad[SPAN * p:SPAN * (p + 1)].rearrange("p (c s) (k n) -> p c s k n", s=2, n=DIAGONAL)
                       [:, :, :, :, p * V:(p + 1) * V] for p in range(2)]
                for p in range(2):
                    for span in range(2):
                        nc.vector.memset(own[p][:, :, span, :, D:V], 1.0).then_inc(ones_set, 1)
                dve.wait_ge(ones_set, 11)

                def weights_in(l, slot):
                    wait_staged(dve, l, slot)
                    nc.vector.tensor_copy(bv[:], next_rows[:, 0:P]).then_inc(made_in["dve"], 1)
                    dve.wait_ge(made_in["dve"], l + 2)
                    dve.nop(nofuse=True)

                def weights_out(l, slot):
                    wait_staged(dve, l, slot)
                    nc.vector.tensor_copy(cols_v[:], next_cols[:, 2:4 + FT])
                    nc.vector.tensor_copy(w_1[:], next_1[:])
                    nc.vector.tensor_copy(w_2[:].rearrange("p a n -> p (a n)"),
                                          next_2[:]).then_inc(made_out["dve"], 1)
                    dve.wait_ge(made_out["dve"], l + 2)
                    dve.nop(nofuse=True)

                def norm(slot, k):
                    for c in range(TILES):
                        nc.vector.bn_stats(m["stats"][:, c, :], res[:, c, :]).then_inc(s["stats"], 1)
                    wait(dve, "stats", slot, TILES * (k + 1))
                    dve.nop(nofuse=True)
                    for c in range(TILES):
                        nc.vector.bn_aggr(m["mean_var"][:, c, :], m["stats"][:, c, :]).then_inc(s["mv"], 1)
                    wait(dve, "mv", slot, TILES * (k + 1))
                    nc.vector.tensor_scalar(m["var_eps"][:], m["mean_var"][:, :, 1], LN_EPS, None,
                                            ALU.add).then_inc(s["eps"], 1)
                    wait(dve, "rstd", slot, k + 1)
                    for c in range(TILES):
                        nc.vector.tensor_scalar(m["xn"][:, c, :], res[:, c, :], m["mean_var"][:, c, 0:1],
                                                m["rstd"][:, c:c + 1], ALU.subtract,
                                                ALU.mult).then_inc(s["xn"], 1)

                def body(step, slot, sequence):
                    def full(bank):
                        wait_filled(dve, bank, slot, step)

                    if step == "values":
                        wait(dve, "v_pad", slot, 0)
                        full("w1")
                        for span, size in ((1, P), (0, SPAN)):
                            t = nc.vector.tensor_tensor(
                                v_tok[0:size, :, span, :, 0:D],
                                ps["w1"][0:size, :].rearrange("p (c h d) -> p c h d", c=TILES, h=H),
                                bv[0:size, :].rearrange("p (h d) -> p h d", h=H).unsqueeze(1)
                                .broadcast_to([size, TILES, H, D]), ALU.add)
                            t.then_inc(*((s["v_tok"], 1) if span else (emptied["w1"], 1)))
                    elif step == "mapk":
                        for t_ in range(2):
                            wait_emptied(dve, f"s{t_}", slot, "mapk")
                            for p in range(2):
                                nc.vector.tensor_scalar(kz[t_][:, :, p, :],
                                                        phi_k[t_][:].rearrange("p (u n) -> p u n", u=SPANS),
                                                        mem["strip_head"][:, p:p + 1], None,
                                                        ALU.mult).then_inc(s["kz"], 1)
                    elif step == "keys":
                        for t_, bank in enumerate(("w0", "w1")):
                            full(bank)
                            nc.vector.tensor_copy(k_tok[:, t_, :, :].rearrange("p c n -> p (c n)"),
                                                  ps[bank][:]).then_inc(emptied[bank], 1)
                    elif step == "sums":
                        for t_, bank in enumerate(("w0", "s3")):
                            full(bank)
                            nc.vector.tensor_tensor(
                                kv[:, t_, :, :],
                                ps[bank][:, 0:(SPANS - 1) * HALF].rearrange("p (c n) -> p c n", c=SPANS - 1),
                                mem["own_head"][:].unsqueeze(1).broadcast_to([P, SPANS - 1, HALF]),
                                ALU.mult).then_inc(emptied[bank], 1)
                        wait_emptied(dve, "w0", slot, "sums")
                        wait_emptied(dve, "s3", slot, "sums")
                        for c in range(1, TILES):
                            if c > 1:
                                wait(dve, "kv_sum", slot, c - 1)
                            sums = kv[:, :, 2 * c:min(2 * c + 2, SPANS - 1), :]
                            n = sums.shape[2]
                            nc.vector.tensor_tensor(sums, sums, kv[:, :, 2 * c - 1:2 * c, :]
                                                    .broadcast_to([P, 2, n, HALF]), ALU.add).then_inc(s["kv_sum"], 1)
                        dve.wait_ge(filled["n1"], slot.of("in") + 1)
                        wait(dve, "v_tok", slot, 1)
                        for p in range(2):
                            for span in range(2):
                                rows_ = slice(SPAN * span, SPAN * (span + 1))
                                t = nc.vector.tensor_copy(
                                    own[p][:, :, span, :, 0:D],
                                    v_tok[rows_, :, 1, :, 0:D].rearrange("p c (k q) d -> p c k q d", q=2)
                                    [:, :, :, p, :])
                        t.then_inc(s["v_pad"], 1)
                    elif step[0] == "S":
                        i, t_ = int(step[1]), int(step[2])
                        for n in (2 * t_, 2 * t_ + 1):
                            full(f"s{n}")
                            nc.vector.tensor_tensor(mixed[i][n][:].rearrange("p u r n -> p (u r) n"),
                                                    ps[f"s{n}"][:].rearrange("p (k n) -> p k n", k=8),
                                                    mem["upto"][:].unsqueeze(1).broadcast_to([P, 8, SPAN]),
                                                    ALU.mult).then_inc(emptied[f"s{n}"], 1)
                    elif step == "nums":
                        for t_, bank in enumerate(("w0", "w1")):
                            full(bank)
                            nums = ps[bank][:, 0:TILES * HALF].rearrange("p (c k d) -> p c k d", c=TILES, d=V)
                            nc.vector.tensor_scalar(den[:, t_, :, :], nums[:, :, :, D], EPS, None,
                                                    ALU.add).then_inc(s["den"], 1)
                            wait(dve, "den", slot, t_ + 1)
                            nc.vector.reciprocal(inv[:, t_, :, :], den[:, t_, :, :]).then_inc(s["inv"], 1)
                            wait(dve, "inv", slot, t_ + 1)
                            nc.vector.tensor_tensor(
                                att[:].rearrange("p c (t k d) -> p c t k d", t=2, k=8)[:, :, t_, :, :],
                                nums[:, :, :, 0:D], inv[:, t_, :, :].unsqueeze(3).broadcast_to([P, TILES, 8, D]),
                                ALU.mult).then_inc(emptied[bank], 1)
                    elif step == "Wo":
                        wait(dve, "xn", slot, 0)
                        wait(dve, "o_bias", slot, 1)
                        full("w1")
                        nc.vector.tensor_tensor(res[:].rearrange("p c d -> p (c d)"), ps["w1"][:],
                                                o_bias[:].rearrange("p c d -> p (c d)"),
                                                ALU.add).then_inc(emptied["w1"], 1)
                        wait_emptied(dve, "w1", slot, "Wo")
                        norm(slot, 0)
                    elif step == "W1":
                        for f in (1, 3):
                            full(f"s{f}")
                            nc.vector.tensor_scalar(hid[f][:], ps[f"s{f}"][:], cols_v[:, 2 + f:3 + f], 0.0,
                                                    ALU.add, ALU.max).then_inc(emptied[f"s{f}"], 1)
                    elif step == "W2":
                        wait(dve, "xn", slot, TILES)
                        wait(dve, "h1b", slot, 1)
                        full("w1")
                        nc.vector.tensor_tensor(res[:].rearrange("p c d -> p (c d)"), ps["w1"][:],
                                                h1b[:].rearrange("p c d -> p (c d)"),
                                                ALU.add).then_inc(emptied["w1"], 1)
                        wait_emptied(dve, "w1", slot, "W2")
                        norm(slot, 1)

                dve.sem_inc(made_in["dve"], 1)
                dve.sem_inc(made_out["dve"], 1)
                begin(dve, "kv_sum stats mv eps xn den inv kz v_tok v_pad")
                pipeline(dve, plan, weights_in, weights_out, body)

        added = sem("added")
        with nc.Block() as block:
            @block.vector
            def _(dve):
                with dve.Fori(0, B) as b:
                    x4 = mem["x"][:, bass.ds(b * SEQ, SEQ)]
                    nc.vector.tensor_tensor(x4, x4, mem["o"][:, bass.ds(b * SEQ, SEQ)], ALU.add).then_inc(added, 1)


def moe_block(nc, mem, groups, tag):
    E, K, ROUTE_SCALE = mem["experts"], 8, 2.826
    x_all = mem["x"]
    w_gate, w_up, w_down = mem["moe_gate"], mem["moe_up"], mem["moe_down"]
    with ExitStack() as ctx:
        def sb(name, shape, dt=F32):
            return ctx.enter_context(nc.sbuf_tensor(tag + name, shape, dt))

        def bank(name):
            return ctx.enter_context(nc.psum_tensor(tag + name, [P, 512], F32))

        def sem(name):
            return ctx.enter_context(nc.semaphore(tag + name))

        stats = sb("stats", [P, TILES, 6])
        mean_var = sb("mean_var", [P, TILES, 2])
        var_eps = sb("var_eps", [P, TILES])
        rstd = sb("rstd", [P, TILES])
        xn = sb("xn", [P, TILES, P])
        xT = sb("xT", [P, SEQ])
        x_hi = [sb(f"x_hi{i}", [P, SEQ], F32R) for i in range(2)]
        x_lo = [sb(f"x_lo{i}", [P, SEQ], F32R) for i in range(2)]
        parts = [[sb(f"{n}_{part}", [P, (E + 1) * P], F32R) for part in ("hi", "lo")] for n in ("gate", "up")]
        score = sb("score", [P, TILES, E])
        select = sb("select", [P, TILES, E])
        top8 = sb("top8", [P, TILES, 8])
        rest = sb("rest", [P, TILES, E])
        chosen = sb("chosen", [P, TILES, E])
        picked = sb("picked", [P, TILES, E])
        total = sb("total", [P, TILES])
        inv_total = sb("inv_total", [P, TILES])
        combine = [sb(f"combine{i}", [P, TILES, E]) for i in range(2)]
        silu = [sb(f"silu{i}", [P, SEQ]) for i in range(2)]
        hidden = [sb(f"hidden{i}", [P, SEQ]) for i in range(3)]
        acc = sb("acc", [P, TILES, P])
        ps_g = [bank(f"ps_g{i}") for i in range(2)]
        ps_u = [bank(f"ps_u{i}") for i in range(2)]
        ps_y = [bank(f"ps_y{i}") for i in range(2)]
        ps_t = bank("ps_t")
        ps_gate = bank("ps_gate")

        stats_done, mv_done, eps_done = sem("stats_done"), sem("mv_done"), sem("eps_done")
        rstd_done, xn_done, turned, xT_done = sem("rstd_done"), sem("xn_done"), sem("turned"), sem("xT_done")
        gates_done, score_done, route_step = sem("gates_done"), sem("score_done"), sem("route_step")
        g_done, u_done, silu_done, hid_done = sem("g_done"), sem("u_done"), sem("silu_done"), sem("hid_done")
        y_done, acc_done, group_done = sem("y_done"), sem("acc_done"), sem("group_done")
        x_hi_done, x_lo_done, w_hi_done, w_lo_done = (sem(n) for n in ("x_hi_done", "x_lo_done", "w_hi_done",
                                                                       "w_lo_done"))
        N = E + 1
        STEPS = [(w, parts[n], slice(a * P, b * P)) for a, b in ((0, 4), (4, N))
                 for n, w in enumerate((w_gate, w_up))]
        ROUTE = 3 + 3 * TILES
        with nc.Block() as block:

            def groups_by_two(e, prepare, work):
                prepare(0, 0)
                with e.Fori(0, groups // 2) as pair:
                    for parity in range(2):
                        work(pair * 2 + parity, parity)

            @block.tensor
            def _(pe):
                def turn(g):
                    pe.wait_ge(xn_done, g * TILES + TILES)
                    for c in range(TILES):
                        t = nc.tensor.transpose(ps_t[:, c * P:(c + 1) * P], xn[:, c, :], mem["ident"][:])
                    t.then_inc(turned, 1)

                def route(g):
                    pe.wait_ge(xT_done, g + 1)
                    for c in range(TILES):
                        t = nc.tensor.matmul(ps_gate[:, c * E:(c + 1) * E], xT[:, c * P:(c + 1) * P],
                                             mem["router"][:], start=True, stop=True)
                    t.then_inc(gates_done, 1)

                def prepare(g, parity):
                    turn(g)
                    route(g)

                def work(g, parity):
                    def down(e):
                        pe.wait_ge(hid_done, g * N + e + 1)
                        if e >= 2:
                            pe.wait_ge(acc_done, g * N + e - 1)
                        else:
                            pe.wait_ge(group_done, g + 1)
                        for c in range(TILES):
                            t = nc.tensor.matmul(ps_y[e % 2][:, c * P:(c + 1) * P],
                                                 hidden[e % 3][:, c * P:(c + 1) * P],
                                                 w_down[:, e * P:(e + 1) * P], start=True, stop=True)
                        t.then_inc(y_done, 1)

                    def up(bank, w, e):
                        for k, (part, x) in enumerate(((0, x_hi), (0, x_lo), (1, x_hi))):
                            t = nc.tensor.matmul(bank[:], parts[w][part][:, e * P:(e + 1) * P], x[parity][:],
                                                 start=k == 0, stop=k == 2)
                        return t

                    pe.wait_ge(x_lo_done, g + 1)
                    for e in range(N + 2):
                        if e in (0, 4):
                            pe.wait_ge(w_lo_done, 2 if e == 0 else 4)
                            pe.nop(nofuse=True)
                        if e < N:
                            if e >= 2:
                                pe.wait_ge(silu_done, g * N + e - 1)
                            up(ps_g[e % 2], 0, e).then_inc(g_done, 1)
                            if e >= 2:
                                pe.wait_ge(hid_done, g * N + e - 1)
                            up(ps_u[e % 2], 1, e).then_inc(u_done, 1)
                        if e >= 2:
                            down(e - 2)
                        if e == 8:
                            turn(g + 1)
                        elif e == 10:
                            route(g + 1)

                groups_by_two(pe, prepare, work)

            @block.scalar
            def _(act):
                for w, (hi, lo), at in STEPS:
                    nc.scalar.copy(hi[:, at], w[:, at]).then_inc(w_hi_done, 1)

                def copy_turned(g, parity):
                    act.wait_ge(turned, g + 1)
                    nc.scalar.copy(xT[:], ps_t[:]).then_inc(xT_done, 1)
                    nc.scalar.copy(x_hi[parity][:], ps_t[:]).then_inc(x_hi_done, 1)

                def scores(g):
                    act.wait_ge(gates_done, g + 1)
                    act.wait_ge(route_step, g * ROUTE + 1)
                    nc.scalar.activation(score[:].rearrange("p c e -> p (c e)"), ps_gate[:, 0:TILES * E],
                                         ACT.Sigmoid).then_inc(score_done, 1)

                def prepare(g, parity):
                    copy_turned(g, parity)
                    scores(g)

                def work(g, parity):
                    for e in range(N):
                        act.wait_ge(g_done, g * N + e + 1)
                        if e >= 2:
                            act.wait_ge(hid_done, g * N + e - 1)
                        nc.scalar.activation(silu[e % 2][:], ps_g[e % 2][:], ACT.Silu).then_inc(silu_done, 1)
                        if e == 8:
                            copy_turned(g + 1, 1 - parity)
                        elif e == 10:
                            scores(g + 1)

                groups_by_two(act, prepare, work)

            @block.gpsimd
            def _(pool):
                with pool.Fori(0, groups + 1) as g:
                    pool.wait_ge(eps_done, g + 1)
                    nc.gpsimd.tensor_tensor(rstd[:], var_eps[:], mem["minus_half"][:, 0:TILES],
                                            ALU.pow).then_inc(rstd_done, 1)

            @block.vector
            def _(dve):
                dve.sem_inc(group_done, 1)
                dve.sem_inc(route_step, 1)
                for n, (w, (hi, lo), at) in enumerate(STEPS):
                    dve.wait_ge(w_hi_done, n + 1)
                    nc.vector.tensor_tensor(lo[:, at], w[:, at], hi[:, at].bitcast(F32),
                                            ALU.subtract).then_inc(w_lo_done, 1)
                def x_tile(g, c, n=1):
                    return x_all[:, bass.ds(g * SEQ + c * P, n * P)]

                def normalise(g, piece):
                    if piece == 0:
                        for c in range(TILES):
                            nc.vector.bn_stats(stats[:, c, :], x_tile(g, c)).then_inc(stats_done, 1)
                    elif piece == 1:
                        dve.wait_ge(stats_done, (g + 1) * TILES)
                        dve.nop(nofuse=True)
                        for c in range(TILES):
                            nc.vector.bn_aggr(mean_var[:, c, :], stats[:, c, :]).then_inc(mv_done, 1)
                        dve.wait_ge(mv_done, (g + 1) * TILES)
                        nc.vector.tensor_scalar(var_eps[:], mean_var[:, :, 1], LN_EPS, None,
                                                ALU.add).then_inc(eps_done, 1)
                    else:
                        dve.wait_ge(rstd_done, g + 1)
                        for c in range(TILES):
                            nc.vector.tensor_scalar(xn[:, c, :], x_tile(g, c), mean_var[:, c, 0:1], rstd[:, c:c + 1],
                                                    ALU.subtract, ALU.mult).then_inc(xn_done, 1)

                def low(g, parity):
                    dve.wait_ge(xT_done, g + 1)
                    dve.wait_ge(x_hi_done, g + 1)
                    nc.vector.tensor_tensor(x_lo[parity][:], xT[:], x_hi[parity][:].bitcast(F32),
                                            ALU.subtract).then_inc(x_lo_done, 1)

                def choose(g, parity, piece):
                    done = g * ROUTE + 1
                    if piece == 0:
                        dve.wait_ge(score_done, g + 1)
                        nc.vector.tensor_tensor(select[:], score[:],
                                                mem["expert_bias"][:].unsqueeze(1).broadcast_to([P, TILES, E]),
                                                ALU.add).then_inc(route_step, 1)
                    elif piece == 1:
                        dve.wait_ge(route_step, done + 1)
                        dve.nop(nofuse=True)
                        for c in range(TILES):
                            nc.vector.max(top8[:, c, :], select[:, c, :]).then_inc(route_step, 1)
                    elif piece == 2:
                        dve.wait_ge(route_step, done + 1 + TILES)
                        dve.nop(nofuse=True)
                        for c in range(TILES):
                            nc.vector.match_replace(rest[:, c, :], top8[:, c, :], select[:, c, :],
                                                    -3.0e38).then_inc(route_step, 1)
                    elif piece == 3:
                        dve.wait_ge(route_step, done + 1 + 2 * TILES)
                        nc.vector.tensor_tensor(chosen[:], rest[:], select[:], ALU.not_equal).then_inc(route_step, 1)
                        dve.wait_ge(route_step, done + 2 + 2 * TILES)
                        nc.vector.tensor_tensor(picked[:], chosen[:], score[:], ALU.mult).then_inc(route_step, 1)
                        dve.wait_ge(route_step, done + 3 + 2 * TILES)
                        nc.vector.reduce_sum(total[:], picked[:], AX.X).then_inc(route_step, 1)
                    else:
                        dve.wait_ge(route_step, done + 4 + 2 * TILES)
                        nc.vector.reciprocal(inv_total[:], total[:]).then_inc(route_step, 1)
                        dve.wait_ge(route_step, done + 5 + 2 * TILES)
                        nc.vector.scalar_tensor_tensor(combine[parity][:], picked[:], ROUTE_SCALE,
                                                       inv_total[:].unsqueeze(2).broadcast_to([P, TILES, E]),
                                                       ALU.mult, ALU.mult).then_inc(route_step, TILES - 2)

                def prepare(g, parity):
                    for piece in range(3):
                        normalise(g, piece)
                    low(g, parity)
                    for piece in range(5):
                        choose(g, parity, piece)

                def work(g, parity):
                    def gather(e):
                        dve.wait_ge(y_done, g * N + e + 1)
                        if e == 0:
                            dve.wait_ge(route_step, g * ROUTE + (ROUTE + 1))
                        elif e >= 1:
                            dve.wait_ge(acc_done, g * N + e)
                        for c in range(TILES):
                            y = ps_y[e % 2][:, c * P:(c + 1) * P]
                            if e == 0:
                                t = nc.vector.tensor_scalar(acc[:, c, :], y, combine[parity][:, c, 0:1], None, ALU.mult)
                            elif e < E:
                                t = nc.vector.scalar_tensor_tensor(acc[:, c, :], y, combine[parity][:, c, e:e + 1],
                                                                   acc[:, c, :], ALU.mult, ALU.add)
                        if e == E:
                            t = nc.vector.tensor_tensor(acc[:].rearrange("p c d -> p (c d)"), ps_y[e % 2][:],
                                                        acc[:].rearrange("p c d -> p (c d)"), ALU.add)
                        t.then_inc(acc_done, 1)

                    for e in range(N):
                        dve.wait_ge(silu_done, g * N + e + 1)
                        dve.wait_ge(u_done, g * N + e + 1)
                        if e >= 3:
                            dve.wait_ge(y_done, g * N + e - 2)
                        nc.vector.tensor_tensor(hidden[e % 3][:], silu[e % 2][:], ps_u[e % 2][:],
                                                ALU.mult).then_inc(hid_done, 1)
                        if e >= 2:
                            gather(e - 2)
                        if 4 <= e < 7:
                            normalise(g + 1, e - 4)
                        elif e == 9:
                            low(g + 1, 1 - parity)
                        elif 11 <= e < 16:
                            choose(g + 1, 1 - parity, e - 11)
                    gather(N - 2)
                    gather(N - 1)
                    dve.wait_ge(acc_done, g * N + N)
                    nc.vector.tensor_tensor(x_tile(g, 0, TILES), x_tile(g, 0, TILES),
                                            acc[:].rearrange("p c d -> p (c d)"), ALU.add).then_inc(group_done, 1)

                groups_by_two(dve, prepare, work)


def build(nc, ins, out, stages):
    B = ins["x"].shape[0]
    with ExitStack() as ctx:
        mem = {}

        def keep(name, shape, dt=F32):
            mem[name] = ctx.enter_context(nc.sbuf_tensor(name, shape, dt))
            return mem[name]

        keep("x", [P, (B + 1) * SEQ])
        keep("ident", [P, P])
        keep("minus_half", [P, 16])
        E = ins["router"].shape[1]
        mem["experts"] = E
        for n in ("moe_gate", "moe_up", "moe_down"):
            keep(n, [P, (E + 1) * P])
        keep("plus_half", [P, 16])
        keep("router", [P, E])
        keep("expert_bias", [P, E])
        keep("o", [P, B * SEQ])
        names = ["ident", "router", "moe_gate", "moe_up", "moe_down"]
        for n in ("ident16", "future16", "upto", "half_norm", "own_head", "strip_head"):
            keep(n, list(ins[n].shape), ins[n].dtype)
            names.append(n)
        tables_a = ctx.enter_context(ExitStack())
        for n in ("twos_upto", "twos", "state0", "lin_mask", "cos2", "sin2", "cos_sin"):
            mem[n] = tables_a.enter_context(nc.sbuf_tensor(n, list(ins[n].shape), ins[n].dtype))
            names.append(n)
        mem["xT"] = tables_a.enter_context(nc.sbuf_tensor("xT", [P, (B + 1) * SEQ], F32))
        mem["b_out4"] = tables_a.enter_context(nc.sbuf_tensor("b_out4", [P, SEQ], F32))
        loaded = ctx.enter_context(nc.semaphore("loaded"))
        consts = ctx.enter_context(nc.semaphore("consts"))
        stored = ctx.enter_context(nc.semaphore("stored"))
        loads = [(mem["x"][:, 0:B * SEQ].rearrange("p (t d) -> p t d", d=P),
                  ins["x"].rearrange("b (c p) d -> p (b c) d", p=P))]
        for n in names:
            loads.append((mem[n][:], ins[n]))
        loads.append((mem["expert_bias"][:], ins["expert_bias"].partition_broadcast(P)))
        for c in range(TILES):
            loads.append((mem["b_out4"][:, c * P:(c + 1) * P], ins["b_out"].partition_broadcast(P)))
        with nc.Block() as block:
            @block.sync
            def _(sp):
                for dst, src in loads:
                    sp.dma_start(dst, src).then_inc(loaded, 16)
                sp.wait_ge(loaded, 16 * len(loads))

            @block.vector
            def _(dve):
                nc.vector.memset(mem["minus_half"][:], -0.5).then_inc(consts, 1)
                nc.vector.memset(mem["plus_half"][:], 0.5).then_inc(consts, 1)
                nc.vector.memset(mem["x"][:, B * SEQ:], 0.0).then_inc(consts, 1)
                dve.wait_ge(consts, 3)
        for n, s in enumerate(stages):
            tag = f"{s}{n}_"
            if s == "a":
                norm_block(nc, mem, B, attention=True, tag=tag)
                attention_block(nc, mem, ins, B)
                tables_a.close()
            if s == "b":
                norm_block(nc, mem, B, attention=False, tag=tag)
                transformer_block(nc, mem, ins, B)
            if s == "ffn":
                moe_block(nc, mem, B, tag)
        with nc.Block() as block:
            @block.sync
            def _(sp):
                sp.dma_start(out.rearrange("b (c p) d -> p (b c) d", p=P),
                             mem["x"][:, 0:B * SEQ].rearrange("p (t d) -> p t d", d=P)).then_inc(stored, 16)
                sp.wait_ge(stored, 16)


def lay_out(t):
    f = "L0_ffn_"
    a = {"x": t["L0_attn_a_X"], "expert_bias": t[f + "expert_bias"],
         "router": t[f + "gate_w"].T, "ident": np.eye(P, dtype=np.float32)}
    for name, experts, shared in (("moe_gate", "w_gate", "shared_gate_w"), ("moe_up", "w_up", "shared_up_w"),
                                  ("moe_down", "w_down", "shared_down_w")):
        w = np.concatenate([t[f + experts], t[f + shared][None]], axis=0)
        a[name] = w.transpose(2, 0, 1).reshape(P, -1)
    f = "L0_attn_a_"
    HHD = t[f + "w_out"].shape[0]
    HD, pairs = 64, HHD // P
    q, k, v = (t[f + "w_qkv"][:, i * HHD:(i + 1) * HHD] for i in range(3))
    kk, vk = (t[f + "w_kvkv"][:, i * HHD:(i + 1) * HHD] for i in range(2))
    blocks = [w.reshape(P, pairs, P).transpose(1, 0, 2) for w in (q, vk, k, kk, v)]
    a["pairs"] = np.concatenate(blocks + [t[f + "w_out"].reshape(pairs, P, P)], axis=2)
    a["pairs"] = np.concatenate([a["pairs"], np.zeros_like(a["pairs"][:1])])
    a["b_out"] = t[f + "b_out"]
    a.update(tables(HD))
    f = "L0_attn_b_"
    L = t[f + "Wq"].shape[0]
    a["t_sq"] = np.concatenate([t[f + n] for n in ("Wq", "Wk", "Wv", "Wo")], axis=2)
    a["t_w1"] = t[f + "W1"]
    a["t_w2"] = t[f + "W2"].reshape(L, -1, P, P).transpose(0, 2, 1, 3).reshape(L, P, -1)
    heads, _, at = feature_places()
    omega = np.zeros((L, P // 2, 2 * P), np.float32)
    for col in range(2 * P):
        row = heads[col] % 8 * 8
        omega[:, row:row + 8, col] = t[f + "omega"][:, :, at[col]]
    a["t_omega"] = omega
    columns = [t[f + n][:, :, None] for n in ("bq", "bk", "g1", "be1")]
    a["t_cols"] = np.concatenate(columns + [t[f + "bf1"].reshape(L, -1, P).transpose(0, 2, 1)], axis=2)
    a["t_rows"] = np.concatenate([t[f + n] for n in ("bv", "bo", "g1", "be1", "bf2", "g2", "be2")], axis=1)
    for n in ("t_sq", "t_w1", "t_w2", "t_omega", "t_cols", "t_rows"):
        a[n] = np.concatenate([a[n], np.zeros_like(a[n][:1])])
    return a


def feature_places():
    col = np.arange(2 * P)
    half, strip, head, sign, m = col // P, col // 32 % 4, col // 16 % 2, 1 - 2 * (col // 8 % 2), col % 8
    return 8 * half + 2 * strip + head, sign, m


def tables(HD):
    f32 = np.float32
    i, j = np.arange(P)[:, None], np.arange(P)[None, :]
    freq = (f32(1.0) / f32(10000.0) ** (np.arange(0, HD, 2, dtype=f32) / f32(HD))).astype(f32)
    angle = np.repeat(np.arange(SEQ, dtype=f32)[:, None] * freq[None, :], 2, axis=1).T
    cos, sin = np.cos(angle).astype(f32), np.sin(angle).astype(f32)
    eye = np.eye(HD, dtype=f32) * f32(HD ** 0.5)
    turned = np.zeros((HD, HD), f32)
    turned[1::2, 0::2] = -eye[0::2, 0::2]
    turned[0::2, 1::2] = eye[0::2, 0::2]
    state0 = np.concatenate([eye, turned], axis=1)
    bf16 = mybir.dt.np(BF16)
    key, query = i % (P // 2), j[:, :P // 2]
    heads, _, _ = feature_places()
    root = 8 ** -0.25
    squares = (np.arange(P)[:, None] - P // 2) // 8 == heads[None, :] % 8
    return {
        "upto": (key <= query).astype(f32),
        "half_norm": (squares * f32(-0.5 * root * root)).astype(f32),
        "own_head": (heads[:P, None] == np.arange(8 * 9)[None, :] // 9).astype(f32),
        "strip_head": np.stack([(np.arange(P) // 16 % 2 == p) for p in range(2)], axis=1).astype(f32),
        "twos_upto": 2.0 * (i <= j).astype(f32), "twos": np.full((P, P), 2.0, f32),
        "state0": np.concatenate([state0, state0], axis=0),
        "lin_mask": np.concatenate([(i <= j), (i < j) + 0.5 * (i == j)], axis=1).astype(f32),
        "cos2": np.concatenate([cos, cos]), "sin2": np.concatenate([sin, sin]),
        "cos_sin": np.concatenate([cos, sin]),
        "ident16": np.eye(P).astype(bf16), "future16": np.where(j > i, -1e30, 0.0).astype(bf16),
    }


def kernel(**inputs):
    import concourse.bacc as bacc
    from concourse.bass_utils import run_bass_kernel_spmd

    t = {k: np.asarray(v) for k, v in inputs.items()}
    arrays = {k: np.ascontiguousarray(v) for k, v in lay_out(t).items()}
    nc = bacc.Bacc("TRN2", target_bir_lowering=False, num_devices=1)
    ins = {k: nc.dram_tensor("in_" + k, list(v.shape), mybir.dt.from_np(v.dtype), kind="ExternalInput").ap()
           for k, v in arrays.items()}
    out = nc.dram_tensor("out", list(arrays["x"].shape), F32, kind="ExternalOutput").ap()
    build(nc, ins, out, STAGES)
    r = run_bass_kernel_spmd(nc, [{"in_" + k: v for k, v in arrays.items()}], core_ids=[0])
    return r.results[0]["out"]
```
